# Optimizing a Trainium2 kernel written in Bass

```python
import numpy as np
import jax
import jax.numpy as jnp

def _softmax(x, axis=-1):
    return jax.nn.softmax(x, axis=axis)

def _gelu(x):
    return jax.nn.gelu(x, approximate=True)

def _silu(x):
    return jax.nn.silu(x)

def _sigmoid(x):
    return jax.nn.sigmoid(x)

def _layernorm(x, axis=-1, eps=1e-05):
    m = jnp.mean(x, axis=axis, keepdims=True)
    v = jnp.var(x, axis=axis, keepdims=True)
    return (x - m) / jnp.sqrt(v + eps)

def _scatter_add(tgt, idx, src, axis=0):
    return tgt.at[idx].add(src)

def _segment_sum(src, seg, n):
    return jax.ops.segment_sum(src, seg, n)
kernel_name = 'mk_adaln_d2_jaxref_r8_e35100'

def setup_inputs(seed: int=0):
    np.random.seed(seed)
    _w = jnp.asarray

    def _L0_attn_setup():
        import jax, jax.numpy as jnp
        import numpy as np
        import math
        D_MODEL = 256
        N_HEADS = 16
        D_HEAD = 128
        BATCH = 2
        SEQ = 256
        key = jax.random.key(seed)
        ks = jax.random.split(key, 5)
        std = 0.02
        x = jax.random.normal(ks[0], (BATCH, SEQ, D_MODEL), dtype=jnp.float32)
        W_Q = std * jax.random.normal(ks[1], (N_HEADS, D_HEAD, D_MODEL), dtype=jnp.float32)
        W_K = std * jax.random.normal(ks[2], (N_HEADS, D_HEAD, D_MODEL), dtype=jnp.float32)
        W_V = std * jax.random.normal(ks[3], (N_HEADS, D_HEAD, D_MODEL), dtype=jnp.float32)
        W_O = std * jax.random.normal(ks[4], (N_HEADS, D_MODEL, D_HEAD), dtype=jnp.float32)
        return {'x': x, 'W_Q': W_Q, 'W_K': W_K, 'W_V': W_V, 'W_O': W_O}
    _L0_attn_in = _L0_attn_setup()

    def _L0_ffn_setup():
        import jax, jax.numpy as jnp
        import numpy as np
        H = 256
        I = 128
        K = 8
        E = 128
        TOPK = 4
        EPS = 1e-08
        key = jax.random.key(seed)
        ks = jax.random.split(key, 10)
        s = 0.02
        return {'x': jax.random.normal(ks[0], (4, 256, H), jnp.float32), 'w_router': jax.random.normal(ks[1], (H, E), jnp.float32) * s, 'w_gate': jax.random.normal(ks[2], (H, K * I), jnp.float32) * s, 'w_up': jax.random.normal(ks[3], (H, K * I), jnp.float32) * s, 'w_down': jax.random.normal(ks[4], (I, H), jnp.float32) * s, 'amplitudes': jax.random.normal(ks[5], (E, K, 2), jnp.float32) * 0.1, 'expert_scale': jnp.ones((E,), jnp.float32), 'shared_w_gate': jax.random.normal(ks[6], (H, 2 * I), jnp.float32) * s, 'shared_w_up': jax.random.normal(ks[7], (H, 2 * I), jnp.float32) * s, 'shared_w_down': jax.random.normal(ks[8], (2 * I, H), jnp.float32) * s}
    _L0_ffn_in = _L0_ffn_setup()
    _L0_c = _w((lambda *s: np.random.randn(*s).astype(np.float32) * 0.05)(8, 256))
    _L0_wmod = _w((lambda *s: np.random.randn(*s).astype(np.float32) * 0.05)(256, 6 * 256) * 256 ** (-0.5))

    def _L1_attn_setup():
        import jax, jax.numpy as jnp
        import numpy as np
        B, T, D = (2, 256, 256)
        H = 8
        KEY_DIM, VAL_DIM = (128, 256)
        HK, HV = (KEY_DIM // H, VAL_DIM // H)
        LOW_RANK = 16
        GATE_NORM = 16.0
        CHUNK = 64
        HIDDEN = (D * 4 * 2 // 3 + 63) // 64 * 64
        EPS = 1e-06

        def rmsnorm(x, w):
            return x * jax.lax.rsqrt(jnp.mean(x * x, axis=-1, keepdims=True) + EPS) * w

        def _gla(h, wq, wk, wv, gk_w1, gk_w2, gk_b, wg, gnorm_w, wo):
            Bb, Tt, _ = h.shape
            nc = Tt // CHUNK

            def split(t, hd):
                t = t.reshape(Bb, nc, CHUNK, H, hd)
                return jnp.transpose(t, (1, 0, 3, 2, 4))
            q = split(h @ wq, HK) * HK ** (-0.5)
            k = split(h @ wk, HK)
            v = split(h @ wv, HV)
            g = split(jax.nn.log_sigmoid(h @ gk_w1 @ gk_w2 + gk_b) / GATE_NORM, HK)
            mask = jnp.tril(jnp.ones((CHUNK, CHUNK), jnp.float32))

            def step(S, inp):
                qc, kc, vc, gc = inp
                b = jnp.cumsum(gc, axis=-2)
                qe = qc * jnp.exp(b)
                A = jnp.einsum('bhik,bhjk->bhij', qe, kc * jnp.exp(-b)) * mask
                o = jnp.einsum('bhck,bhkv->bhcv', qe, S) + jnp.einsum('bhij,bhjv->bhiv', A, vc)
                bl = b[:, :, -1:, :]
                S = jnp.exp(bl[:, :, 0, :])[..., None] * S + jnp.einsum('bhck,bhcv->bhkv', kc * jnp.exp(bl - b), vc)
                return (S, o)
            S0 = jnp.zeros((Bb, H, HK, HV), h.dtype)
            _, o = jax.lax.scan(step, S0, (q, k, v, g))
            o = jnp.transpose(o, (1, 0, 3, 2, 4)).reshape(Bb, Tt, H, HV)
            gate = (h @ wg).reshape(Bb, Tt, H, HV)
            o = rmsnorm(o, gnorm_w) * gate * jax.nn.sigmoid(gate)
            return o.reshape(Bb, Tt, VAL_DIM) @ wo
        key = jax.random.key(seed)
        ks = jax.random.split(key, 12)
        w = lambda k, s: jax.random.normal(k, s, jnp.float32) * 0.02
        return {'x': jax.random.normal(ks[0], (B, T, D), jnp.float32), 'norm1_w': jnp.ones((D,), jnp.float32), 'wq': w(ks[1], (D, KEY_DIM)), 'wk': w(ks[2], (D, KEY_DIM)), 'wv': w(ks[3], (D, VAL_DIM)), 'gk_w1': w(ks[4], (D, LOW_RANK)), 'gk_w2': w(ks[5], (LOW_RANK, KEY_DIM)), 'gk_b': jnp.zeros((KEY_DIM,), jnp.float32), 'wg': w(ks[6], (D, VAL_DIM)), 'gnorm_w': jnp.ones((HV,), jnp.float32), 'wo': w(ks[7], (VAL_DIM, D)), 'ffn_norm_w': jnp.ones((D,), jnp.float32), 'w_gate': w(ks[8], (D, HIDDEN)), 'w_up': w(ks[9], (D, HIDDEN)), 'w_down': w(ks[10], (HIDDEN, D))}
    _L1_attn_in = _L1_attn_setup()

    def _L1_ffn_setup():
        import jax, jax.numpy as jnp
        import numpy as np

        def _sparsify_2to4(h):
            B, S, I = h.shape
            g = h.reshape(B, S, I // 4, 4)
            a = jnp.abs(g)
            _, idx = jax.lax.top_k(a, 2)
            pos = jnp.arange(4)
            mask = (pos == idx[..., 0:1]) | (pos == idx[..., 1:2])
            return (g * mask.astype(g.dtype)).reshape(B, S, I)
        key = jax.random.key(seed)
        k1, k2, k3, k4 = jax.random.split(key, 4)
        B, S, H, I = (4, 256, 256, 1024)
        x = jax.random.normal(k1, (B, S, H), dtype=jnp.float32)
        w_gate = jax.random.normal(k2, (H, I), dtype=jnp.float32) / np.sqrt(H)
        w_up = jax.random.normal(k3, (H, I), dtype=jnp.float32) / np.sqrt(H)
        w_down = jax.random.normal(k4, (I, H), dtype=jnp.float32) / np.sqrt(I)
        return {'x': x, 'w_gate': w_gate, 'w_up': w_up, 'w_down': w_down}
    _L1_ffn_in = _L1_ffn_setup()
    _L1_c = _w((lambda *s: np.random.randn(*s).astype(np.float32) * 0.05)(8, 256))
    _L1_wmod = _w((lambda *s: np.random.randn(*s).astype(np.float32) * 0.05)(256, 6 * 256) * 256 ** (-0.5))
    _d = {'L0_attn_x': _L0_attn_in['x'], 'L0_attn_W_Q': _L0_attn_in['W_Q'], 'L0_attn_W_K': _L0_attn_in['W_K'], 'L0_attn_W_V': _L0_attn_in['W_V'], 'L0_attn_W_O': _L0_attn_in['W_O'], 'L0_ffn_w_router': _L0_ffn_in['w_router'], 'L0_ffn_w_gate': _L0_ffn_in['w_gate'], 'L0_ffn_w_up': _L0_ffn_in['w_up'], 'L0_ffn_w_down': _L0_ffn_in['w_down'], 'L0_ffn_amplitudes': _L0_ffn_in['amplitudes'], 'L0_ffn_expert_scale': _L0_ffn_in['expert_scale'], 'L0_ffn_shared_w_gate': _L0_ffn_in['shared_w_gate'], 'L0_ffn_shared_w_up': _L0_ffn_in['shared_w_up'], 'L0_ffn_shared_w_down': _L0_ffn_in['shared_w_down'], 'L0_c': _L0_c, 'L0_wmod': _L0_wmod, 'L1_attn_norm1_w': _L1_attn_in['norm1_w'], 'L1_attn_wq': _L1_attn_in['wq'], 'L1_attn_wk': _L1_attn_in['wk'], 'L1_attn_wv': _L1_attn_in['wv'], 'L1_attn_gk_w1': _L1_attn_in['gk_w1'], 'L1_attn_gk_w2': _L1_attn_in['gk_w2'], 'L1_attn_gk_b': _L1_attn_in['gk_b'], 'L1_attn_wg': _L1_attn_in['wg'], 'L1_attn_gnorm_w': _L1_attn_in['gnorm_w'], 'L1_attn_wo': _L1_attn_in['wo'], 'L1_attn_ffn_norm_w': _L1_attn_in['ffn_norm_w'], 'L1_attn_w_gate': _L1_attn_in['w_gate'], 'L1_attn_w_up': _L1_attn_in['w_up'], 'L1_attn_w_down': _L1_attn_in['w_down'], 'L1_ffn_w_gate': _L1_ffn_in['w_gate'], 'L1_ffn_w_up': _L1_ffn_in['w_up'], 'L1_ffn_w_down': _L1_ffn_in['w_down'], 'L1_c': _L1_c, 'L1_wmod': _L1_wmod}
    _x0 = _d['L0_attn_x']
    _d['L0_attn_x'] = jax.random.normal(jax.random.fold_in(jax.random.key(seed), 1), (8, 512, 256), dtype=_x0.dtype)
    del _x0
    return _d

def reference(L0_attn_x, L0_attn_W_Q, L0_attn_W_K, L0_attn_W_V, L0_attn_W_O, L0_ffn_w_router, L0_ffn_w_gate, L0_ffn_w_up, L0_ffn_w_down, L0_ffn_amplitudes, L0_ffn_expert_scale, L0_ffn_shared_w_gate, L0_ffn_shared_w_up, L0_ffn_shared_w_down, L0_c, L0_wmod, L1_attn_norm1_w, L1_attn_wq, L1_attn_wk, L1_attn_wv, L1_attn_gk_w1, L1_attn_gk_w2, L1_attn_gk_b, L1_attn_wg, L1_attn_gnorm_w, L1_attn_wo, L1_attn_ffn_norm_w, L1_attn_w_gate, L1_attn_w_up, L1_attn_w_down, L1_ffn_w_gate, L1_ffn_w_up, L1_ffn_w_down, L1_c, L1_wmod):

    def _L0_attn_ref(x, W_Q, W_K, W_V, W_O):
        import jax, jax.numpy as jnp
        import numpy as np
        import math
        D_MODEL = 256
        N_HEADS = 16
        D_HEAD = 128
        BATCH = 2
        SEQ = 256
        d_head = W_Q.shape[1]
        seq_len = x.shape[1]
        scale = 1.0 / math.sqrt(d_head)
        q = jnp.einsum('bsd,hed->bhse', x, W_Q)
        k = jnp.einsum('bsd,hed->bhse', x, W_K)
        v = jnp.einsum('bsd,hed->bhse', x, W_V)
        scores = jnp.einsum('bhse,bhme->bhsm', q, k) * scale
        causal = jnp.triu(jnp.ones((seq_len, seq_len), dtype=bool), k=1)
        scores = jnp.where(causal, jnp.float32(-1000000000.0), scores)
        pattern = jax.nn.softmax(scores, axis=-1)
        z = jnp.einsum('bhsm,bhme->bhse', pattern, v)
        out = jnp.einsum('bhse,hde->bsd', z, W_O)
        return out

    def _L0_ffn_ref(x, w_router, w_gate, w_up, w_down, amplitudes, expert_scale, shared_w_gate, shared_w_up, shared_w_down):
        import jax, jax.numpy as jnp
        import numpy as np
        H = 256
        I = 128
        K = 8
        E = 128
        TOPK = 4
        EPS = 1e-08
        B, S, _ = x.shape
        T = B * S
        xt = x.reshape(T, H)
        probs = jax.nn.softmax(xt @ w_router, axis=-1)
        topk_p, topk_idx = jax.lax.top_k(probs, TOPK)
        topk_w = topk_p / (jnp.sum(topk_p, axis=-1, keepdims=True) + EPS)
        gate = (xt @ w_gate).reshape(T, K, I)
        up = (xt @ w_up).reshape(T, K, I)
        basis = jax.nn.silu(gate) * up
        p = amplitudes[..., 0] ** 2 + amplitudes[..., 1] ** 2
        mix = p / (jnp.sum(p, axis=-1, keepdims=True) + EPS)
        mix_sel = mix[topk_idx]
        mixed = jnp.einsum('tek,tki->tei', mix_sel, basis)
        down = jnp.einsum('tei,ih->teh', mixed, w_down)
        coeff = topk_w * expert_scale[topk_idx]
        out = jnp.einsum('teh,te->th', down, coeff)
        shared = jax.nn.silu(xt @ shared_w_gate) * (xt @ shared_w_up) @ shared_w_down
        out = out + shared
        return out.reshape(B, S, H)

    def _L1_attn_ref(x, norm1_w, wq, wk, wv, gk_w1, gk_w2, gk_b, wg, gnorm_w, wo, ffn_norm_w, w_gate, w_up, w_down):
        import jax, jax.numpy as jnp
        import numpy as np
        B, T, D = (2, 256, 256)
        H = 8
        KEY_DIM, VAL_DIM = (128, 256)
        HK, HV = (KEY_DIM // H, VAL_DIM // H)
        LOW_RANK = 16
        GATE_NORM = 16.0
        CHUNK = 64
        HIDDEN = (D * 4 * 2 // 3 + 63) // 64 * 64
        EPS = 1e-06

        def rmsnorm(x, w):
            return x * jax.lax.rsqrt(jnp.mean(x * x, axis=-1, keepdims=True) + EPS) * w

        def _gla(h, wq, wk, wv, gk_w1, gk_w2, gk_b, wg, gnorm_w, wo):
            Bb, Tt, _ = h.shape
            nc = Tt // CHUNK

            def split(t, hd):
                t = t.reshape(Bb, nc, CHUNK, H, hd)
                return jnp.transpose(t, (1, 0, 3, 2, 4))
            q = split(h @ wq, HK) * HK ** (-0.5)
            k = split(h @ wk, HK)
            v = split(h @ wv, HV)
            g = split(jax.nn.log_sigmoid(h @ gk_w1 @ gk_w2 + gk_b) / GATE_NORM, HK)
            mask = jnp.tril(jnp.ones((CHUNK, CHUNK), jnp.float32))

            def step(S, inp):
                qc, kc, vc, gc = inp
                b = jnp.cumsum(gc, axis=-2)
                qe = qc * jnp.exp(b)
                A = jnp.einsum('bhik,bhjk->bhij', qe, kc * jnp.exp(-b)) * mask
                o = jnp.einsum('bhck,bhkv->bhcv', qe, S) + jnp.einsum('bhij,bhjv->bhiv', A, vc)
                bl = b[:, :, -1:, :]
                S = jnp.exp(bl[:, :, 0, :])[..., None] * S + jnp.einsum('bhck,bhcv->bhkv', kc * jnp.exp(bl - b), vc)
                return (S, o)
            S0 = jnp.zeros((Bb, H, HK, HV), h.dtype)
            _, o = jax.lax.scan(step, S0, (q, k, v, g))
            o = jnp.transpose(o, (1, 0, 3, 2, 4)).reshape(Bb, Tt, H, HV)
            gate = (h @ wg).reshape(Bb, Tt, H, HV)
            o = rmsnorm(o, gnorm_w) * gate * jax.nn.sigmoid(gate)
            return o.reshape(Bb, Tt, VAL_DIM) @ wo
        h = rmsnorm(x, norm1_w)
        x = x + _gla(h, wq, wk, wv, gk_w1, gk_w2, gk_b, wg, gnorm_w, wo)
        h2 = rmsnorm(x, ffn_norm_w)
        ffn = jax.nn.silu(h2 @ w_gate) * (h2 @ w_up) @ w_down
        return x + ffn

    def _L1_ffn_ref(x, w_gate, w_up, w_down):
        import jax, jax.numpy as jnp
        import numpy as np

        def _sparsify_2to4(h):
            B, S, I = h.shape
            g = h.reshape(B, S, I // 4, 4)
            a = jnp.abs(g)
            _, idx = jax.lax.top_k(a, 2)
            pos = jnp.arange(4)
            mask = (pos == idx[..., 0:1]) | (pos == idx[..., 1:2])
            return (g * mask.astype(g.dtype)).reshape(B, S, I)
        h = jax.nn.silu(jnp.einsum('bsh,hi->bsi', x, w_gate)) * jnp.einsum('bsh,hi->bsi', x, w_up)
        h_sparse = _sparsify_2to4(h)
        return jnp.einsum('bsi,ih->bsh', h_sparse, w_down)
    x = L0_attn_x
    mod = (_silu(L0_c) @ L0_wmod).reshape(L0_c.shape[0], 6, 1, -1)
    sa, ca, ga, sb, cb, gb = (mod[:, 0], mod[:, 1], mod[:, 2], mod[:, 3], mod[:, 4], mod[:, 5])
    ga = (2 * (ga >= 0) - 1) * jnp.maximum(jnp.abs(ga), 0.25)
    gb = (2 * (gb >= 0) - 1) * jnp.maximum(jnp.abs(gb), 0.25)
    h = _layernorm(x, axis=-1) * (1 + ca) + sa
    x = x + ga * _L0_attn_ref(h, L0_attn_W_Q, L0_attn_W_K, L0_attn_W_V, L0_attn_W_O)
    h = _layernorm(x, axis=-1) * (1 + cb) + sb
    x = x + gb * _L0_ffn_ref(h, L0_ffn_w_router, L0_ffn_w_gate, L0_ffn_w_up, L0_ffn_w_down, L0_ffn_amplitudes, L0_ffn_expert_scale, L0_ffn_shared_w_gate, L0_ffn_shared_w_up, L0_ffn_shared_w_down)
    mod = (_silu(L1_c) @ L1_wmod).reshape(L1_c.shape[0], 6, 1, -1)
    sa, ca, ga, sb, cb, gb = (mod[:, 0], mod[:, 1], mod[:, 2], mod[:, 3], mod[:, 4], mod[:, 5])
    ga = (2 * (ga >= 0) - 1) * jnp.maximum(jnp.abs(ga), 0.25)
    gb = (2 * (gb >= 0) - 1) * jnp.maximum(jnp.abs(gb), 0.25)
    h = _layernorm(x, axis=-1) * (1 + ca) + sa
    x = x + ga * _L1_attn_ref(h, L1_attn_norm1_w, L1_attn_wq, L1_attn_wk, L1_attn_wv, L1_attn_gk_w1, L1_attn_gk_w2, L1_attn_gk_b, L1_attn_wg, L1_attn_gnorm_w, L1_attn_wo, L1_attn_ffn_norm_w, L1_attn_w_gate, L1_attn_w_up, L1_attn_w_down)
    h = _layernorm(x, axis=-1) * (1 + cb) + sb
    x = x + gb * _L1_ffn_ref(h, L1_ffn_w_gate, L1_ffn_w_up, L1_ffn_w_down)
    return x

_drawn_inputs = setup_inputs


def setup_inputs(seed=0):
    import zlib

    import numpy as np

    out = dict(_drawn_inputs(seed))
    spreads = {'L0_ffn_expert_scale': (1.0, 0.6),
     'L1_attn_norm1_w': (1.0, 0.6),
     'L1_attn_gk_b': (0.0, 0.8),
     'L1_attn_gnorm_w': (1.0, 0.6),
     'L1_attn_ffn_norm_w': (1.0, 0.6)}
    factors = {'L0_attn_W_Q': 8.0,
     'L0_attn_W_K': 8.0,
     'L0_attn_W_V': 6.335,
     'L0_attn_W_O': 6.218,
     'L0_ffn_w_router': 8.0,
     'L0_ffn_w_gate': 8.0,
     'L0_ffn_w_up': 8.0,
     'L0_ffn_w_down': 8.0,
     'L0_ffn_amplitudes': 8.0,
     'L0_ffn_shared_w_gate': 8.0,
     'L0_ffn_shared_w_up': 8.0,
     'L0_ffn_shared_w_down': 8.0,
     'L0_c': 5.524,
     'L0_wmod': 5.493,
     'L1_attn_wq': 3.811,
     'L1_attn_wk': 3.826,
     'L1_attn_wv': 3.786,
     'L1_attn_gk_w1': 8.0,
     'L1_attn_gk_w2': 8.0,
     'L1_attn_wg': 3.855,
     'L1_attn_wo': 3.806,
     'L1_attn_w_gate': 7.109,
     'L1_attn_w_up': 7.053,
     'L1_attn_w_down': 7.041,
     'L1_ffn_w_gate': 3.005,
     'L1_ffn_w_up': 2.797,
     'L1_ffn_w_down': 2.796}
    for name, (base, spread) in spreads.items():
        noise = np.random.default_rng([zlib.crc32(name.encode()), seed]).standard_normal(out[name].shape)
        drawn = base * np.exp(spread * noise) if base else spread * noise
        out[name] = jnp.asarray(drawn.astype(out[name].dtype))
    for name, factor in factors.items():
        out[name] = (out[name] * factor).astype(out[name].dtype)
    return out
```

```python
from contextlib import ExitStack

import concourse.bass as bass
from concourse import mybir

ALU = mybir.AluOpType
ACT = mybir.ActivationFunctionType
AX = mybir.AxisListType
F32 = mybir.dt.float32
F32R = mybir.dt.float32r
BF16 = mybir.dt.bfloat16

P = 128
B, S, D = 8, 512, 256
TILES = S // P
KD = D // P
NH, DH = 16, 128
PAIRS = NH // 2
LN_EPS = 1e-5
MODS = 6
SA, CA, GA, SB, CB, GB = range(MODS)
MASKED = -1.0e30


class Signal:

    def __init__(self, sem, per, credit=0):
        self.sem, self.per, self.credit = sem, per, credit

    def done(self, r):
        return self.after(r, self.per)

    def after(self, r, k):
        return r * self.per + (self.credit + k)

    def before(self, r, k, back=1):
        return r * self.per + (self.credit + k - back * self.per)


def wait_on(eng, sem, value):
    eng.wait_ge(sem, value)


class Apart:
    passed = None


def wait_apart(eng, sem, value):
    eng.wait_ge(sem, value)
    eng.sem_inc(Apart.passed, 1)


def products(nc, out, still, moving, start, stop, **kw):
    nc.tensor.matmul(out, still[0], moving[0], start=start, stop=False, **kw)
    nc.tensor.matmul(out, still[0], moving[1], start=False, stop=False, **kw)
    return nc.tensor.matmul(out, still[1], moving[0], start=False, stop=stop, **kw)


def low(nc, out, whole, high):
    return nc.vector.tensor_tensor(out, whole, high.bitcast(F32), ALU.subtract)


class Alloc:
    def __init__(self, nc, ctx, prefix):
        self.nc, self.ctx, self.prefix, self.sems = nc, ctx, prefix, []

    def sb(self, name, shape, dt=F32):
        return self.ctx.enter_context(self.nc.sbuf_tensor(f"{self.prefix}_{name}", shape, dt))

    def ps(self, name, shape, dt=F32):
        return self.ctx.enter_context(self.nc.psum_tensor(f"{self.prefix}_{name}", shape, dt))

    def sem(self, name):
        self.sems.append(self.ctx.enter_context(self.nc.semaphore(f"{self.prefix}_{name}")))
        return self.sems[-1]

    def begin(self):
        self.body = ExitStack()
        return self.body.enter_context(self.nc.Block())

    def end(self):
        self.body.close()
        with self.nc.Block() as block:
            @block.sync
            def _(sp):
                for s in self.sems:
                    sp.sem_clear(s)

    def counted(self, name, per, credit=0):
        return Signal(self.sem(name), per, credit)


def modulation_stage(nc, io, keep):
    with ExitStack() as ctx:
        m = Alloc(nc, ctx, "mod")
        c_in = m.sb("c_in", [P, 2, KD, B])
        c_act = m.sb("c_act", [P, 2, KD, B])
        wmod = m.sb("wmod", [P, 2, KD, MODS * D])
        rows = m.sb("rows", [B, 2, MODS * D])
        gates = m.sb("gates", [B, 2, 2, D])
        signs = m.sb("signs", [B, 2, 2, D])
        col_ps = m.ps("col_ps", [P, 2, MODS * KD, B])
        row_ps = m.ps("row_ps", [B, MODS * D])
        loaded = m.sem("loaded")
        zeroed = m.sem("zeroed")
        consts_made = m.sem("consts_made")
        c_ready = m.sem("c_ready")
        cols_done = m.sem("cols_done")
        rows_done = m.sem("rows_done")
        rows_copied = m.sem("rows_copied")
        chain = m.sem("chain")
        rows_final = m.sem("rows_final")
        stored = m.sem("stored")
        block = m.begin()

        @block.sync
        def _(sp):
            for l in range(2):
                sp.dma_start(c_in[:, l], io[f"c{l}"].rearrange("p (k b) -> p k b", k=KD)).then_inc(loaded, 16)
            for l in range(2):
                sp.dma_start(wmod[:, l], io[f"wmod{l}"].rearrange("(k p) n -> p k n", p=P)).then_inc(loaded, 16)
            sp.wait_ge(rows_final, 1)
            for l in range(2):
                sp.dma_start(io["mod_rows"][l], rows[:, l]).then_inc(stored, 16)
            sp.wait_ge(stored, 32)

        @block.gpsimd
        def _(pool):
            nc.gpsimd.memset(keep["ident"][:], 0.0).then_inc(zeroed, 1)
            nc.gpsimd.memset(keep["causal"][:], 0.0).then_inc(zeroed, 1)
            pool.wait_ge(zeroed, 2)
            nc.gpsimd.affine_select(out=keep["ident"][:], in_=keep["ident"][:], compare_op=ALU.not_equal, fill=1.0,
                                    base=0, pattern=[[-1, P]], channel_multiplier=1).then_inc(consts_made, 1)
            last = keep["causal"][:, S - P:S]
            nc.gpsimd.affine_select(out=last, in_=last, compare_op=ALU.is_ge, fill=MASKED,
                                    base=0, pattern=[[-1, P]], channel_multiplier=1).then_inc(consts_made, 1)

        @block.scalar
        def _(act):
            act.wait_ge(loaded, 64)
            nc.scalar.activation(c_act[:], c_in[:], ACT.Silu).then_inc(c_ready, 1)

        @block.tensor
        def _(pe):
            pe.wait_ge(c_ready, 1)
            for l in range(2):
                for n in range(MODS * KD):
                    for k in range(KD):
                        mm = nc.tensor.matmul(col_ps[:, l, n, :], wmod[:, l, k, n * P:(n + 1) * P], c_act[:, l, k, :],
                                              start=(k == 0), stop=(k == KD - 1))
            mm.then_inc(cols_done, 1)
            for l in range(2):
                if l:
                    pe.wait_ge(rows_copied, l)
                for n in range(0, MODS * D, 512):
                    for k in range(KD):
                        mm = nc.tensor.matmul(row_ps[:, n:n + 512], c_act[:, l, k, :], wmod[:, l, k, n:n + 512],
                                              start=(k == 0), stop=(k == KD - 1))
                mm.then_inc(rows_done, 1)

        @block.vector
        def _(dve):
            dve.wait_ge(cols_done, 1)
            nc.vector.tensor_copy(keep["mod"][:], col_ps[:]).then_inc(chain, 1)
            dve.wait_ge(chain, 1)
            for l in range(2):
                for n in (CA, CB):
                    one_plus = keep["mod"][:, l, n * KD:(n + 1) * KD, :]
                    last = nc.vector.tensor_scalar(one_plus, one_plus, 1.0, None, ALU.add)
            for l in range(2):
                dve.wait_ge(rows_done, l + 1)
                nc.vector.tensor_copy(rows[:, l], row_ps[:]).then_inc(rows_copied, 1)
            dve.wait_ge(rows_copied, 2)
            for l in range(2):
                g = rows[:, l].rearrange("b (h m d) -> b h m d", h=2, m=3)[:, :, 2, :]
                last = nc.vector.tensor_scalar(signs[:, l], g, 0.0, 2.0, ALU.is_ge, ALU.mult)
                for h in range(2):
                    nc.vector.scalar_tensor_tensor(gates[:, l, h], g[:, h], -1.0, g[:, h], ALU.mult, ALU.max)
                one = rows[:, l, CA * D:(CA + 1) * D]
                last = nc.vector.tensor_scalar(one, one, 1.0, None, ALU.add)
            last.then_inc(chain, 1)
            dve.wait_ge(chain, 2)
            nc.vector.tensor_scalar(gates[:], gates[:], 0.25, None, ALU.max).then_inc(chain, 1)
            dve.wait_ge(chain, 3)
            for l in range(2):
                g = rows[:, l].rearrange("b (h m d) -> b h m d", h=2, m=3)[:, :, 2, :]
                for h in range(2):
                    last = nc.vector.scalar_tensor_tensor(g[:, h], signs[:, l, h], -1.0, gates[:, l, h], ALU.add, ALU.mult)
            last.then_inc(rows_final, 1)
        m.end()


def moments_of_rows(nc, link, x, stats, mv, var_eps):
    for t in range(TILES):
        last = nc.vector.bn_stats(stats[:, t, :], x[:, t, :])
    link(last, wait_apart)
    for t in range(TILES):
        last = nc.vector.bn_aggr(mv[:, t, :], stats[:, t, :])
    link(last)
    return nc.vector.tensor_scalar(var_eps[:], mv[:, :, 1], LN_EPS, None, ALU.add)


def root_guess(nc, act, var_eps_ready, logged, r, var_eps, log_var, rstd):
    act.wait_ge(var_eps_ready.sem, var_eps_ready.after(r, 1))
    nc.scalar.activation(log_var[:], var_eps[:], ACT.Ln).then_inc(logged.sem, 1)
    act.wait_ge(logged.sem, logged.after(r, 1))
    return nc.scalar.activation(rstd[:], log_var[:], ACT.Exp, scale=-0.5)


def refine_root(nc, link, var_eps, tmp, rstd):
    link(nc.vector.tensor_tensor(tmp[:], rstd[:], rstd[:], ALU.mult))
    link(nc.vector.scalar_tensor_tensor(tmp[:], tmp[:], -0.5, var_eps[:], ALU.mult, ALU.mult))
    link(nc.vector.scalar_tensor_tensor(rstd[:], tmp[:], 1.5, rstd[:], ALU.add, ALU.mult))


def norm_rows(nc, x, xn, mv, rstd):
    for t in range(TILES):
        last = nc.vector.tensor_scalar(xn[:, t, :], x[:, t, :], mv[:, t, 0:1], rstd[:, t:t + 1],
                                       ALU.subtract, ALU.mult)
    return last


def transpose_rows(nc, out, xn, ident):
    for k in range(KD):
        for t in range(TILES):
            mm = nc.tensor.transpose(out[:, k, t * P:(t + 1) * P], xn[:, t, k * P:(k + 1) * P], ident[:])
    return mm


def attention_stage(nc, io, keep):
    scale = DH ** -0.5
    off = [P * (i * (i + 1) // 2) for i in range(TILES + 1)]
    pt_off = [0, 512, 896, 1152]
    pt_bank = [(0, 0), (1, 0), (2, 0), (2, 256)]
    pt_groups = [(0, 0, 512), (1, 512, 896), (2, 896, 1280)]
    s_place = [(0, 0), (0, P), (1, 0), (2, 0)]
    ident = keep["ident"]
    with ExitStack() as ctx:
        m = Alloc(nc, ctx, "att")
        w_qk = m.sb("w_qk", [P, NH, 4, KD * P], F32R)
        w_v = [m.sb(f"w_v{i}", [P, PAIRS, KD, 2 * DH], F32R) for i in "hl"]
        w_o = [m.sb(f"w_o{i}", [P, NH, D], F32R) for i in "hl"]
        raw = m.sb("raw", [P, 4, 512])
        staged = m.sb("staged", [P, 2, 4, KD * P], F32R)
        x_in = m.sb("x_in", [P, TILES, D])
        x_res = m.sb("x_res", [P, TILES, D])
        xn = m.sb("xn", [P, TILES, D])
        gate = m.sb("gate", [P, D])
        hT = [m.sb(f"hT{i}", [P, KD, S], F32R) for i in "hl"]
        qkT = [m.sb(f"qkT{i}", [P, 2, S], F32R) for i in "hl"]
        v = [m.sb(f"v{i}", [P, TILES, 2 * DH], F32R) for i in "hl"]
        probs = m.sb("probs", [P, off[TILES]])
        probs_t = [m.sb(f"probs_t{i}", [P, off[TILES]], F32R) for i in "hl"]
        zT = [m.sb(f"zT{i}", [P, S], F32R) for i in "hl"]
        stats = m.sb("stats", [P, TILES, 6])
        mv = m.sb("mv", [P, TILES, 2])
        rstd = m.sb("rstd", [P, TILES])
        var_eps = m.sb("var_eps", [P, TILES])
        log_var = m.sb("log_var", [P, TILES])
        top = m.sb("top", [P, TILES])
        neg_top = m.sb("neg_top", [P, TILES])
        total = m.sb("total", [P, TILES])
        inv_total = m.sb("inv_total", [P, TILES])
        proj = m.ps("proj", [P, 2, 512])
        work = m.ps("work", [P, 3, 512])
        z_ps = m.ps("z_ps", [P, 512])
        o_ps = m.ps("o_ps", [P, TILES, D])

        x_loaded = m.counted("x_loaded", 16)
        res_loaded = m.counted("res_loaded", 32)
        raw_loaded = keep["raw_loaded"]
        w_high = m.counted("w_high", 4)
        w_split = m.counted("w_split", 4)
        stage_loaded = [m.counted(f"stage_loaded{a}", 16) for a in range(2)]
        link_b = m.counted("link_b", 7)
        var_ready = m.counted("var_ready", 1)
        logged = m.counted("logged", 1)
        rstd_guessed = m.counted("rstd_guessed", 1)
        link_h = m.counted("link_h", 2)
        ln_done = m.counted("ln_done", 1)
        ht_in_psum = m.counted("ht_in_psum", 1)
        ht_whole = m.counted("ht_whole", 1)
        ht_ready = m.counted("ht_ready", 1)
        qk_done = m.counted("qk_done", 1, credit=2)
        qk_high = m.counted("qk_high", 1)
        qk_low = m.counted("qk_low", 1)
        v_done = m.counted("v_done", 1)
        v_high = m.counted("v_high", 1)
        v_low = m.counted("v_low", 1)
        s_done = m.counted("s_done", 3)
        top_ready = m.counted("top_ready", 1)
        exp_done = m.counted("exp_done", 1)
        probs_ready = m.counted("probs_ready", 1)
        pt_done = m.counted("pt_done", 3)
        pt_high = m.counted("pt_high", 3)
        pt_low = m.counted("pt_low", 3)
        z_done = m.counted("z_done", 1)
        z_high = m.counted("z_high", 1)
        z_low = m.counted("z_low", 1)
        o_done = m.counted("o_done", 1)
        y_done = m.counted("y_done", 1, credit=1)
        y_stored = m.counted("y_stored", 16, credit=16)
        whole_hT = xn[:].rearrange("p t d -> p (t d)").rearrange("p (k s) -> p k s", k=KD)
        block = m.begin()

        def batches(eng):
            return eng.Fori(0, B)

        def pairs(eng, pair, b):
            pair(b, 0, True, False)
            with eng.Fori(1, PAIRS - 1) as p:
                pair(b, p, False, False)
            pair(b, PAIRS - 1, False, True)

        @block.sync
        def _(sp):
            sp.sem_inc(qk_done.sem, qk_done.credit)
            sp.sem_inc(y_done.sem, y_done.credit)
            sp.sem_inc(y_stored.sem, y_stored.credit)
            with batches(sp) as b:
                wait_apart(sp, y_done.sem, y_done.before(b, 1))
                sp.dma_start(x_in[:], io["x"][bass.ds(b * S, S), :].rearrange("(t p) d -> p t d", p=P)).then_inc(x_loaded.sem, 16)
                sp.dma_start(x_res[:], io["x"][bass.ds(b * S, S), :].rearrange("(t p) d -> p t d", p=P)).then_inc(res_loaded.sem, 16)
                sp.dma_start(gate[:], io["mod_rows"][0, bass.ds(b, 1), GA * D:(GA + 1) * D].to_broadcast([P, D])).then_inc(res_loaded.sem, 16)
                with sp.Fori(0, PAIRS) as p:
                    for a in range(2):
                        g = b * NH + p * 2 + a
                        wait_apart(sp, w_split.sem, w_split.after(p, 4))
                        wait_apart(sp, qk_done.sem, qk_done.before(g, 1, back=2))
                        sp.dma_start(staged[:, a].bitcast(F32), w_qk[:, bass.ds(p * 2 + a, 1)].rearrange("p o m n -> p (o m) n").bitcast(F32)).then_inc(stage_loaded[a].sem, 16)
                wait_apart(sp, y_done.sem, y_done.after(b, 1))
                sp.dma_start(io["x1"][bass.ds(b * S, S), :].rearrange("(t p) d -> p t d", p=P), xn[:]).then_inc(y_stored.sem, 16)
            sp.wait_ge(y_stored.sem, y_stored.after(B - 1, 16))

        @block.gpsimd
        def _(pool):
            def fetch(n, p):
                if n < 2:
                    src = io["wqk"][:, bass.ds(p * 2, 2), n, :]
                    dst = raw[:, n].rearrange("p (h n) -> p h n", h=2)
                elif n == 2:
                    src, dst = io["wv"][:, bass.ds(p, 1), :].rearrange("p o n -> p (o n)"), raw[:, n]
                else:
                    src, dst = io["wo"][:, bass.ds(p, 1), :].rearrange("p o n -> p (o n)"), raw[:, n]
                pool.dma_start(dst, src).then_inc(raw_loaded[n].sem, 16)

            def place(n, p, half):
                if n < 2:
                    return w_qk[:, bass.ds(p * 2, 2), 2 * n + half, :], raw[:, n].rearrange("p (h n) -> p h n", h=2)
                if n == 2:
                    return w_v[half][:, bass.ds(p, 1)].rearrange("p o k n -> p (o k n)"), raw[:, n]
                return w_o[half][:, bass.ds(p * 2, 2)].rearrange("p h n -> p (h n)"), raw[:, n]

            def split(p, more):
                for n in range(4):
                    pool.wait_ge(raw_loaded[n].sem, raw_loaded[n].after(p, 16))
                    dst, src = place(n, p, 0)
                    nc.gpsimd.tensor_copy(dst, src).then_inc(w_high.sem, 1)
                    pool.wait_ge(w_high.sem, w_high.after(p, n + 1))
                    dst, src = place(n, p, 1)
                    nc.gpsimd.tensor_tensor(dst, src, place(n, p, 0)[0].bitcast(F32), ALU.subtract).then_inc(w_split.sem, 1)
                    if more:
                        wait_apart(pool, w_split.sem, w_split.after(p, n + 1))
                        fetch(n, p + 1)

            for n in range(4):
                fetch(n, 0)
            with pool.Fori(0, PAIRS - 1) as p:
                split(p, True)
            split(PAIRS - 1, False)

        @block.tensor
        def _(pe):
            def project_qk(g, a):
                for w in range(2):
                    for k in range(KD):
                        at = slice(k * P, (k + 1) * P)
                        mm = products(nc, proj[:, w, :], (staged[:, a, 2 * w, at], staged[:, a, 2 * w + 1, at]),
                                      (hT[0][:, k, :], hT[1][:, k, :]), k == 0, k == KD - 1)
                mm.then_inc(qk_done.sem, 1)

            def project_v(b, p):
                pe.wait_ge(w_split.sem, w_split.after(p, 4))
                for t in range(TILES):
                    for k in range(KD):
                        at = slice(t * P, (t + 1) * P)
                        mv_ = tuple(w_v[i][:, bass.ds(p, 1), k, :].rearrange("p o n -> p (o n)") for i in range(2))
                        mm = products(nc, proj[:, t // 2, (t % 2) * D:(t % 2 + 1) * D],
                                      (hT[0][:, k, at], hT[1][:, k, at]), mv_, k == 0, k == KD - 1)
                mm.then_inc(v_done.sem, 1)

            def scores(g):
                pe.wait_ge(qk_low.sem, qk_low.after(g, 1))
                for i in range(TILES):
                    bank, col = s_place[i]
                    at = slice(i * P, (i + 1) * P)
                    keys = slice(0, (i + 1) * P)
                    mm = products(nc, work[:, bank, col:col + (i + 1) * P], (qkT[0][:, 0, at], qkT[1][:, 0, at]),
                                  (qkT[0][:, 1, keys], qkT[1][:, 1, keys]), True, True)
                    if i:
                        mm.then_inc(s_done.sem, 1)

            def transpose_probs(g):
                pe.wait_ge(probs_ready.sem, probs_ready.after(g, 1))
                for j in range(TILES):
                    bank, col = pt_bank[j]
                    for i in range(j, TILES):
                        c = col + (i - j) * P
                        mm = nc.tensor.transpose(work[:, bank, c:c + P], probs[:, off[i] + j * P:off[i] + (j + 1) * P], ident[:])
                    if j != 2:
                        mm.then_inc(pt_done.sem, 1)

            def times_v(g, a):
                for j in range(TILES):
                    if j < 3:
                        pe.wait_ge(pt_low.sem, pt_low.after(g, j + 1))
                    at = slice(pt_off[j], pt_off[j] + S - j * P)
                    head = slice(a * DH, (a + 1) * DH)
                    mm = products(nc, z_ps[:, j * P:S], (v[0][:, j, head], v[1][:, j, head]),
                                  (probs_t[0][:, at], probs_t[1][:, at]), j == 0, j == TILES - 1, skip_group_check=True)
                mm.then_inc(z_done.sem, 1)

            def project_out(g, h, first):
                pe.wait_ge(z_low.sem, z_low.after(g, 1))
                for t in range(TILES):
                    at = slice(t * P, (t + 1) * P)
                    for c, (i, j) in enumerate(((0, 0), (0, 1), (1, 0))):
                        mm = nc.tensor.matmul(o_ps[:, t, :], zT[i][:, at], w_o[j][:, bass.ds(h, 1), :].rearrange("p o n -> p (o n)"),
                                              start=(first and t % 2 == 0 and c == 0), stop=True, skip_group_check=True)
                return mm

            def pair(b, p, first, last):
                r = b * PAIRS + p
                for a in range(2):
                    g = r * 2 + a
                    scores(g)
                    if a == 0:
                        pe.wait_ge(v_low.sem, v_low.after(r, 1))
                    if not (last and a == 1):
                        nxt = stage_loaded[1 - a]
                        pe.wait_ge(nxt.sem, nxt.after(r + a, 16))
                        project_qk(g + 1, 1 - a)
                    transpose_probs(g)
                    if not (first and a == 0):
                        project_out(g - 1, p * 2 + a - 1, first and a == 1)
                    times_v(g, a)
                if not last:
                    pe.wait_ge(qk_low.sem, qk_low.after(r * 2 + 2, 1))
                    project_v(b, p + 1)
                else:
                    project_out(r * 2 + 1, NH - 1, False).then_inc(o_done.sem, 1)

            with batches(pe) as b:
                pe.wait_ge(ln_done.sem, ln_done.after(b, 1))
                transpose_rows(nc, proj, xn, ident).then_inc(ht_in_psum.sem, 1)
                pe.wait_ge(ht_ready.sem, ht_ready.after(b, 1))
                pe.wait_ge(stage_loaded[0].sem, stage_loaded[0].after(b * PAIRS, 16))
                project_qk(b * NH, 0)
                pe.wait_ge(qk_low.sem, qk_low.after(b * NH, 1))
                project_v(b, 0)
                pe.wait_ge(y_done.sem, y_done.before(b, 1))
                pairs(pe, pair, b)

        @block.scalar
        def _(act):
            def qk_halves(g):
                act.wait_ge(qk_done.sem, qk_done.after(g, 1))
                nc.scalar.activation(qkT[0][:], proj[:], ACT.Copy).then_inc(qk_high.sem, 1)

            def v_halves(r):
                act.wait_ge(v_done.sem, v_done.after(r, 1))
                nc.scalar.activation(v[0][:], proj[:].rearrange("p w (t n) -> p (w t) n", t=2), ACT.Copy).then_inc(v_high.sem, 1)

            def pair(b, p, first, last):
                r = b * PAIRS + p
                for a in range(2):
                    g = r * 2 + a
                    act.wait_ge(top_ready.sem, top_ready.after(g, 1))
                    for i in range(TILES):
                        row = probs[:, off[i]:off[i + 1]]
                        last_exp = nc.scalar.activation(row, row, ACT.Exp, bias=neg_top[:, i:i + 1], scale=scale,
                                                        accum_out=total[:, i:i + 1])
                    last_exp.then_inc(exp_done.sem, 1)
                    if not (last and a == 1):
                        qk_halves(g + 1)
                    for n, (bank, lo, hi) in enumerate(pt_groups):
                        act.wait_ge(pt_done.sem, pt_done.after(g, n + 1))
                        nc.scalar.activation(probs_t[0][:, lo:hi], work[:, bank, 0:hi - lo], ACT.Copy).then_inc(pt_high.sem, 1)
                    act.wait_ge(z_done.sem, z_done.after(g, 1))
                    nc.scalar.activation(zT[0][:], z_ps[:], ACT.Copy).then_inc(z_high.sem, 1)
                if not last:
                    v_halves(r + 1)

            with batches(act) as b:
                root_guess(nc, act, var_ready, logged, b, var_eps, log_var, rstd).then_inc(rstd_guessed.sem, 1)
                act.wait_ge(ht_in_psum.sem, ht_in_psum.after(b, 1))
                for k in range(KD):
                    mod = [keep["mod"][:, 0, n * KD + k, bass.ds(b, 1)] for n in (CA, SA)]
                    last = nc.scalar.activation(whole_hT[:, k, :], proj[:, k, :], ACT.Identity, bias=mod[1], scale=mod[0])
                last.then_inc(ht_whole.sem, 1)
                qk_halves(b * NH)
                v_halves(b * PAIRS)
                pairs(act, pair, b)

        @block.vector
        def _(dve):
            def qk_halves(g):
                dve.wait_ge(qk_high.sem, qk_high.after(g, 1))
                low(nc, qkT[1][:], proj[:], qkT[0][:]).then_inc(qk_low.sem, 1)

            def v_halves(r):
                dve.wait_ge(v_high.sem, v_high.after(r, 1))
                low(nc, v[1][:], proj[:].rearrange("p w (t n) -> p (w t) n", t=2), v[0][:]).then_inc(v_low.sem, 1)

            def pair(b, p, first, last):
                r = b * PAIRS + p
                for a in range(2):
                    g = r * 2 + a
                    for i in range(TILES):
                        bank, col = s_place[i]
                        if i != 1:
                            wait_apart(dve, s_done.sem, s_done.after(g, max(i, 1)))
                        n = (i + 1) * P
                        ins = nc.vector.tensor_tensor_reduce(
                            out=probs[:, off[i]:off[i + 1]], in0=work[:, bank, col:col + n], in1=keep["causal"][:, S - n:S],
                            scale=1.0, scalar=-3.0e38, op0=ALU.add, op1=ALU.max, accum_out=top[:, i:i + 1])
                    ins.then_inc(link_h.sem, 1)
                    dve.wait_ge(link_h.sem, link_h.after(g, 1))
                    nc.vector.tensor_scalar(neg_top[:], top[:], -scale, None, ALU.mult).then_inc(top_ready.sem, 1)
                    dve.wait_ge(exp_done.sem, exp_done.after(g, 1))
                    nc.vector.reciprocal(inv_total[:], total[:]).then_inc(link_h.sem, 1)
                    dve.wait_ge(link_h.sem, link_h.after(g, 2))
                    for i in range(TILES):
                        row = probs[:, off[i]:off[i + 1]]
                        ins = nc.vector.tensor_scalar(row, row, inv_total[:, i:i + 1], None, ALU.mult)
                    ins.then_inc(probs_ready.sem, 1)
                    if not (last and a == 1):
                        qk_halves(g + 1)
                    for n, (bank, lo, hi) in enumerate(pt_groups):
                        dve.wait_ge(pt_high.sem, pt_high.after(g, n + 1))
                        low(nc, probs_t[1][:, lo:hi], work[:, bank, 0:hi - lo], probs_t[0][:, lo:hi]).then_inc(pt_low.sem, 1)
                    dve.wait_ge(z_high.sem, z_high.after(g, 1))
                    low(nc, zT[1][:], z_ps[:], zT[0][:]).then_inc(z_low.sem, 1)
                if not last:
                    v_halves(r + 1)

            with batches(dve) as b:
                count = [0]

                def link(ins, wait=wait_on):
                    count[0] += 1
                    ins.then_inc(link_b.sem, 1)
                    wait(dve, link_b.sem, link_b.after(b, count[0]))

                dve.wait_ge(x_loaded.sem, x_loaded.after(b, 16))
                dve.wait_ge(y_stored.sem, y_stored.before(b, 16))
                moments_of_rows(nc, link, x_in, stats, mv, var_eps).then_inc(var_ready.sem, 1)
                dve.wait_ge(rstd_guessed.sem, rstd_guessed.after(b, 1))
                refine_root(nc, link, var_eps, log_var, rstd)
                norm_rows(nc, x_in, xn, mv, rstd).then_inc(ln_done.sem, 1)
                dve.wait_ge(ht_whole.sem, ht_whole.after(b, 1))
                link(nc.vector.tensor_copy(hT[0][:], whole_hT))
                low(nc, hT[1][:], whole_hT, hT[0][:]).then_inc(ht_ready.sem, 1)
                qk_halves(b * NH)
                v_halves(b * PAIRS)
                pairs(dve, pair, b)
                dve.wait_ge(o_done.sem, o_done.after(b, 1))
                dve.wait_ge(res_loaded.sem, res_loaded.after(b, 32))
                gate_rows = gate[:].rearrange("p (o d) -> p o d", o=1).to_broadcast([P, TILES, D])
                link(nc.vector.tensor_tensor(xn[:], o_ps[:], gate_rows, ALU.mult))
                nc.vector.tensor_tensor(xn[:], xn[:], x_res[:], ALU.add).then_inc(y_done.sem, 1)
                assert count[0] == link_b.per, count[0]
        m.end()


class SplitWeights:

    def __init__(self, nc, m, io, entries, raw):
        self.nc, self.io, self.entries, self.raw = nc, io, entries, raw
        self.at = {}
        n = 0
        for name, width in entries:
            self.at[name] = slice(n, n + width)
            n += width
        self.halves = [m.sb(f"weights{i}", [P, n], F32R) for i in "hl"]
        self.loaded = [m.sem(f"{name}_loaded") for name, _ in entries]
        self.high = m.sem("weights_high")
        self.ready = m.sem("weights_ready")

    def load(self, sp):
        for (name, _), sem in zip(self.entries, self.loaded):
            sp.dma_start(self.raw[:, self.at[name]], self.io[name]).then_inc(sem, 16)

    def split(self, dve):
        for n, (name, _) in enumerate(self.entries):
            at = self.at[name]
            dve.wait_ge(self.loaded[n], 16)
            self.nc.vector.tensor_copy(self.halves[0][:, at], self.raw[:, at]).then_inc(self.high, 1)
            dve.wait_ge(self.high, n + 1)
            low(self.nc, self.halves[1][:, at], self.raw[:, at], self.halves[0][:, at]).then_inc(self.ready, 1)

    def count(self, name):
        return [n for n, _ in self.entries].index(name) + 1

    def part(self, name, lo, hi):
        start = self.at[name].start
        return tuple(h[:, start + lo:start + hi] for h in self.halves)


def in_batches(eng, body):
    body(0, 0, True, False)
    with eng.Fori(0, B // 2 - 1) as i:
        body(i * 2 + 1, 1, False, False)
        body(i * 2 + 2, 0, False, False)
    body(B - 1, 1, False, True)


class NormedInput:

    def __init__(self, nc, m, io, keep, source, layer, scale, shift, ps, ps_free):
        self.nc, self.io, self.keep, self.source = nc, io, keep, source
        self.layer, self.scale, self.shift, self.ps, self.ps_free = layer, scale, shift, ps, ps_free
        self.x = m.sb("x", [P, 2, TILES, D])
        self.xn = m.sb("xn", [P, TILES, D])
        self.hT = [[m.sb(f"hT{i}{q}", [P, KD, S], F32R) for i in "hl"] for q in range(2)]
        self.stats = m.sb("stats", [P, TILES, 6])
        self.mv = m.sb("mv", [P, TILES, 2])
        self.rstd, self.var_eps, self.log_var = (m.sb(n, [P, TILES]) for n in ("rstd", "var_eps", "log_var"))
        self.x_loaded = [m.counted(f"x_loaded{q}", 16) for q in range(2)]
        self.link_n = m.counted("link_n", 6)
        self.var_ready = m.counted("var_ready", 1)
        self.logged = m.counted("logged", 1)
        self.guessed = m.counted("guessed", 1)
        self.normed = m.counted("normed", 1)
        self.in_psum = m.counted("in_psum", 1)
        self.whole = m.counted("whole", 1)
        self.ready = m.counted("ready", 1)
        self.whole_hT = self.xn[:].rearrange("p t d -> p (t d)").rearrange("p (k s) -> p k s", k=KD)

    def load(self, sp, b, q):
        src = self.io[self.source][bass.ds(b * S, S), :].rearrange("(t p) d -> p t d", p=P)
        sp.dma_start(self.x[:, q], src).then_inc(self.x_loaded[q].sem, 16)

    def norm(self, dve, b, q):
        nc, count = self.nc, [0]

        def link(ins, wait=wait_on):
            count[0] += 1
            ins.then_inc(self.link_n.sem, 1)
            wait(dve, self.link_n.sem, self.link_n.after(b, count[0]))

        dve.wait_ge(self.x_loaded[q].sem, self.x_loaded[q].after((b - q) // 2, 16))
        moments_of_rows(nc, link, self.x[:, q], self.stats, self.mv, self.var_eps).then_inc(self.var_ready.sem, 1)
        dve.wait_ge(self.guessed.sem, self.guessed.after(b, 1))
        refine_root(nc, link, self.var_eps, self.log_var, self.rstd)
        norm_rows(nc, self.x[:, q], self.xn, self.mv, self.rstd).then_inc(self.normed.sem, 1)

    def guess(self, act, b):
        root_guess(self.nc, act, self.var_ready, self.logged, b, self.var_eps, self.log_var, self.rstd).then_inc(self.guessed.sem, 1)

    def transpose(self, pe, b):
        pe.wait_ge(self.normed.sem, self.normed.after(b, 1))
        self.ps_free(pe, b)
        transpose_rows(self.nc, self.ps, self.xn, self.keep["ident"]).then_inc(self.in_psum.sem, 1)

    def modulate(self, act, b):
        act.wait_ge(self.in_psum.sem, self.in_psum.after(b, 1))
        for k in range(KD):
            mod = [self.keep["mod"][:, self.layer, n * KD + k, bass.ds(b, 1)] for n in (self.scale, self.shift)]
            last = self.nc.scalar.activation(self.whole_hT[:, k, :], self.ps[:, k, :], ACT.Identity, bias=mod[1], scale=mod[0])
        last.then_inc(self.whole.sem, 1)

    def halve(self, dve, b, q):
        dve.wait_ge(self.whole.sem, self.whole.after(b, 1))
        self.nc.vector.tensor_copy(self.hT[q][0][:], self.whole_hT).then_inc(self.link_n.sem, 1)
        dve.wait_ge(self.link_n.sem, self.link_n.after(b, 6))
        low(self.nc, self.hT[q][1][:], self.whole_hT, self.hT[q][0][:]).then_inc(self.ready.sem, 1)


def moe_stage(nc, io, keep):
    experts, basis, inner = 128, 8, 128
    wide = basis * inner
    shared = 2 * inner
    row = experts + 8
    top = 4
    with ExitStack() as ctx:
        m = Alloc(nc, ctx, "moe")
        entries = [("router", KD * experts), ("sh_gate", KD * shared), ("sh_up", KD * shared),
                   ("ex_gate", KD * wide), ("ex_up", KD * wide), ("ex_down", D), ("sh_down", 2 * D)]
        raw = m.sb("raw", [P, sum(n for _, n in entries)])
        w = SplitWeights(nc, m, io, entries, raw)
        gate_row = m.sb("gate_row", [P, 2, D])
        amp = m.sb("amp", [P, basis, 2])
        e_scale = m.sb("e_scale", [P, 1])
        mix = m.sb("mix", [P, basis])
        mix_sum = m.sb("mix_sum", [P, 1])
        top_logit = m.sb("top_logit", [P, TILES])
        neg_top = m.sb("neg_top", [P, TILES])
        probs = m.sb("probs", [P, TILES, row])
        rest = m.sb("rest", [P, TILES, row])
        total = m.sb("total", [P, TILES])
        best = m.sb("best", [P, TILES, 8])
        best_sum = m.sb("best_sum", [P, TILES])
        route_t = m.sb("route_t", [P, S])
        coeff = m.sb("coeff", [P, 2, TILES, basis])
        silu = m.sb("silu", [P, 2, wide])
        base = m.sb("base", [P, 2, wide])
        tree = m.sb("tree", [P, wide // 2])
        mixed = m.sb("mixed", [P, 2, inner])
        mixedT = [m.sb(f"mixedT{i}", [P, S], F32R) for i in "hl"]
        sh_silu = m.sb("sh_silu", [P, 2, S])
        sh_hid = m.sb("sh_hid", [P, 2, S])
        sh_hT = [m.sb(f"sh_hT{i}", [P, 2, S], F32R) for i in "hl"]
        y = m.sb("y", [P, TILES, D])
        gu = m.ps("gu", [P, 2, 2, 512])
        route_ps = m.ps("route_ps", [P, 512])
        small_ps = m.ps("small_ps", [P, 512])
        o_ps = m.ps("o_ps", [P, TILES, D])

        amp_loaded = m.sem("amp_loaded")
        mix_link = m.sem("mix_link")
        mix_ready = m.sem("mix_ready")
        row_loaded = [m.counted(f"row_loaded{q}", 16) for q in range(2)]
        link_r = m.counted("link_r", 9)
        logits_done = m.counted("logits_done", 1)
        neg_ready = m.counted("neg_ready", 1)
        exp_done = m.counted("exp_done", 1)
        routed = m.counted("routed", 1)
        rt_done = m.counted("rt_done", 1)
        rt_copied = m.counted("rt_copied", 1)
        coeff_done = m.counted("coeff_done", 1)
        coeff_ready = m.counted("coeff_ready", 1)
        gu_done = m.counted("gu_done", 2)
        silu_done = m.counted("silu_done", 2)
        base_done = m.counted("base_done", 2, credit=2)
        link_m = m.counted("link_m", 1)
        weighed = m.counted("weighed", 1)
        link_p = m.counted("link_p", 2)
        mixed_done = m.counted("mixed_done", 1, credit=2)
        sh_done = m.counted("sh_done", 2)
        sh_silu_done = m.counted("sh_silu_done", 2)
        sh_hid_done = m.counted("sh_hid_done", 2)
        sh_high = m.counted("sh_high", 1)
        sh_low = m.counted("sh_low", 1)
        mt_done = m.counted("mt_done", 4)
        mt_high = m.counted("mt_high", 1)
        mt_low = m.counted("mt_low", 1)
        o_done = m.counted("o_done", 1)
        link_y = m.counted("link_y", 1)
        y_done = m.counted("y_done", 1, credit=1)
        y_stored = m.counted("y_stored", 16, credit=16)
        xin = NormedInput(nc, m, io, keep, "x1", 0, CB, SB, o_ps[:].rearrange("p t d -> p (t d)").rearrange("p (k s) -> p k s", k=KD), lambda pe, b: None)
        block = m.begin()

        def load_batch(sp, b, q):
            xin.load(sp, b, q)
            sp.dma_start(gate_row[:, q], io["mod_rows"][0, bass.ds(b, 1), GB * D:(GB + 1) * D].to_broadcast([P, D])).then_inc(row_loaded[q].sem, 16)

        @block.sync
        def _(sp):
            for s in (base_done, mixed_done, y_done, y_stored):
                sp.sem_inc(s.sem, s.credit)
            load_batch(sp, 0, 0)
            sp.dma_start(amp[:], io["amplitudes"]).then_inc(amp_loaded, 16)
            sp.dma_start(e_scale[:], io["expert_scale"]).then_inc(amp_loaded, 16)
            w.load(sp)

            def store(b):
                wait_apart(sp, y_done.sem, y_done.after(b, 1))
                sp.dma_start(io["x2"][bass.ds(b * S, S), :].rearrange("(t p) d -> p t d", p=P), y[:]).then_inc(y_stored.sem, 16)

            def body(b, q, first, last):
                if not last:
                    wait_apart(sp, y_done.sem, y_done.before(b, 1))
                    load_batch(sp, b + 1, 1 - q)
                if not first:
                    store(b - 1)

            in_batches(sp, body)
            store(B - 1)
            sp.wait_ge(y_stored.sem, y_stored.after(B - 1, 16))

        @block.gpsimd
        def _(pool):
            def body(b, q, first, last):
                for t in range(TILES):
                    n = b * TILES + t
                    pool.wait_ge(mixed_done.sem, mixed_done.before(n, 1))
                    pool.wait_ge(weighed.sem, weighed.after(n, 1))
                    s = t % 2
                    half = wide // 2
                    nc.gpsimd.tensor_tensor(tree[:], base[:, s, 0:half], base[:, s, half:wide], ALU.add).then_inc(link_p.sem, 1)
                    pool.wait_ge(link_p.sem, link_p.after(n, 1))
                    nc.gpsimd.tensor_tensor(tree[:, 0:half // 2], tree[:, 0:half // 2], tree[:, half // 2:half], ALU.add).then_inc(link_p.sem, 1)
                    pool.wait_ge(link_p.sem, link_p.after(n, 2))
                    if t >= 2:
                        pool.wait_ge(mt_done.sem, mt_done.after(b, t - 1))
                    nc.gpsimd.tensor_tensor(mixed[:, s], tree[:, 0:inner], tree[:, inner:2 * inner], ALU.add).then_inc(mixed_done.sem, 1)

            in_batches(pool, body)

        @block.tensor
        def _(pe):
            def gate_up(n, t, q):
                for c in range(2):
                    pe.wait_ge(base_done.sem, base_done.before(n, c + 1))
                    for g, name in enumerate(("ex_gate", "ex_up")):
                        for k in range(KD):
                            at = slice(t * P, (t + 1) * P)
                            col = k * wide + c * 512
                            mm = products(nc, gu[:, c, g, :], (xin.hT[q][0][:, k, at], xin.hT[q][1][:, k, at]),
                                          w.part(name, col, col + 512), k == 0, k == KD - 1)
                    mm.then_inc(gu_done.sem, 1)

            def route(b, q):
                pe.wait_ge(xin.ready.sem, xin.ready.after(b, 1))
                for t in range(TILES):
                    for k in range(KD):
                        at = slice(t * P, (t + 1) * P)
                        mm = products(nc, route_ps[:, t * P:(t + 1) * P], (xin.hT[q][0][:, k, at], xin.hT[q][1][:, k, at]),
                                      w.part("router", k * experts, (k + 1) * experts), k == 0, k == KD - 1)
                mm.then_inc(logits_done.sem, 1)

            def mix_coefficients(b):
                pe.wait_ge(routed.sem, routed.after(b, 1))
                for t in range(TILES):
                    mm = nc.tensor.transpose(route_ps[:, t * P:(t + 1) * P], rest[:, t, 0:experts], keep["ident"][:])
                mm.then_inc(rt_done.sem, 1)
                pe.wait_ge(rt_copied.sem, rt_copied.after(b, 1))
                for t in range(TILES):
                    mm = nc.tensor.matmul(small_ps[:, t * basis:(t + 1) * basis], route_t[:, t * P:(t + 1) * P], mix[:], start=True, stop=True)
                mm.then_inc(coeff_done.sem, 1)

            def shared_up(b, q, after_tile):
                for i in range(2):
                    pe.wait_ge(base_done.sem, after_tile(i))
                    for g, name in enumerate(("sh_gate", "sh_up")):
                        for k in range(KD):
                            col = k * shared + i * P
                            mm = products(nc, gu[:, i, g, :], w.part(name, col, col + P),
                                          (xin.hT[q][0][:, k, :], xin.hT[q][1][:, k, :]), k == 0, k == KD - 1)
                    mm.then_inc(sh_done.sem, 1)

            def turn_mixed(b, t):
                pe.wait_ge(mixed_done.sem, mixed_done.after(b * TILES + t, 1))
                nc.tensor.transpose(small_ps[:, t * P:(t + 1) * P], mixed[:, t % 2], keep["ident"][:]).then_inc(mt_done.sem, 1)

            def down(b):
                pe.wait_ge(mt_low.sem, mt_low.after(b, 1))
                for t in range(TILES):
                    at = slice(t * P, (t + 1) * P)
                    products(nc, o_ps[:, t, :], (mixedT[0][:, at], mixedT[1][:, at]), w.part("ex_down", 0, D), True, False)
                    for i in range(2):
                        mm = products(nc, o_ps[:, t, :], (sh_hT[0][:, i, at], sh_hT[1][:, i, at]),
                                      w.part("sh_down", i * D, (i + 1) * D), False, i == 1)
                mm.then_inc(o_done.sem, 1)

            def body(b, q, first, last):
                pe.wait_ge(coeff_ready.sem, coeff_ready.after(b, 1))
                pe.wait_ge(sh_hid_done.sem, sh_hid_done.after(b, 2))
                for t in range(TILES):
                    gate_up(b * TILES + t, t, q)
                    if t == 0 and not last:
                        pe.wait_ge(y_done.sem, y_done.before(b, 1))
                        xin.transpose(pe, b + 1)
                    if t == 1 and not last:
                        route(b + 1, 1 - q)
                    if t:
                        turn_mixed(b, t - 1)
                turn_mixed(b, TILES - 1)
                if not last:
                    pe.wait_ge(sh_low.sem, sh_low.after(b, 1))
                    shared_up(b + 1, 1 - q, lambda i: base_done.after(b * TILES + TILES - 1, i + 1))
                down(b)
                if not last:
                    mix_coefficients(b + 1)

            xin.transpose(pe, 0)
            pe.wait_ge(w.ready, w.count("sh_down"))
            route(0, 0)
            shared_up(0, 0, lambda i: base_done.credit)
            pe.wait_ge(mix_ready, 1)
            mix_coefficients(0)
            in_batches(pe, body)

        @block.scalar
        def _(act):
            def exponentials(b):
                act.wait_ge(neg_ready.sem, neg_ready.after(b, 1))
                for t in range(TILES):
                    ins = nc.scalar.activation(probs[:, t, 0:experts], route_ps[:, t * P:(t + 1) * P], ACT.Exp,
                                               bias=neg_top[:, t:t + 1], accum_out=total[:, t:t + 1])
                ins.then_inc(exp_done.sem, 1)

            def copy_routes(b):
                act.wait_ge(rt_done.sem, rt_done.after(b, 1))
                nc.scalar.activation(route_t[:], route_ps[:], ACT.Copy).then_inc(rt_copied.sem, 1)

            def shared_silu(b):
                for i in range(2):
                    act.wait_ge(sh_done.sem, sh_done.after(b, i + 1))
                    nc.scalar.activation(sh_silu[:, i, :], gu[:, i, 0, :], ACT.Silu).then_inc(sh_silu_done.sem, 1)

            def shared_high(b):
                if not isinstance(b, int) or b:
                    act.wait_ge(o_done.sem, o_done.after(b - 1, 1))
                act.wait_ge(sh_hid_done.sem, sh_hid_done.after(b, 2))
                nc.scalar.activation(sh_hT[0][:], sh_hid[:], ACT.Copy).then_inc(sh_high.sem, 1)

            def mixed_high(b):
                act.wait_ge(mt_done.sem, mt_done.after(b, TILES))
                nc.scalar.activation(mixedT[0][:], small_ps[:], ACT.Copy).then_inc(mt_high.sem, 1)

            def body(b, q, first, last):
                for t in range(TILES):
                    n = b * TILES + t
                    for c in range(2):
                        act.wait_ge(gu_done.sem, gu_done.after(n, c + 1))
                        nc.scalar.activation(silu[:, t % 2, c * 512:(c + 1) * 512], gu[:, c, 0, :], ACT.Silu).then_inc(silu_done.sem, 1)
                    if t == 0 and not last:
                        xin.guess(act, b + 1)
                        xin.modulate(act, b + 1)
                    if t == 2 and not last:
                        exponentials(b + 1)
                mixed_high(b)
                if not last:
                    shared_silu(b + 1)
                    shared_high(b + 1)
                    copy_routes(b + 1)

            xin.guess(act, 0)
            xin.modulate(act, 0)
            exponentials(0)
            shared_silu(0)
            shared_high(0)
            copy_routes(0)
            in_batches(act, body)

        @block.vector
        def _(dve):
            def route_tops(b, link):
                dve.wait_ge(logits_done.sem, logits_done.after(b, 1))
                link(nc.vector.tensor_reduce(top_logit[:], route_ps[:].rearrange("p (t e) -> p t e", t=TILES), AX.X, ALU.max))
                nc.vector.tensor_scalar(neg_top[:], top_logit[:], -1.0, None, ALU.mult).then_inc(neg_ready.sem, 1)

            def route_weights(b, link):
                dve.wait_ge(exp_done.sem, exp_done.after(b, 1))
                link(nc.vector.reciprocal(total[:], total[:]))
                for t in range(TILES):
                    ins = nc.vector.tensor_scalar(probs[:, t, 0:experts], probs[:, t, 0:experts], total[:, t:t + 1], None, ALU.mult)
                link(ins, wait_apart)
                for t in range(TILES):
                    ins = nc.vector.max(best[:, t, :], probs[:, t, 0:experts])
                link(ins)
                nc.vector.memset(best[:, :, top:8], -1.0)
                link(nc.vector.tensor_reduce(best_sum[:], best[:, :, 0:top], AX.X, ALU.add), wait_apart)
                for t in range(TILES):
                    ins = nc.vector.match_replace(rest[:, t, :], best[:, t, :], probs[:, t, :], 0.0)
                link(ins)
                link(nc.vector.tensor_scalar(best_sum[:], best_sum[:], 1e-8, None, ALU.add))
                link(nc.vector.reciprocal(best_sum[:], best_sum[:]))
                link(nc.vector.tensor_tensor(rest[:], probs[:], rest[:], ALU.subtract))
                for t in range(TILES):
                    ins = nc.vector.tensor_scalar(rest[:, t, :], rest[:, t, :], best_sum[:, t:t + 1], None, ALU.mult)
                ins.then_inc(routed.sem, 1)

            def copy_coefficients(b, q):
                dve.wait_ge(coeff_done.sem, coeff_done.after(b, 1))
                nc.vector.tensor_copy(coeff[:, q], small_ps[:, 0:TILES * basis].rearrange("p (t k) -> p t k", t=TILES)).then_inc(coeff_ready.sem, 1)

            def shared_hidden(b):
                for i in range(2):
                    dve.wait_ge(sh_silu_done.sem, sh_silu_done.after(b, i + 1))
                    nc.vector.tensor_tensor(sh_hid[:, i, :], sh_silu[:, i, :], gu[:, i, 1, :], ALU.mult).then_inc(sh_hid_done.sem, 1)

            def shared_low(b):
                dve.wait_ge(sh_high.sem, sh_high.after(b, 1))
                low(nc, sh_hT[1][:], sh_hid[:], sh_hT[0][:]).then_inc(sh_low.sem, 1)

            def mixed_low(b):
                dve.wait_ge(mt_high.sem, mt_high.after(b, 1))
                low(nc, mixedT[1][:], small_ps[:], mixedT[0][:]).then_inc(mt_low.sem, 1)

            def residual(b, q):
                dve.wait_ge(o_done.sem, o_done.after(b, 1))
                dve.wait_ge(row_loaded[q].sem, row_loaded[q].after((b - q) // 2, 16))
                dve.wait_ge(y_stored.sem, y_stored.before(b, 16))
                rows = gate_row[:, q:q + 1, :].to_broadcast([P, TILES, D])
                nc.vector.tensor_tensor(y[:], o_ps[:], rows, ALU.mult).then_inc(link_y.sem, 1)
                dve.wait_ge(link_y.sem, link_y.after(b, 1))
                nc.vector.tensor_tensor(y[:], y[:], xin.x[:, q], ALU.add).then_inc(y_done.sem, 1)

            def linker(b):
                count = [0]

                def link(ins, wait=wait_on):
                    count[0] += 1
                    ins.then_inc(link_r.sem, 1)
                    wait(dve, link_r.sem, link_r.after(b, count[0]))
                return link, count

            def body(b, q, first, last):
                link, count = linker(b + 1)
                for t in range(TILES):
                    n = b * TILES + t
                    s = t % 2
                    dve.wait_ge(mixed_done.sem, mixed_done.before(n, 1, back=2))
                    for c in range(2):
                        at = slice(c * 512, (c + 1) * 512)
                        dve.wait_ge(silu_done.sem, silu_done.after(n, c + 1))
                        nc.vector.tensor_tensor(base[:, s, at], silu[:, s, at], gu[:, c, 1, :], ALU.mult).then_inc(base_done.sem, 1)
                    dve.wait_ge(base_done.sem, base_done.after(n, 2))
                    grid = base[:, s].rearrange("p (k i) -> p k i", k=basis)
                    by = coeff[:, q, t, :].rearrange("p (k o) -> p k o", o=1).to_broadcast([P, basis, inner])
                    nc.vector.tensor_tensor(grid, grid, by, ALU.mult).then_inc(weighed.sem, 1)
                    if t == 0 and not last:
                        if not first:
                            residual(b - 1, 1 - q)
                        xin.norm(dve, b + 1, 1 - q)
                        xin.halve(dve, b + 1, 1 - q)
                    if t == 0 and last:
                        residual(b - 1, 1 - q)
                    if t == 2 and not last:
                        route_tops(b + 1, link)
                        route_weights(b + 1, link)
                mixed_low(b)
                if not last:
                    shared_hidden(b + 1)
                    shared_low(b + 1)
                    copy_coefficients(b + 1, 1 - q)
                    assert count[0] == link_r.per, count[0]

            nc.vector.memset(probs[:], -1.0)
            xin.norm(dve, 0, 0)
            xin.halve(dve, 0, 0)
            dve.wait_ge(amp_loaded, 32)
            links = [0]

            def link(ins):
                links[0] += 1
                ins.then_inc(mix_link, 1)
                dve.wait_ge(mix_link, links[0])

            link(nc.vector.tensor_tensor(amp[:], amp[:], amp[:], ALU.mult))
            link(nc.vector.tensor_tensor(mix[:], amp[:, :, 0], amp[:, :, 1], ALU.add))
            link(nc.vector.tensor_reduce(mix_sum[:], mix[:], AX.X, ALU.add))
            link(nc.vector.tensor_scalar(mix_sum[:], mix_sum[:], 1e-8, None, ALU.add))
            link(nc.vector.reciprocal(mix_sum[:], mix_sum[:]))
            nc.vector.tensor_scalar(mix[:], mix[:], mix_sum[:, 0:1], e_scale[:, 0:1], ALU.mult, ALU.mult).then_inc(mix_ready, 1)
            w.split(dve)
            link, _ = linker(0)
            route_tops(0, link)
            route_weights(0, link)
            shared_hidden(0)
            shared_low(0)
            copy_coefficients(0, 0)
            in_batches(dve, body)
            residual(B - 1, 1)
        m.end()


class Root:

    def __init__(self, nc, m, name, width):
        self.nc = nc
        self.v, self.log, self.root = (m.sb(f"{name}_{n}", [P, width]) for n in ("v", "log", "root"))
        self.asked, self.logged, self.guessed = (m.counted(f"{name}_{n}", 1) for n in ("asked", "logged", "guessed"))

    def guess(self, act, i):
        root_guess(self.nc, act, self.asked, self.logged, i, self.v, self.log, self.root).then_inc(self.guessed.sem, 1)

    def refine(self, dve, i, link):
        dve.wait_ge(self.guessed.sem, self.guessed.after(i, 1))
        refine_root(self.nc, link, self.v, self.log, self.root)


def gla_stage(nc, io, keep):
    heads, hk, hv, chunk, rank = 8, 16, 32, 64, 16
    keys, vals = heads * hk, heads * hv
    chunks = S // chunk
    inner = 768
    ki = inner // P
    gate_norm = 16.0
    rms_eps = 1e-6
    with ExitStack() as ctx:
        m = Alloc(nc, ctx, "gla")
        entries = [("g_q", KD * keys), ("g_k", KD * keys), ("g_vg", KD * 2 * vals), ("g_o", KD * D),
                   ("g_gate", KD * inner), ("g_up", KD * inner), ("g_down", ki * D)]
        low1 = m.sb("low1", [P, KD, rank])
        low2 = m.sb("low2", [rank, keys])
        low_bias = m.sb("low_bias", [P, 1])
        norm_cols = m.sb("norm_cols", [P, 2, KD])
        gnorm = m.sb("gnorm", [P, hv])
        own_head = m.sb("own_head", [P, heads])
        state_mask = m.sb("state_mask", [P, vals])
        tri = m.sb("tri", [P, chunk])
        carry = m.sb("carry", [P, S])
        one = m.sb("one", [P, 1])

        class Lane:

            def __init__(self, q):
                n = f"{q}_"
                self.q = q
                self.x, self.h0, self.t1 = (m.sb(n + k, [P, TILES, D]) for k in ("x", "h0", "t1"))
                self.rows = m.sb(n + "rows", [P, 3, D])
                self.t2 = m.sb(n + "t2", [P, 1024])
                self.t3 = m.sb(n + "t3", [P, 1024])
                self.hT = [m.sb(f"{n}hT{i}", [P, KD, S], F32R) for i in "hl"]
                self.act = [m.sb(f"{n}act{i}", [P, 2, S], F32R) for i in "hl"]
                area = self.area = m.sb(n + "area", [P, 8192])
                cut = [area[:, i * 512:(i + 1) * 512] for i in range(16)]
                self.eb, self.enb, self.g, self.bs = cut[0:4]
                self.low = area[0:rank, 0:512]
                self.a = area[:, 0:2048].rearrange("p (t n) -> p t n", t=TILES)
                self.qe, self.ke, self.kd = cut[4:7]
                self.kd_tok = area[:, 3584:4096].rearrange("p (t n) -> p t n", t=TILES)
                self.v = area[:, 4096:5120].rearrange("p (t n) -> p t n", t=TILES)
                self.gs = area[:, 5120:6144].rearrange("p (t n) -> p t n", t=TILES)
                self.state = area[:, 6144:8192].rearrange("p (c n) -> p c n", c=chunks)
                self.ebl = m.sb(n + "ebl", [P, chunks])
                self.stats = m.sb(n + "stats", [P, TILES, 6])
                self.mv = m.sb(n + "mv", [P, TILES, 2])
                self.sq = m.sb(n + "sq", [P, TILES])
                self.X = m.ps(n + "X", [P, 2, 512])
                self.Y = m.ps(n + "Y", [P, 2, 512])
                self.Yt = self.Y[:].rearrange("p w n -> p (w n)").rearrange("p (t d) -> p t d", t=TILES)
                self.whole = self.t1[:].rearrange("p t d -> p (t d)").rearrange("p (k s) -> p k s", k=KD)
                self.qx = [t[:].rearrange("p (c h n) -> p c h n", c=2, h=heads) for t in (self.t2, self.t3)]
                self.ln, self.rms1, self.rms2 = (Root(nc, m, n + k, TILES) for k in ("ln", "rms1", "rms2"))
                self.rmsh = Root(nc, m, n + "rmsh", TILES * heads)
                self.loaded = m.counted(n + "loaded", 32)
                self.link = m.counted(n + "link", 24)
                self.alink = m.counted(n + "alink", 1)
                self.h0_done = m.counted(n + "h0_done", 1)
                self.sq1 = m.counted(n + "sq1", 1)
                self.hn_done = m.counted(n + "hn_done", 1)
                self.in_psum = m.counted(n + "in_psum", 3)
                self.whole_done = m.counted(n + "whole_done", 2)
                self.ht_link = m.counted(n + "ht_link", 2)
                self.ht_ready = m.counted(n + "ht_ready", 2)
                self.low_done = m.counted(n + "low_done", 1)
                self.low_copied = m.counted(n + "low_copied", 1)
                self.qk_done = m.counted(n + "qk_done", 1)
                self.gk_done = m.counted(n + "gk_done", 1)
                self.abs_done = m.counted(n + "abs_done", 1)
                self.min_done = m.counted(n + "min_done", 1)
                self.zl_done = m.counted(n + "zl_done", 1)
                self.scan_done = m.counted(n + "scan_done", 1)
                self.exps_done = m.counted(n + "exps_done", 1)
                self.qk_used = m.counted(n + "qk_used", 1)
                self.qx_done = m.counted(n + "qx_done", 4)
                self.vg_done = m.counted(n + "vg_done", 4)
                self.vg_used = m.counted(n + "vg_used", 4)
                self.gs_done = m.counted(n + "gs_done", 1)
                self.kd_done = m.counted(n + "kd_done", 1)
                self.kd_copied = m.counted(n + "kd_copied", 1)
                self.a_done = m.counted(n + "a_done", 4)
                self.a_used = m.counted(n + "a_used", 4)
                self.u_done = m.counted(n + "u_done", 2)
                self.u_used = m.counted(n + "u_used", 2)
                self.state_done = m.counted(n + "state_done", 1)
                self.o_done = m.counted(n + "o_done", 1)
                self.sq2 = m.counted(n + "sq2", 1)
                self.o_used = m.counted(n + "o_used", 1)
                self.on_done = m.counted(n + "on_done", 1)
                self.ot_high = m.counted(n + "ot_high", 1)
                self.ot_ready = m.counted(n + "ot_ready", 1)
                self.wo_done = m.counted(n + "wo_done", 1)
                self.x1_done = m.counted(n + "x1_done", 1)
                self.sq3 = m.counted(n + "sq3", 1)
                self.h2_done = m.counted(n + "h2_done", 1)
                self.gu_done = m.counted(n + "gu_done", ki)
                self.sg_done = m.counted(n + "sg_done", ki)
                self.f_done = m.counted(n + "f_done", ki)
                self.fh_done = m.counted(n + "fh_done", ki)
                self.fl_done = m.counted(n + "fl_done", ki)
                self.down_done = m.counted(n + "down_done", ki)
                self.sum_done = m.counted(n + "sum_done", 1)
                self.plink = m.counted(n + "plink", 1)
                self.y_done = m.counted(n + "y_done", 1, credit=1)
                self.y_stored = m.counted(n + "y_stored", 16, credit=16)

            def linker(self, eng, signal, i):
                count = [0]

                def link(ins, wait=wait_on):
                    count[0] += 1
                    ins.then_inc(signal.sem, 1)
                    wait(eng, signal.sem, signal.after(i, count[0]))
                return link, count

        lanes = [Lane(q) for q in range(2)]
        w = SplitWeights(nc, m, io, entries, lanes[1].area)
        small_loaded = m.sem("small_loaded")
        zeroed = m.sem("zeroed")
        masks_made = m.sem("masks_made")
        block = m.begin()
        ident = keep["ident"]

        def rounds(eng):
            return eng.Fori(0, B // 2)

        @block.sync
        def _(sp):
            for ln in lanes:
                sp.sem_inc(ln.y_done.sem, ln.y_done.credit)
                sp.sem_inc(ln.y_stored.sem, ln.y_stored.credit)
            w.load(sp)
            for dst, name in ((low1[:], "gk_w1"), (low2[:], "gk_w2"), (low_bias[:], "gk_b"), (norm_cols[:], "norm_cols")):
                sp.dma_start(dst, io[name]).then_inc(small_loaded, 16)
            sp.dma_start(gnorm[:], io["gnorm"].to_broadcast([P, hv])).then_inc(small_loaded, 16)
            with rounds(sp) as i:
                for ln in lanes:
                    b = i * 2 + ln.q
                    y = ln.y_done
                    wait_apart(sp, y.sem, y.before(i, 1))
                    sp.dma_start(ln.x[:], io["x2"][bass.ds(b * S, S), :].rearrange("(t p) d -> p t d", p=P)).then_inc(ln.loaded.sem, 16)
                    sp.dma_start(ln.rows[:], io["mod_rows"][1, bass.ds(b, 1), 0:3 * D].rearrange("o (r d) -> o r d", r=3).to_broadcast([P, 3, D])
                                 ).then_inc(ln.loaded.sem, 16)
                for ln in lanes:
                    b = i * 2 + ln.q
                    y = ln.y_done
                    wait_apart(sp, y.sem, y.after(i, 1))
                    sp.dma_start(io["x3"][bass.ds(b * S, S), :].rearrange("(t p) d -> p t d", p=P), ln.t1[:]).then_inc(ln.y_stored.sem, 16)
            for ln in lanes:
                sp.wait_ge(ln.y_stored.sem, ln.y_stored.done(B // 2 - 1))

        @block.gpsimd
        def _(pool):
            for t in (own_head, state_mask, tri, carry, one):
                nc.gpsimd.memset(t[:], 1.0).then_inc(zeroed, 1)
            pool.wait_ge(zeroed, 5)
            nc.gpsimd.memset(carry[:].rearrange("p (c n) -> p c n", c=chunks)[:, :, 0:1], 0.0).then_inc(masks_made, 1)
            for t, pattern in ((own_head[:], [[-hk, heads]]), (state_mask[:].rearrange("p (h n) -> p h n", h=heads), [[-hk, heads], [0, hv]])):
                nc.gpsimd.affine_select(out=t, in_=t, compare_op=ALU.is_ge, fill=0.0, base=0, pattern=pattern,
                                        channel_multiplier=1).then_inc(masks_made, 1)
            pool.wait_ge(masks_made, 3)
            for t, pattern in ((own_head[:], [[hk, heads]]), (state_mask[:].rearrange("p (h n) -> p h n", h=heads), [[hk, heads], [0, hv]])):
                nc.gpsimd.affine_select(out=t, in_=t, compare_op=ALU.is_ge, fill=0.0, base=hk - 1, pattern=pattern,
                                        channel_multiplier=-1).then_inc(masks_made, 1)
            for n in range(2):
                t = tri[n * chunk:(n + 1) * chunk, :]
                pool.wait_ge(masks_made, 5 + n)
                nc.gpsimd.affine_select(out=t, in_=t, compare_op=ALU.is_ge, fill=0.0, base=0, pattern=[[1, chunk]],
                                        channel_multiplier=-1).then_inc(masks_made, 1)
            pool.wait_ge(masks_made, 7)
            pool.wait_ge(small_loaded, 80)

            def spread_queries(ln, i, t):
                if t == 0:
                    pool.wait_ge(ln.qk_used.sem, ln.qk_used.done(i))
                if t >= 2:
                    pool.wait_ge(ln.a_done.sem, ln.a_done.after(i, t - 1))
                for c in range(2):
                    at = slice(t * P + c * chunk, t * P + (c + 1) * chunk)
                    src = ln.qe[:, at].rearrange("p (o n) -> p o n", o=1).to_broadcast([P, heads, chunk])
                    own = own_head[:].rearrange("p (h o) -> p h o", o=1).to_broadcast([P, heads, chunk])
                    ins = nc.gpsimd.tensor_tensor(ln.qx[t % 2][:, c], src, own, ALU.mult)
                ins.then_inc(ln.qx_done.sem, 1)

            def scale_gate(ln, i):
                pool.wait_ge(ln.vg_used.sem, ln.vg_used.done(i))
                g = ln.gs.rearrange("p t n -> p (t n)").rearrange("p (a v) -> p a v", v=hv)
                by = gnorm[:].rearrange("p (o v) -> p o v", o=1).to_broadcast([P, TILES * heads, hv])
                nc.gpsimd.tensor_tensor(g, g, by, ALU.mult).then_inc(ln.gs_done.sem, 1)

            def act_low(ln, i, c):
                pool.wait_ge(ln.fh_done.sem, ln.fh_done.after(i, c + 1))
                src = ln.t1[:].rearrange("p t d -> p (t d)")[:, (c % 2) * 512:(c % 2 + 1) * 512]
                nc.gpsimd.tensor_tensor(ln.act[1][:, c % 2, :], src, ln.act[0][:, c % 2, :].bitcast(F32), ALU.subtract).then_inc(ln.fl_done.sem, 1)

            def last_sum(ln, i):
                pool.wait_ge(ln.sum_done.sem, ln.sum_done.done(i))
                gate = ln.rows[:, 2:3, :].to_broadcast([P, TILES, D])
                nc.gpsimd.tensor_tensor(ln.t1[:], ln.t1[:], gate, ALU.mult).then_inc(ln.plink.sem, 1)
                pool.wait_ge(ln.plink.sem, ln.plink.done(i))
                nc.gpsimd.tensor_tensor(ln.t1[:], ln.t1[:], ln.x[:], ALU.add).then_inc(ln.y_done.sem, 1)

            with rounds(pool) as i:
                for t in range(TILES):
                    for ln in lanes:
                        spread_queries(ln, i, t)
                for ln in lanes:
                    scale_gate(ln, i)
                for c in range(ki):
                    for ln in lanes:
                        act_low(ln, i, c)
                for ln in lanes:
                    last_sum(ln, i)

        @block.tensor
        def _(pe):
            def turn(ln, src):
                return transpose_rows(nc, ln.X, src, ident)

            def inputs(ln, i, ready):
                pe.wait_ge(ready.sem, ready.done(i))
                turn(ln, ln.t1).then_inc(ln.in_psum.sem, 1)

            def projections(ln, i):
                pe.wait_ge(ln.whole_done.sem, ln.whole_done.after(i, 1))
                for k in range(KD):
                    mm = nc.tensor.matmul(ln.X[0:rank, 0, :], low1[:, k, :], ln.whole[:, k, :], start=(k == 0), stop=(k == KD - 1))
                mm.then_inc(ln.low_done.sem, 1)
                pe.wait_ge(ln.ht_ready.sem, ln.ht_ready.after(i, 1))
                for n, name in enumerate(("g_q", "g_k")):
                    for k in range(KD):
                        mm = products(nc, ln.Y[:, n, :], w.part(name, k * keys, (k + 1) * keys),
                                      (ln.hT[0][:, k, :], ln.hT[1][:, k, :]), k == 0, k == KD - 1)
                mm.then_inc(ln.qk_done.sem, 1)

            def decay_logits(ln, i):
                pe.wait_ge(ln.low_copied.sem, ln.low_copied.done(i))
                nc.tensor.matmul(ln.X[:, 1, :], low2[:], ln.low, start=True, stop=True).then_inc(ln.gk_done.sem, 1)

            def values_gates(ln, i, t):
                if t == 0:
                    pe.wait_ge(ln.min_done.sem, ln.min_done.done(i))
                if t >= 2:
                    pe.wait_ge(ln.vg_used.sem, ln.vg_used.after(i, t - 1))
                at = slice(t * P, (t + 1) * P)
                for k in range(KD):
                    mm = products(nc, ln.X[:, t % 2, :], (ln.hT[0][:, k, at], ln.hT[1][:, k, at]),
                                  w.part("g_vg", k * 512, (k + 1) * 512), k == 0, k == KD - 1)
                mm.then_inc(ln.vg_done.sem, 1)

            def keys_by_token(ln, i):
                pe.wait_ge(ln.qk_used.sem, ln.qk_used.done(i))
                pe.wait_ge(ln.vg_used.sem, ln.vg_used.done(i))
                for t in range(TILES):
                    mm = nc.tensor.transpose(ln.X[:, 0, t * P:(t + 1) * P], ln.kd[:, t * P:(t + 1) * P], ident[:])
                mm.then_inc(ln.kd_done.sem, 1)

            def chunk_products(ln, i, t):
                pe.wait_ge(ln.qx_done.sem, ln.qx_done.after(i, t + 1))
                if t >= 2:
                    pe.wait_ge(ln.a_used.sem, ln.a_used.after(i, t - 1))
                elif t == 1:
                    pe.wait_ge(ln.kd_copied.sem, ln.kd_copied.done(i))
                for c in range(2):
                    at = slice(t * P + c * chunk, t * P + (c + 1) * chunk)
                    mm = nc.tensor.matmul(ln.X[c * chunk:(c + 1) * chunk, 1 - t % 2, :], ln.ke[:, at],
                                          ln.qx[t % 2][:, c].rearrange("p h n -> p (h n)"), start=True, stop=True, skip_group_check=True)
                mm.then_inc(ln.a_done.sem, 1)

            def state_updates(ln, i, n):
                if n == 0:
                    pe.wait_ge(ln.kd_copied.sem, ln.kd_copied.done(i))
                else:
                    pe.wait_ge(ln.u_used.sem, ln.u_used.after(i, 1))
                for c in range(4 * n, min(4 * n + 4, chunks - 1)):
                    at = slice((c % 2) * chunk, (c % 2 + 1) * chunk)
                    mm = nc.tensor.matmul(ln.Yt[:, (c % 2) * 2 + c // 2 % 2, :], ln.kd_tok[at, c // 2, :], ln.v[at, c // 2, :], start=True, stop=True)
                mm.then_inc(ln.u_done.sem, 1)

            def outputs(ln, i):
                pe.wait_ge(ln.state_done.sem, ln.state_done.done(i))
                pe.wait_ge(ln.a_used.sem, ln.a_used.done(i))
                for c in range(chunks):
                    t = c // 2
                    at = slice((c % 2) * chunk, (c % 2 + 1) * chunk)
                    nc.tensor.matmul(ln.Yt[at, t, :], ln.qe[:, c * chunk:(c + 1) * chunk], ln.state[:, c, :],
                                     start=True, stop=False, skip_group_check=True)
                    for h in range(heads):
                        mm = nc.tensor.matmul(ln.Yt[at, t, h * hv:(h + 1) * hv], ln.a[at, t, h * chunk:(h + 1) * chunk],
                                              ln.v[at, t, h * hv:(h + 1) * hv], start=False, stop=(h == heads - 1), skip_group_check=True)
                mm.then_inc(ln.o_done.sem, 1)

            def project_out(ln, i):
                pe.wait_ge(ln.ot_ready.sem, ln.ot_ready.done(i))
                for t in range(TILES):
                    at = slice(t * P, (t + 1) * P)
                    for k in range(KD):
                        mm = products(nc, ln.Yt[:, t, :], (ln.hT[0][:, k, at], ln.hT[1][:, k, at]),
                                      w.part("g_o", k * D, (k + 1) * D), k == 0, k == KD - 1)
                mm.then_inc(ln.wo_done.sem, 1)

            def gate_up(ln, i, c):
                if c == 0:
                    pe.wait_ge(ln.ht_ready.sem, ln.ht_ready.done(i))
                else:
                    pe.wait_ge(ln.f_done.sem, ln.f_done.after(i, c))
                for g, name in enumerate(("g_gate", "g_up")):
                    for k in range(KD):
                        col = k * inner + c * P
                        mm = products(nc, ln.X[:, g, :], w.part(name, col, col + P),
                                      (ln.hT[0][:, k, :], ln.hT[1][:, k, :]), k == 0, k == KD - 1)
                mm.then_inc(ln.gu_done.sem, 1)

            def down(ln, i, c):
                pe.wait_ge(ln.fl_done.sem, ln.fl_done.after(i, c + 1))
                for t in range(TILES):
                    at = slice(t * P, (t + 1) * P)
                    for n, (x, y) in enumerate(((0, 0), (0, 1), (1, 0))):
                        mm = nc.tensor.matmul(ln.Yt[:, t, :], ln.act[x][:, c % 2, at], w.part("g_down", c * D, (c + 1) * D)[y],
                                              start=(c == 0 and t % 2 == 0 and n == 0), stop=(c == ki - 1 and n == 2), skip_group_check=True)
                mm.then_inc(ln.down_done.sem, 1)

            pe.wait_ge(small_loaded, 80)
            pe.wait_ge(w.ready, w.count("g_down"))
            with rounds(pe) as i:
                for ln in lanes:
                    inputs(ln, i, ln.hn_done)
                for ln in lanes:
                    projections(ln, i)
                for ln in lanes:
                    decay_logits(ln, i)
                for t in range(TILES):
                    for ln in lanes:
                        values_gates(ln, i, t)
                for ln in lanes:
                    keys_by_token(ln, i)
                for ln in lanes:
                    chunk_products(ln, i, 0)
                for ln in lanes:
                    state_updates(ln, i, 0)
                for ln in lanes:
                    chunk_products(ln, i, 1)
                for ln in lanes:
                    state_updates(ln, i, 1)
                for t in range(2, TILES):
                    for ln in lanes:
                        chunk_products(ln, i, t)
                for ln in lanes:
                    outputs(ln, i)
                for ln in lanes:
                    inputs(ln, i, ln.on_done)
                for ln in lanes:
                    project_out(ln, i)
                for ln in lanes:
                    inputs(ln, i, ln.h2_done)
                for c in range(ki):
                    for ln in lanes:
                        gate_up(ln, i, c)
                        if c:
                            down(ln, i, c - 1)
                for ln in lanes:
                    down(ln, i, ki - 1)

        @block.scalar
        def _(act):
            def squares(ln, i, ready, done):
                act.wait_ge(ready.sem, ready.done(i))
                for t in range(TILES):
                    ins = nc.scalar.activation(ln.t2[:, t * D:(t + 1) * D], ln.h0[:, t, :], ACT.Square, accum_out=ln.sq[:, t:t + 1])
                ins.then_inc(done.sem, 1)

            def whole(ln, i, n):
                act.wait_ge(ln.in_psum.sem, ln.in_psum.after(i, n))
                for k in range(KD):
                    ins = nc.scalar.activation(ln.whole[:, k, :], ln.X[:, k, :], ACT.Copy, scale=norm_cols[:, n // 2, k:k + 1])
                ins.then_inc(ln.whole_done.sem, 1)

            def copy_low(ln, i):
                act.wait_ge(ln.low_done.sem, ln.low_done.done(i))
                nc.scalar.activation(ln.low, ln.X[0:rank, 0, :], ACT.Copy).then_inc(ln.low_copied.sem, 1)

            def decay_logs(ln, i):
                link, _ = ln.linker(act, ln.alink, i)
                act.wait_ge(ln.gk_done.sem, ln.gk_done.done(i))
                ins = nc.scalar.activation(ln.enb, ln.X[:, 1, :], ACT.Abs, bias=low_bias[:])
                ins.then_inc(ln.abs_done.sem, 1)
                act.wait_ge(ln.abs_done.sem, ln.abs_done.done(i))
                link(nc.scalar.activation(ln.enb, ln.enb, ACT.Exp, scale=-1.0))
                nc.scalar.activation(ln.enb, ln.enb, ACT.Ln, bias=one[:]).then_inc(ln.zl_done.sem, 1)

            def decays(ln, i):
                act.wait_ge(ln.scan_done.sem, ln.scan_done.done(i))
                nc.scalar.activation(ln.eb, ln.bs, ACT.Exp, scale=1.0 / gate_norm)
                nc.scalar.activation(ln.enb, ln.bs, ACT.Exp, scale=-1.0 / gate_norm)
                nc.scalar.activation(ln.g, ln.g, ACT.Exp, scale=1.0 / gate_norm).then_inc(ln.exps_done.sem, 1)

            def values_gates(ln, i, t):
                act.wait_ge(ln.vg_done.sem, ln.vg_done.after(i, t + 1))
                nc.scalar.activation(ln.v[:, t, :], ln.X[:, t % 2, 0:vals], ACT.Copy)
                nc.scalar.activation(ln.gs[:, t, :], ln.X[:, t % 2, vals:2 * vals], ACT.Silu).then_inc(ln.vg_used.sem, 1)

            def copy_keys(ln, i):
                act.wait_ge(ln.kd_done.sem, ln.kd_done.done(i))
                nc.scalar.activation(ln.kd_tok, ln.X[:, 0, :].rearrange("p (t n) -> p t n", t=TILES), ACT.Copy).then_inc(ln.kd_copied.sem, 1)

            def head_squares(ln, i):
                act.wait_ge(ln.o_done.sem, ln.o_done.done(i))
                nc.scalar.activation(ln.t2[:].rearrange("p (w n) -> p w n", w=2), ln.Y[:], ACT.Square).then_inc(ln.sq2.sem, 1)

            def out_high(ln, i):
                act.wait_ge(ln.in_psum.sem, ln.in_psum.after(i, 2))
                nc.scalar.activation(ln.hT[0][:], ln.X[:], ACT.Copy).then_inc(ln.ot_high.sem, 1)

            def activate(ln, i, c):
                act.wait_ge(ln.gu_done.sem, ln.gu_done.after(i, c + 1))
                at = slice((c % 2) * 512, (c % 2 + 1) * 512)
                nc.scalar.activation(ln.t2[:, at], ln.X[:, 0, :], ACT.Silu).then_inc(ln.sg_done.sem, 1)

            def act_high(ln, i, c):
                act.wait_ge(ln.f_done.sem, ln.f_done.after(i, c + 1))
                if c >= 2:
                    act.wait_ge(ln.down_done.sem, ln.down_done.after(i, c - 1))
                src = ln.t1[:].rearrange("p t d -> p (t d)")[:, (c % 2) * 512:(c % 2 + 1) * 512]
                nc.scalar.activation(ln.act[0][:, c % 2, :], src, ACT.Copy).then_inc(ln.fh_done.sem, 1)

            act.wait_ge(small_loaded, 80)
            act.wait_ge(masks_made, 7)
            with rounds(act) as i:
                for ln in lanes:
                    ln.ln.guess(act, i)
                for ln in lanes:
                    squares(ln, i, ln.h0_done, ln.sq1)
                for ln in lanes:
                    ln.rms1.guess(act, i)
                for ln in lanes:
                    whole(ln, i, 1)
                for ln in lanes:
                    copy_low(ln, i)
                for ln in lanes:
                    decay_logs(ln, i)
                for ln in lanes:
                    decays(ln, i)
                for t in range(TILES):
                    for ln in lanes:
                        values_gates(ln, i, t)
                for ln in lanes:
                    copy_keys(ln, i)
                for ln in lanes:
                    head_squares(ln, i)
                for ln in lanes:
                    ln.rmsh.guess(act, i)
                for ln in lanes:
                    out_high(ln, i)
                for ln in lanes:
                    squares(ln, i, ln.x1_done, ln.sq3)
                for ln in lanes:
                    ln.rms2.guess(act, i)
                for ln in lanes:
                    whole(ln, i, 3)
                for c in range(ki):
                    for ln in lanes:
                        activate(ln, i, c)
                    for ln in lanes:
                        act_high(ln, i, c)

        @block.vector
        def _(dve):
            links = {}

            def root_of_rows(ln, i, root, ready):
                dve.wait_ge(ready.sem, ready.done(i))
                ins = nc.vector.tensor_scalar(root.v[:], ln.sq[:], 1.0 / D, rms_eps, ALU.mult, ALU.add)
                ins.then_inc(root.asked.sem, 1)

            def norm(ln, i, link):
                dve.wait_ge(ln.loaded.sem, ln.loaded.done(i))
                y = ln.y_stored
                dve.wait_ge(y.sem, y.before(i, 16))
                moments_of_rows(nc, link, ln.x, ln.stats, ln.mv, ln.ln.v).then_inc(ln.ln.asked.sem, 1)

            def modulate(ln, i, link):
                ln.ln.refine(dve, i, link)
                link(norm_rows(nc, ln.x, ln.t1, ln.mv, ln.ln.root))
                link(nc.vector.tensor_tensor(ln.t1[:], ln.t1[:], ln.rows[:, 1:2, :].to_broadcast([P, TILES, D]), ALU.mult))
                nc.vector.tensor_tensor(ln.h0[:], ln.t1[:], ln.rows[:, 0:1, :].to_broadcast([P, TILES, D]), ALU.add).then_inc(ln.h0_done.sem, 1)

            def root_norm(ln, i, link, root, done):
                root.refine(dve, i, link)
                for t in range(TILES):
                    ins = nc.vector.tensor_scalar(ln.t1[:, t, :], ln.h0[:, t, :], root.root[:, t:t + 1], None, ALU.mult)
                ins.then_inc(done.sem, 1)

            def halve(ln, i, n):
                dve.wait_ge(ln.whole_done.sem, ln.whole_done.after(i, n))
                nc.vector.tensor_copy(ln.hT[0][:], ln.whole).then_inc(ln.ht_link.sem, 1)
                dve.wait_ge(ln.ht_link.sem, ln.ht_link.after(i, n))
                low(nc, ln.hT[1][:], ln.whole, ln.hT[0][:]).then_inc(ln.ht_ready.sem, 1)

            def decay_sums(ln, i, link):
                dve.wait_ge(ln.abs_done.sem, ln.abs_done.done(i))
                nc.vector.tensor_scalar(ln.g, ln.X[:, 1, :], low_bias[:, 0:1], 0.0, ALU.add, ALU.min).then_inc(ln.min_done.sem, 1)
                dve.wait_ge(ln.min_done.sem, ln.min_done.done(i))
                dve.wait_ge(ln.zl_done.sem, ln.zl_done.done(i))
                link(nc.vector.tensor_tensor(ln.g, ln.g, ln.enb, ALU.subtract))
                link(nc.vector.tensor_tensor_scan(ln.bs, carry[:], ln.g, 0.0, ALU.mult, ALU.add))
                b3 = ln.bs.rearrange("p (c n) -> p c n", c=chunks)
                ends = b3[:, :, chunk - 1:chunk].to_broadcast([P, chunks, chunk])
                nc.vector.tensor_tensor(ln.g.rearrange("p (c n) -> p c n", c=chunks), ends, b3, ALU.subtract).then_inc(ln.scan_done.sem, 1)

            def decay_queries_keys(ln, i):
                dve.wait_ge(ln.exps_done.sem, ln.exps_done.done(i))
                dve.wait_ge(ln.qk_done.sem, ln.qk_done.done(i))
                nc.vector.scalar_tensor_tensor(ln.qe, ln.Y[:, 0, :], hk ** -0.5, ln.eb, ALU.mult, ALU.mult)
                nc.vector.tensor_tensor(ln.ke, ln.Y[:, 1, :], ln.enb, ALU.mult)
                nc.vector.tensor_tensor(ln.kd, ln.Y[:, 1, :], ln.g, ALU.mult)
                nc.vector.tensor_copy(ln.ebl[:], ln.eb.rearrange("p (c n) -> p c n", c=chunks)[:, :, chunk - 1]).then_inc(ln.qk_used.sem, 1)

            def masked(ln, i, t):
                if t == 0:
                    dve.wait_ge(ln.qk_used.sem, ln.qk_used.done(i))
                dve.wait_ge(ln.a_done.sem, ln.a_done.after(i, t + 1))
                src = ln.X[:, 1 - t % 2, :].rearrange("p (h n) -> p h n", h=heads)
                by = tri[:].rearrange("p (o n) -> p o n", o=1).to_broadcast([P, heads, chunk])
                nc.vector.tensor_tensor(ln.a[:, t, :].rearrange("p (h n) -> p h n", h=heads), src, by, ALU.mult).then_inc(ln.a_used.sem, 1)

            def own_blocks(ln, i, n):
                dve.wait_ge(ln.u_done.sem, ln.u_done.after(i, n + 1))
                for a in range(2):
                    lo = 4 * n + 2 * a
                    hi = min(lo + 2, chunks - 1)
                    by = state_mask[:].rearrange("p (o n) -> p o n", o=1).to_broadcast([P, hi - lo, vals])
                    src = ln.Y[:, 0:hi - lo, a * vals:(a + 1) * vals]
                    ins = nc.vector.tensor_tensor(ln.state[:, lo + 1:hi + 1, :], src, by, ALU.mult)
                ins.then_inc(ln.u_used.sem, 1)

            def states(ln, i, link, c):
                if c == 1:
                    dve.wait_ge(ln.u_used.sem, ln.u_used.after(i, 2))
                ins = nc.vector.scalar_tensor_tensor(ln.state[:, c + 1, :], ln.state[:, c, :], ln.ebl[:, c:c + 1],
                                                     ln.state[:, c + 1, :], ALU.mult, ALU.add)
                if c < chunks - 2:
                    link(ins)
                else:
                    ins.then_inc(ln.state_done.sem, 1)

            def head_sums(ln, i, link):
                dve.wait_ge(ln.sq2.sem, ln.sq2.done(i))
                link(nc.vector.tensor_reduce(ln.rmsh.log[:], ln.t2[:].rearrange("p (a v) -> p a v", v=hv), AX.X, ALU.add))
                nc.vector.tensor_scalar(ln.rmsh.v[:], ln.rmsh.log[:], 1.0 / hv, rms_eps, ALU.mult, ALU.add).then_inc(ln.rmsh.asked.sem, 1)

            def gated(ln, i, link):
                ln.rmsh.refine(dve, i, link)
                t1 = ln.t1[:].rearrange("p t d -> p (t d)").rearrange("p (a v) -> p a v", v=hv)
                y = ln.Y[:].rearrange("p w n -> p (w n)").rearrange("p (a v) -> p a v", v=hv)
                by = ln.rmsh.root[:].rearrange("p (a o) -> p a o", o=1).to_broadcast([P, TILES * heads, hv])
                nc.vector.tensor_tensor(t1, y, by, ALU.mult).then_inc(ln.o_used.sem, 1)
                dve.wait_ge(ln.o_used.sem, ln.o_used.done(i))
                dve.wait_ge(ln.gs_done.sem, ln.gs_done.done(i))
                nc.vector.tensor_tensor(ln.t1[:], ln.t1[:], ln.gs, ALU.mult).then_inc(ln.on_done.sem, 1)

            def out_low(ln, i):
                dve.wait_ge(ln.ot_high.sem, ln.ot_high.done(i))
                low(nc, ln.hT[1][:], ln.X[:], ln.hT[0][:]).then_inc(ln.ot_ready.sem, 1)

            def add_out(ln, i):
                dve.wait_ge(ln.wo_done.sem, ln.wo_done.done(i))
                nc.vector.tensor_tensor(ln.h0[:], ln.Yt, ln.h0[:], ALU.add).then_inc(ln.x1_done.sem, 1)

            def hidden(ln, i, c):
                dve.wait_ge(ln.sg_done.sem, ln.sg_done.after(i, c + 1))
                if c >= 2:
                    dve.wait_ge(ln.fl_done.sem, ln.fl_done.after(i, c - 1))
                elif c == 0:
                    dve.wait_ge(ln.ht_ready.sem, ln.ht_ready.after(i, 2))
                at = slice((c % 2) * 512, (c % 2 + 1) * 512)
                nc.vector.tensor_tensor(ln.t1[:].rearrange("p t d -> p (t d)")[:, at], ln.t2[:, at], ln.X[:, 1, :], ALU.mult).then_inc(ln.f_done.sem, 1)

            def sum_up(ln, i):
                dve.wait_ge(ln.down_done.sem, ln.down_done.done(i))
                dve.wait_ge(ln.fl_done.sem, ln.fl_done.done(i))
                nc.vector.tensor_tensor(ln.t1[:], ln.Yt, ln.h0[:], ALU.add).then_inc(ln.sum_done.sem, 1)

            w.split(dve)
            dve.wait_ge(w.ready, w.count("g_down"))
            dve.wait_ge(small_loaded, 80)
            dve.wait_ge(masks_made, 7)
            for ln in lanes:
                nc.vector.memset(ln.state[:, 0, :], 0.0)
            with rounds(dve) as i:
                made = [ln.linker(dve, ln.link, i) for ln in lanes]
                both = [(ln, made[ln.q][0]) for ln in lanes]
                for ln, link in both:
                    norm(ln, i, link)
                for ln, link in both:
                    modulate(ln, i, link)
                for ln, link in both:
                    root_of_rows(ln, i, ln.rms1, ln.sq1)
                for ln, link in both:
                    root_norm(ln, i, link, ln.rms1, ln.hn_done)
                for ln in lanes:
                    halve(ln, i, 1)
                for ln, link in both:
                    decay_sums(ln, i, link)
                for ln in lanes:
                    decay_queries_keys(ln, i)
                for ln in lanes:
                    masked(ln, i, 0)
                for ln in lanes:
                    own_blocks(ln, i, 0)
                for ln in lanes:
                    masked(ln, i, 1)
                for ln in lanes:
                    own_blocks(ln, i, 1)
                for c in range(1, chunks - 1):
                    for ln, link in both:
                        states(ln, i, link, c)
                for t in range(2, TILES):
                    for ln in lanes:
                        masked(ln, i, t)
                for ln, link in both:
                    head_sums(ln, i, link)
                for ln, link in both:
                    gated(ln, i, link)
                for ln in lanes:
                    out_low(ln, i)
                for ln in lanes:
                    add_out(ln, i)
                for ln, link in both:
                    root_of_rows(ln, i, ln.rms2, ln.sq3)
                for ln, link in both:
                    root_norm(ln, i, link, ln.rms2, ln.h2_done)
                for ln in lanes:
                    halve(ln, i, 2)
                for c in range(ki):
                    for ln in lanes:
                        hidden(ln, i, c)
                for ln in lanes:
                    sum_up(ln, i)
                for ln in lanes:
                    assert made[ln.q][1][0] == ln.link.per, made[ln.q][1][0]
        m.end()


def sparse_ffn_stage(nc, io, keep):
    inner = 1024
    halves = inner // 512
    groups = inner // 4
    ki = inner // P
    with ExitStack() as ctx:
        m = Alloc(nc, ctx, "spf")
        entries = [("sp_gate", KD * inner), ("sp_up", KD * inner), ("sp_down", ki * D)]
        raw = m.sb("raw", [P, sum(n for _, n in entries)])
        w = SplitWeights(nc, m, io, entries, raw)
        gate_row = m.sb("gate_row", [P, 2, D])
        silu = m.sb("silu", [P, 2, inner])
        hid = m.sb("hid", [P, 2, inner])
        mag = m.sb("mag", [P, inner])
        lead = m.sb("lead", [P, 3, 2, groups])
        wins = m.sb("wins", [P, 3, 2, groups], BF16)
        sums = m.sb("sums", [P, 4, groups], BF16)
        margin = m.sb("margin", [P, 4, groups], BF16)
        kept = m.sb("kept", [P, inner])
        keptT = [m.sb(f"keptT{i}", [P, ki, P], F32R) for i in "hl"]
        y = m.sb("y", [P, TILES, D])
        gu = m.ps("gu", [P, 2, 2, 512])
        tp = m.ps("tp", [P, 2, 512])
        o_ps = m.ps("o_ps", [P, TILES, D])
        link_t = m.counted("link_t", 2)
        gu_done = m.counted("gu_done", 2)
        silu_done = m.counted("silu_done", 2)
        hid_done = m.counted("hid_done", 2, credit=2)
        mag_done = m.counted("mag_done", 1)
        looked = m.counted("looked", 1, credit=1)
        compared = m.counted("compared", 1, credit=1)
        kept_done = m.counted("kept_done", 1)
        kt_done = m.counted("kt_done", 2)
        kt_high = m.counted("kt_high", 2)
        kt_low = m.counted("kt_low", 2, credit=2)
        o_done = m.counted("o_done", 1)
        link_y = m.counted("link_y", 1)
        y_done = m.counted("y_done", 1, credit=1)
        y_stored = m.counted("y_stored", 16, credit=16)
        row_loaded = [m.counted(f"row_loaded{q}", 16) for q in range(2)]

        xin = NormedInput(nc, m, io, keep, "x3", 1, CB, SB, tp, lambda pe, b: None)
        block = m.begin()

        def load_batch(sp, b, q):
            xin.load(sp, b, q)
            sp.dma_start(gate_row[:, q], io["mod_rows"][1, bass.ds(b, 1), GB * D:(GB + 1) * D].to_broadcast([P, D])).then_inc(row_loaded[q].sem, 16)

        @block.sync
        def _(sp):
            sp.sem_inc(hid_done.sem, hid_done.credit)
            sp.sem_inc(compared.sem, compared.credit)
            sp.sem_inc(looked.sem, looked.credit)
            sp.sem_inc(kt_low.sem, kt_low.credit)
            sp.sem_inc(y_done.sem, y_done.credit)
            sp.sem_inc(y_stored.sem, y_stored.credit)
            load_batch(sp, 0, 0)
            w.load(sp)

            def body(b, q, first, last):
                if not last:
                    wait_apart(sp, y_done.sem, y_done.before(b, 1))
                    load_batch(sp, b + 1, 1 - q)
                if not first:
                    store(b - 1)

            def store(b):
                wait_apart(sp, y_done.sem, y_done.after(b, 1))
                sp.dma_start(io["out_rows"][bass.ds(b * S, S), :].rearrange("(t p) d -> p t d", p=P), y[:]).then_inc(y_stored.sem, 16)

            in_batches(sp, body)
            store(B - 1)
            sp.wait_ge(y_stored.sem, y_stored.after(B - 1, 16))

        @block.gpsimd
        def _(pool):
            def body(b, q, first, last):
                for t in range(TILES):
                    n = b * TILES + t
                    pool.wait_ge(mag_done.sem, mag_done.after(n, 1))
                    pool.wait_ge(looked.sem, looked.before(n, 1))
                    a = mag[:].rearrange("p (g e) -> p e g", e=4)
                    nc.gpsimd.tensor_tensor(lead[:, 0], a[:, 0:4:2, :], a[:, 1:4:2, :], ALU.subtract)
                    nc.gpsimd.tensor_tensor(lead[:, 1], a[:, 0:2, :], a[:, 2:4, :], ALU.subtract)
                    nc.gpsimd.tensor_tensor(lead[:, 2, 0, :], a[:, 0, :], a[:, 3, :], ALU.subtract)
                    ins = nc.gpsimd.tensor_tensor(lead[:, 2, 1, :], a[:, 1, :], a[:, 2, :], ALU.subtract)
                    ins.then_inc(compared.sem, 1)

            in_batches(pool, body)

        @block.tensor
        def _(pe):
            def gate_up(n, t, q):
                for c in range(halves):
                    pe.wait_ge(hid_done.sem, hid_done.before(n, c + 1))
                    for g, name in enumerate(("sp_gate", "sp_up")):
                        for k in range(KD):
                            at = slice(t * P, (t + 1) * P)
                            col = k * inner + c * 512
                            mm = products(nc, gu[:, c, g, :], (xin.hT[q][0][:, k, at], xin.hT[q][1][:, k, at]),
                                          w.part(name, col, col + 512), k == 0, k == KD - 1)
                    mm.then_inc(gu_done.sem, 1)

            def down(n, t):
                pe.wait_ge(kept_done.sem, kept_done.after(n, 1))
                for c in range(2):
                    for j in range(4):
                        at = (c * 4 + j) * P
                        mm = nc.tensor.transpose(tp[:, c, j * P:(j + 1) * P], kept[:, at:at + P], keep["ident"][:])
                    mm.then_inc(kt_done.sem, 1)
                for k in range(ki):
                    if k % 4 == 0:
                        pe.wait_ge(kt_low.sem, kt_low.after(n, k // 4 + 1))
                    mm = products(nc, o_ps[:, t, :], (keptT[0][:, k, :], keptT[1][:, k, :]),
                                  w.part("sp_down", k * D, (k + 1) * D), k == 0, k == ki - 1)
                return mm

            def body(b, q, first, last):
                for t in range(TILES):
                    n = b * TILES + t
                    if t == 0:
                        pe.wait_ge(xin.ready.sem, xin.ready.after(b, 1))
                    gate_up(n, t, q)
                    if t == 0 and not first:
                        down(n - 1, TILES - 1).then_inc(o_done.sem, 1)
                    if t:
                        if t == 1:
                            pe.wait_ge(y_done.sem, y_done.before(b, 1))
                        down(n - 1, t - 1)
                    if t == 2 and not last:
                        xin.transpose(pe, b + 1)
                        pe.wait_ge(xin.whole.sem, xin.whole.after(b + 1, 1))

            xin.transpose(pe, 0)
            pe.wait_ge(w.ready, w.count("sp_down"))
            in_batches(pe, body)
            down(B * TILES - 1, TILES - 1).then_inc(o_done.sem, 1)

        @block.scalar
        def _(act):
            def activate(n, c, s):
                act.wait_ge(gu_done.sem, gu_done.after(n, c + 1))
                nc.scalar.activation(silu[:, s, c * 512:(c + 1) * 512], gu[:, c, 0, :], ACT.Silu).then_inc(silu_done.sem, 1)

            def magnitudes(n, s):
                act.wait_ge(hid_done.sem, hid_done.after(n, 2))
                act.wait_ge(compared.sem, compared.before(n, 1))
                nc.scalar.activation(mag[:], hid[:, s, :], ACT.Abs).then_inc(mag_done.sem, 1)

            def kept_high(n):
                for c in range(2):
                    act.wait_ge(kt_done.sem, kt_done.after(n, c + 1))
                    nc.scalar.activation(keptT[0][:, c * 4:(c + 1) * 4, :], tp[:, c, :].rearrange("p (j n) -> p j n", j=4),
                                         ACT.Copy).then_inc(kt_high.sem, 1)

            def body(b, q, first, last):
                for t in range(TILES):
                    n = b * TILES + t
                    for c in range(halves):
                        activate(n, c, t % 2)
                    magnitudes(n, t % 2)
                    if t or not first:
                        kept_high(n - 1)
                    if t == 1 and not last:
                        xin.guess(act, b + 1)
                    if t == 2 and not last:
                        xin.modulate(act, b + 1)

            xin.guess(act, 0)
            xin.modulate(act, 0)
            in_batches(act, body)
            kept_high(B * TILES - 1)

        @block.vector
        def _(dve):
            def hidden(n, c, s):
                dve.wait_ge(silu_done.sem, silu_done.after(n, c + 1))
                at = slice(c * 512, (c + 1) * 512)
                nc.vector.tensor_tensor(hid[:, s, at], silu[:, s, at], gu[:, c, 1, :], ALU.mult).then_inc(hid_done.sem, 1)

            def kept_low(n):
                for c in range(2):
                    dve.wait_ge(kt_high.sem, kt_high.after(n, c + 1))
                    at = slice(c * 4, (c + 1) * 4)
                    low(nc, keptT[1][:, at, :], tp[:, c, :].rearrange("p (j n) -> p j n", j=4), keptT[0][:, at, :]).then_inc(kt_low.sem, 1)

            def choose(n, s):
                dve.wait_ge(compared.sem, compared.after(n, 1))
                nc.vector.tensor_scalar(wins[:], lead[:], 0.0, None, ALU.is_ge).then_inc(looked.sem, 1)
                dve.wait_ge(looked.sem, looked.after(n, 1))
                x, y_, z = (wins[:, i] for i in range(3))
                nc.vector.tensor_tensor(sums[:, 0:2, :], y_, z, ALU.add)
                nc.vector.tensor_tensor(sums[:, 2, :], y_[:, 0, :], z[:, 1, :], ALU.add)
                nc.vector.scalar_tensor_tensor(sums[:, 3, :], y_[:, 1, :], -1.0, z[:, 0, :], ALU.mult, ALU.subtract).then_inc(link_t.sem, 1)
                dve.wait_ge(link_t.sem, link_t.after(n, 1))
                nc.vector.scalar_tensor_tensor(margin[:, 0, :], sums[:, 0, :], -2.0, x[:, 0, :], ALU.add, ALU.add)
                nc.vector.scalar_tensor_tensor(margin[:, 1, :], sums[:, 1, :], -1.0, x[:, 0, :], ALU.add, ALU.subtract)
                nc.vector.tensor_tensor(margin[:, 2, :], x[:, 1, :], sums[:, 2, :], ALU.subtract)
                nc.vector.scalar_tensor_tensor(margin[:, 3, :], sums[:, 3, :], 1.0, x[:, 1, :], ALU.add, ALU.subtract).then_inc(link_t.sem, 1)
                dve.wait_ge(link_t.sem, link_t.after(n, 2))
                nc.vector.scalar_tensor_tensor(kept[:].rearrange("p (g e) -> p e g", e=4), margin[:], 0.0,
                                               hid[:, s, :].rearrange("p (g e) -> p e g", e=4), ALU.is_ge, ALU.mult).then_inc(kept_done.sem, 1)

            def residual(b, q):
                dve.wait_ge(o_done.sem, o_done.after(b, 1))
                dve.wait_ge(row_loaded[q].sem, row_loaded[q].after((b - q) // 2, 16))
                dve.wait_ge(y_stored.sem, y_stored.before(b, 16))
                rows = gate_row[:, q:q + 1, :].to_broadcast([P, TILES, D])
                nc.vector.tensor_tensor(y[:], o_ps[:], rows, ALU.mult).then_inc(link_y.sem, 1)
                dve.wait_ge(link_y.sem, link_y.after(b, 1))
                nc.vector.tensor_tensor(y[:], y[:], xin.x[:, q], ALU.add).then_inc(y_done.sem, 1)

            def body(b, q, first, last):
                for t in range(TILES):
                    n = b * TILES + t
                    for c in range(halves):
                        hidden(n, c, t % 2)
                    if t or not first:
                        kept_low(n - 1)
                    if t == 1 and not last:
                        xin.norm(dve, b + 1, 1 - q)
                    choose(n, t % 2)
                    if t == 0 and not first:
                        residual(b - 1, 1 - q)
                    if t == 2 and not last:
                        xin.halve(dve, b + 1, 1 - q)

            xin.norm(dve, 0, 0)
            xin.halve(dve, 0, 0)
            w.split(dve)
            in_batches(dve, body)
            kept_low(B * TILES - 1)
            residual(B - 1, 1)
        m.end()


def build(nc, io, stages="full"):
    with ExitStack() as ctx:
        k = Alloc(nc, ctx, "keep")
        keep = {"ident": k.sb("ident", [P, P]), "causal": k.sb("causal", [P, S]),
                "mod": k.sb("mod", [P, 2, MODS * KD, B])}
        Apart.passed = k.sem("passed")
        keep["raw_loaded"] = [k.counted(f"raw_loaded{n}", 16) for n in range(4)]
        modulation_stage(nc, io, keep)
        if stages in ("full", "a"):
            attention_stage(nc, io, keep)
        if stages in ("full", "b"):
            moe_stage(nc, io, keep)
        if stages in ("full", "c"):
            gla_stage(nc, io, keep)
        if stages in ("full", "d"):
            sparse_ffn_stage(nc, io, keep)


def layout(i):
    import numpy as np
    f = {}
    f["x"] = i["L0_attn_x"].reshape(B * S, D)

    def feature_major(w):
        return w.reshape(NH, DH, KD, P).transpose(3, 0, 2, 1).reshape(P, NH, KD * DH)

    f["wqk"] = np.stack([feature_major(i["L0_attn_W_Q"]), feature_major(i["L0_attn_W_K"])], axis=2)
    f["wv"] = i["L0_attn_W_V"].reshape(PAIRS, 2, DH, KD, P).transpose(4, 0, 3, 1, 2).reshape(P, PAIRS, KD * 2 * DH)
    f["wo"] = i["L0_attn_W_O"].transpose(2, 0, 1).reshape(P, PAIRS, 2 * D)
    for l in range(2):
        f[f"c{l}"] = i[f"L{l}_c"].T.reshape(KD, P, B).transpose(1, 0, 2).reshape(P, KD * B)
        f[f"wmod{l}"] = i[f"L{l}_wmod"]

    def rows(w):
        return w.reshape(-1, P, w.shape[1]).transpose(1, 0, 2).reshape(P, -1)

    for n in ("gate", "up", "down"):
        f[f"sp_{n}"] = rows(i[f"L1_ffn_w_{n}"])
        f[f"ex_{n}"] = rows(i[f"L0_ffn_w_{n}"])
        f[f"sh_{n}"] = rows(i[f"L0_ffn_shared_w_{n}"])
    f["g_q"], f["g_k"], f["g_o"] = (rows(i[f"L1_attn_w{n}"]) for n in "qko")
    f["g_vg"] = rows(np.concatenate([i["L1_attn_wv"], i["L1_attn_wg"]], axis=1))
    wide = 768
    for n in ("gate", "up"):
        f[f"g_{n}"] = rows(np.pad(i[f"L1_attn_w_{n}"], ((0, 0), (0, wide - 704))))
    f["g_down"] = rows(np.pad(i["L1_attn_w_down"], ((0, wide - 704), (0, 0))))
    f["gk_w1"] = rows(i["L1_attn_gk_w1"]).reshape(P, KD, 16)
    f["gk_w2"] = i["L1_attn_gk_w2"]
    f["gk_b"] = i["L1_attn_gk_b"].reshape(P, 1)
    f["norm_cols"] = np.stack([i["L1_attn_norm1_w"].reshape(KD, P).T, i["L1_attn_ffn_norm_w"].reshape(KD, P).T], axis=1)
    f["gnorm"] = i["L1_attn_gnorm_w"].reshape(1, 32)
    f["router"] = rows(i["L0_ffn_w_router"])
    f["amplitudes"] = i["L0_ffn_amplitudes"]
    f["expert_scale"] = i["L0_ffn_expert_scale"].reshape(P, 1)
    return {n: np.ascontiguousarray(a) for n, a in f.items()}


def declare(nc, arrays):
    io = {n: nc.dram_tensor(f"in_{n}_dram", a.shape, F32, kind="ExternalInput").ap() for n, a in arrays.items()}
    for n in ("x1", "x2", "x3"):
        io[n] = nc.dram_tensor(n, (B * S, D), F32, kind="Internal").ap()
    io["mod_rows"] = nc.dram_tensor("scratch_mod_rows", (2, B, MODS * D), F32, kind="Internal").ap()
    io["out"] = nc.dram_tensor("out_0_dram", (B, S, D), F32, kind="ExternalOutput").ap()
    io["out_rows"] = io["out"].rearrange("b s d -> (b s) d")
    return io, ["out_0_dram"]


def kernel(**inputs):
    import numpy as np
    import concourse.bacc as bacc
    from concourse.bass_utils import run_bass_kernel_spmd

    nc = bacc.Bacc("TRN2", target_bir_lowering=False, num_devices=1)
    arrays = layout({n: np.asarray(a) for n, a in inputs.items()})
    io, outs = declare(nc, arrays)
    build(nc, io)
    r = run_bass_kernel_spmd(nc, [{f"in_{n}_dram": a for n, a in arrays.items()}], core_ids=[0])
    return r.results[0][outs[0]]
```

```python
from contextlib import ExitStack

import concourse.bass as bass
from concourse import mybir

ALU = mybir.AluOpType
ACT = mybir.ActivationFunctionType
AX = mybir.AxisListType
F32 = mybir.dt.float32
F32R = mybir.dt.float32r
BF16 = mybir.dt.bfloat16
I32 = mybir.dt.int32

P = 128
B, S, D = 8, 512, 256
TILES = S // P
KD = D // P
NH, DH = 16, 128
PAIRS = NH // 2
LN_EPS = 1e-5
MODS = 6
SA, CA, GA, SB, CB, GB = range(MODS)
MASKED = -1.0e30
ROOT_MAGIC = 1597463007.0


class Signal:

    def __init__(self, sem, per, credit=0):
        self.sem, self.per, self.credit = sem, per, credit

    def done(self, r):
        return self.after(r, self.per)

    def after(self, r, k):
        return r * self.per + (self.credit + k)

    def before(self, r, k, back=1):
        return r * self.per + (self.credit + k - back * self.per)


def wait_on(eng, sem, value):
    eng.wait_ge(sem, value)


class Apart:
    passed = None


def wait_apart(eng, sem, value):
    eng.wait_ge(sem, value)
    eng.sem_inc(Apart.passed, 1)


def products(nc, out, still, moving, start, stop, **kw):
    nc.tensor.matmul(out, still[0], moving[0], start=start, stop=False, **kw)
    nc.tensor.matmul(out, still[0], moving[1], start=False, stop=False, **kw)
    return nc.tensor.matmul(out, still[1], moving[0], start=False, stop=stop, **kw)


def low(nc, out, whole, high):
    return nc.vector.tensor_tensor(out, whole, high.bitcast(F32), ALU.subtract)


class Alloc:
    def __init__(self, nc, ctx, prefix):
        self.nc, self.ctx, self.prefix, self.sems = nc, ctx, prefix, []

    def sb(self, name, shape, dt=F32):
        return self.ctx.enter_context(self.nc.sbuf_tensor(f"{self.prefix}_{name}", shape, dt))

    def ps(self, name, shape, dt=F32):
        return self.ctx.enter_context(self.nc.psum_tensor(f"{self.prefix}_{name}", shape, dt))

    def sem(self, name):
        self.sems.append(self.ctx.enter_context(self.nc.semaphore(f"{self.prefix}_{name}")))
        return self.sems[-1]

    def begin(self):
        self.body = ExitStack()
        return self.body.enter_context(self.nc.Block())

    def end(self):
        self.body.close()
        with self.nc.Block() as block:
            @block.sync
            def _(sp):
                for s in self.sems:
                    sp.sem_clear(s)

    def counted(self, name, per, credit=0):
        return Signal(self.sem(name), per, credit)


def modulation_stage(nc, io, keep):
    with ExitStack() as ctx:
        m = Alloc(nc, ctx, "mod")
        c_in = m.sb("c_in", [P, 2, KD, B])
        c_act = m.sb("c_act", [P, 2, KD, B])
        wmod = m.sb("wmod", [P, 2, KD, MODS * D])
        rows = m.sb("rows", [B, 2, MODS * D])
        gates = m.sb("gates", [B, 2, 2, D])
        signs = m.sb("signs", [B, 2, 2, D])
        col_ps = m.ps("col_ps", [P, 2, MODS * KD, B])
        row_ps = m.ps("row_ps", [B, MODS * D])
        loaded = m.sem("loaded")
        zeroed = m.sem("zeroed")
        consts_made = m.sem("consts_made")
        c_ready = m.sem("c_ready")
        cols_done = m.sem("cols_done")
        rows_done = m.sem("rows_done")
        rows_copied = m.sem("rows_copied")
        chain = m.sem("chain")
        rows_final = m.sem("rows_final")
        stored = m.sem("stored")
        block = m.begin()

        @block.sync
        def _(sp):
            for l in range(2):
                sp.dma_start(c_in[:, l], io[f"c{l}"].rearrange("p (k b) -> p k b", k=KD)).then_inc(loaded, 16)
            for l in range(2):
                sp.dma_start(wmod[:, l], io[f"wmod{l}"].rearrange("(k p) n -> p k n", p=P)).then_inc(loaded, 16)
            sp.wait_ge(rows_final, 1)
            for l in range(2):
                sp.dma_start(io["mod_rows"][l], rows[:, l]).then_inc(stored, 16)
            sp.wait_ge(stored, 32)

        @block.gpsimd
        def _(pool):
            nc.gpsimd.memset(keep["ident"][:], 0.0).then_inc(zeroed, 1)
            nc.gpsimd.memset(keep["causal"][:], 0.0).then_inc(zeroed, 1)
            pool.wait_ge(zeroed, 2)
            nc.gpsimd.affine_select(out=keep["ident"][:], in_=keep["ident"][:], compare_op=ALU.not_equal, fill=1.0,
                                    base=0, pattern=[[-1, P]], channel_multiplier=1).then_inc(consts_made, 1)
            last = keep["causal"][:, S - P:S]
            nc.gpsimd.affine_select(out=last, in_=last, compare_op=ALU.is_ge, fill=MASKED,
                                    base=0, pattern=[[-1, P]], channel_multiplier=1).then_inc(consts_made, 1)

        @block.scalar
        def _(act):
            act.wait_ge(loaded, 64)
            nc.scalar.activation(c_act[:], c_in[:], ACT.Silu).then_inc(c_ready, 1)

        @block.tensor
        def _(pe):
            pe.wait_ge(c_ready, 1)
            for l in range(2):
                for n in range(MODS * KD):
                    for k in range(KD):
                        mm = nc.tensor.matmul(col_ps[:, l, n, :], wmod[:, l, k, n * P:(n + 1) * P], c_act[:, l, k, :],
                                              start=(k == 0), stop=(k == KD - 1))
            mm.then_inc(cols_done, 1)
            for l in range(2):
                if l:
                    pe.wait_ge(rows_copied, l)
                for n in range(0, MODS * D, 512):
                    for k in range(KD):
                        mm = nc.tensor.matmul(row_ps[:, n:n + 512], c_act[:, l, k, :], wmod[:, l, k, n:n + 512],
                                              start=(k == 0), stop=(k == KD - 1))
                mm.then_inc(rows_done, 1)

        @block.vector
        def _(dve):
            dve.wait_ge(cols_done, 1)
            nc.vector.tensor_copy(keep["mod"][:], col_ps[:]).then_inc(chain, 1)
            dve.wait_ge(chain, 1)
            for l in range(2):
                for n in (CA, CB):
                    one_plus = keep["mod"][:, l, n * KD:(n + 1) * KD, :]
                    last = nc.vector.tensor_scalar(one_plus, one_plus, 1.0, None, ALU.add)
            for l in range(2):
                dve.wait_ge(rows_done, l + 1)
                nc.vector.tensor_copy(rows[:, l], row_ps[:]).then_inc(rows_copied, 1)
            dve.wait_ge(rows_copied, 2)
            for l in range(2):
                g = rows[:, l].rearrange("b (h m d) -> b h m d", h=2, m=3)[:, :, 2, :]
                last = nc.vector.tensor_scalar(signs[:, l], g, 0.0, 2.0, ALU.is_ge, ALU.mult)
                for h in range(2):
                    nc.vector.scalar_tensor_tensor(gates[:, l, h], g[:, h], -1.0, g[:, h], ALU.mult, ALU.max)
                one = rows[:, l, CA * D:(CA + 1) * D]
                last = nc.vector.tensor_scalar(one, one, 1.0, None, ALU.add)
            last.then_inc(chain, 1)
            dve.wait_ge(chain, 2)
            nc.vector.tensor_scalar(gates[:], gates[:], 0.25, None, ALU.max).then_inc(chain, 1)
            dve.wait_ge(chain, 3)
            for l in range(2):
                g = rows[:, l].rearrange("b (h m d) -> b h m d", h=2, m=3)[:, :, 2, :]
                for h in range(2):
                    last = nc.vector.scalar_tensor_tensor(g[:, h], signs[:, l, h], -1.0, gates[:, l, h], ALU.add, ALU.mult)
            last.then_inc(rows_final, 1)
        m.end()


def moments_of_rows(nc, link, x, stats, mv, var_eps):
    for t in range(TILES):
        last = nc.vector.bn_stats(stats[:, t, :], x[:, t, :])
    link(last, wait_apart)
    for t in range(TILES):
        last = nc.vector.bn_aggr(mv[:, t, :], stats[:, t, :])
    link(last)
    return nc.vector.tensor_scalar(var_eps[:], mv[:, :, 1], LN_EPS, None, ALU.add)


def refine_root(nc, link, var_eps, tmp, rstd):
    link(nc.vector.tensor_tensor(tmp[:], rstd[:], rstd[:], ALU.mult))
    link(nc.vector.scalar_tensor_tensor(tmp[:], tmp[:], -0.5, var_eps[:], ALU.mult, ALU.mult))
    link(nc.vector.scalar_tensor_tensor(rstd[:], tmp[:], 1.5, rstd[:], ALU.add, ALU.mult))


def root_by_halving(nc, link, var_eps, tmp, rstd):
    link(nc.vector.tensor_scalar(rstd[:].bitcast(I32), var_eps[:].bitcast(I32), -0.5, ROOT_MAGIC, ALU.mult, ALU.add))
    for _ in range(3):
        refine_root(nc, link, var_eps, tmp, rstd)


def norm_rows(nc, x, xn, mv, rstd):
    for t in range(TILES):
        last = nc.vector.tensor_scalar(xn[:, t, :], x[:, t, :], mv[:, t, 0:1], rstd[:, t:t + 1],
                                       ALU.subtract, ALU.mult)
    return last


def transpose_rows(nc, out, xn, ident):
    for k in range(KD):
        for t in range(TILES):
            mm = nc.tensor.transpose(out[:, k, t * P:(t + 1) * P], xn[:, t, k * P:(k + 1) * P], ident[:])
    return mm


def attention_stage(nc, io, keep):
    scale = DH ** -0.5
    off = [P * (i * (i + 1) // 2) for i in range(TILES + 1)]
    pt_off = [0, 512, 896, 1152]
    pt_bank = [(0, 0), (1, 0), (2, 0), (2, 256)]
    pt_groups = [(0, 0, 512), (1, 512, 896), (2, 896, 1280)]
    s_place = [(0, 0), (0, P), (1, 0), (2, 0)]
    ident = keep["ident"]
    with ExitStack() as ctx:
        m = Alloc(nc, ctx, "att")
        w_qk = m.sb("w_qk", [P, NH, 4, KD * P], F32R)
        w_v = [m.sb(f"w_v{i}", [P, PAIRS, KD, 2 * DH], F32R) for i in "hl"]
        w_o = [m.sb(f"w_o{i}", [P, NH, D], F32R) for i in "hl"]
        raw = m.sb("raw", [P, 4, 512])
        staged = m.sb("staged", [P, 2, 4, KD * P], F32R)
        x_in = m.sb("x_in", [P, TILES, D])
        x_res = m.sb("x_res", [P, TILES, D])
        whole_hT = m.sb("whole_hT", [P, KD, S])
        gate = m.sb("gate", [P, D])
        hT = [m.sb(f"hT{i}", [P, KD, S], F32R) for i in "hl"]
        qkT = [m.sb(f"qkT{i}", [P, 2, S], F32R) for i in "hl"]
        v = [m.sb(f"v{i}", [P, TILES, 2 * DH], F32R) for i in "hl"]
        probs = m.sb("probs", [P, off[TILES]])
        probs_t = [m.sb(f"probs_t{i}", [P, off[TILES]], F32R) for i in "hl"]
        zT = [m.sb(f"zT{i}", [P, S], F32R) for i in "hl"]
        stats = m.sb("stats", [P, TILES, 6])
        mv = m.sb("mv", [P, TILES, 2])
        rstd = m.sb("rstd", [P, TILES])
        var_eps = m.sb("var_eps", [P, TILES])
        root_tmp = m.sb("root_tmp", [P, TILES])
        top = m.sb("top", [P, TILES])
        neg_top = m.sb("neg_top", [P, TILES])
        total = m.sb("total", [P, TILES])
        inv_total = m.sb("inv_total", [P, TILES])
        proj = m.ps("proj", [P, 2, 512])
        work = m.ps("work", [P, 3, 512])
        z_ps = m.ps("z_ps", [P, 512])
        o_ps = m.ps("o_ps", [P, TILES, D])

        x_loaded = m.counted("x_loaded", 16)
        res_loaded = m.counted("res_loaded", 32)
        raw_loaded = keep["raw_loaded"]
        w_high = m.counted("w_high", 4)
        w_split = m.counted("w_split", 4)
        stage_loaded = [m.counted(f"stage_loaded{a}", 16) for a in range(2)]
        link_n = m.counted("link_n", 13)
        link_y = m.counted("link_y", 1)
        link_h = m.counted("link_h", 2)
        ln_done = m.counted("ln_done", 1)
        ht_in_psum = m.counted("ht_in_psum", KD)
        ht_whole = m.counted("ht_whole", KD)
        ht_high = m.counted("ht_high", KD)
        ht_ready = m.counted("ht_ready", KD)
        qk_done = m.counted("qk_done", 2, credit=4)
        qk_high = m.counted("qk_high", 2)
        qk_low = m.counted("qk_low", 2)
        v_done = m.counted("v_done", 2)
        v_high = m.counted("v_high", 2)
        v_low = m.counted("v_low", 2)
        s_done = m.counted("s_done", 3)
        top_ready = m.counted("top_ready", 1)
        exp_done = m.counted("exp_done", 1)
        probs_ready = m.counted("probs_ready", 1)
        pt_done = m.counted("pt_done", 3)
        pt_high = m.counted("pt_high", 3)
        pt_low = m.counted("pt_low", 3, credit=3)
        z_done = m.counted("z_done", 1)
        z_high = m.counted("z_high", 1)
        z_low = m.counted("z_low", 1)
        o_done = m.counted("o_done", 1)
        y_done = m.counted("y_done", 1, credit=1)
        y_stored = m.counted("y_stored", 16, credit=16)
        y = raw[:, 0:2, :].rearrange("p w (t d) -> p (w t) d", t=2)
        block = m.begin()

        def batches(eng, batch):
            with eng.Fori(0, B - 1) as b:
                batch(b, True)
            batch(B - 1, False)

        def pairs(eng, pair, b):
            pair(b, 0, True, False)
            with eng.Fori(1, PAIRS - 1) as p:
                pair(b, p, False, False)
            pair(b, PAIRS - 1, False, True)

        @block.sync
        def _(sp):
            for signal in (qk_done, pt_low, y_done, y_stored):
                sp.sem_inc(signal.sem, signal.credit)

            def stage_weights(b, p):
                for a in range(2):
                    g = b * NH + p * 2 + a
                    wait_apart(sp, w_split.sem, w_split.after(p, 4))
                    wait_apart(sp, qk_done.sem, qk_done.before(g, 2, back=2))
                    sp.dma_start(staged[:, a].bitcast(F32), w_qk[:, bass.ds(p * 2 + a, 1)].rearrange("p o m n -> p (o m) n").bitcast(F32)).then_inc(stage_loaded[a].sem, 16)

            def tokens(ap, b):
                return ap[bass.ds(b * S, S), :].rearrange("(t p) d -> p t d", p=P)

            def batch(b, first, last):
                stage_weights(b, 0)
                if not first:
                    wait_apart(sp, y_done.sem, y_done.before(b, 1))
                    sp.dma_start(tokens(io["x1"], b - 1), y).then_inc(y_stored.sem, 16)
                sp.dma_start(x_res[:], tokens(io["x"], b)).then_inc(res_loaded.sem, 16)
                sp.dma_start(gate[:], io["mod_rows"][0, bass.ds(b, 1), GA * D:(GA + 1) * D].to_broadcast([P, D])).then_inc(res_loaded.sem, 16)
                if not last:
                    wait_apart(sp, ht_in_psum.sem, ht_in_psum.done(b))
                    sp.dma_start(x_in[:], tokens(io["x"], b + 1)).then_inc(x_loaded.sem, 16)
                with sp.Fori(1, PAIRS) as p:
                    stage_weights(b, p)

            sp.dma_start(x_in[:], tokens(io["x"], 0)).then_inc(x_loaded.sem, 16)
            batch(0, True, False)
            with sp.Fori(1, B - 1) as b:
                batch(b, False, False)
            batch(B - 1, False, True)
            sp.wait_ge(y_done.sem, y_done.done(B - 1))
            sp.dma_start(tokens(io["x1"], B - 1), y).then_inc(y_stored.sem, 16)
            sp.wait_ge(y_stored.sem, y_stored.done(B - 1))

        @block.gpsimd
        def _(pool):
            def fetch(n, p):
                if n < 2:
                    src = io["wqk"][:, bass.ds(p * 2, 2), n, :]
                    dst = raw[:, n].rearrange("p (h n) -> p h n", h=2)
                elif n == 2:
                    src, dst = io["wv"][:, bass.ds(p, 1), :].rearrange("p o n -> p (o n)"), raw[:, n]
                else:
                    src, dst = io["wo"][:, bass.ds(p, 1), :].rearrange("p o n -> p (o n)"), raw[:, n]
                pool.dma_start(dst, src).then_inc(raw_loaded[n].sem, 16)

            def place(n, p, half):
                if n < 2:
                    return w_qk[:, bass.ds(p * 2, 2), 2 * n + half, :], raw[:, n].rearrange("p (h n) -> p h n", h=2)
                if n == 2:
                    return w_v[half][:, bass.ds(p, 1)].rearrange("p o k n -> p (o k n)"), raw[:, n]
                return w_o[half][:, bass.ds(p * 2, 2)].rearrange("p h n -> p (h n)"), raw[:, n]

            def split(p, more):
                for n in range(4):
                    pool.wait_ge(raw_loaded[n].sem, raw_loaded[n].after(p, 16))
                    dst, src = place(n, p, 0)
                    nc.gpsimd.tensor_copy(dst, src).then_inc(w_high.sem, 1)
                    pool.wait_ge(w_high.sem, w_high.after(p, n + 1))
                    dst, src = place(n, p, 1)
                    nc.gpsimd.tensor_tensor(dst, src, place(n, p, 0)[0].bitcast(F32), ALU.subtract).then_inc(w_split.sem, 1)
                    if more:
                        wait_apart(pool, w_split.sem, w_split.after(p, n + 1))
                        fetch(n, p + 1)

            for n in range(4):
                fetch(n, 0)
            with pool.Fori(0, PAIRS - 1) as p:
                split(p, True)
            split(PAIRS - 1, False)

        @block.tensor
        def _(pe):
            def transpose_x():
                for k in range(KD):
                    for t in range(TILES):
                        mm = nc.tensor.transpose(proj[:, k, t * P:(t + 1) * P], x_in[:, t, k * P:(k + 1) * P], ident[:])
                    mm.then_inc(ht_in_psum.sem, 1)

            def project_qk(r, a, v_before=None):
                pe.wait_ge(stage_loaded[a].sem, stage_loaded[a].after(r, 16))
                for w in range(2):
                    if v_before is not None:
                        pe.wait_ge(v_low.sem, v_low.after(v_before, w + 1))
                    for k in range(KD):
                        at = slice(k * P, (k + 1) * P)
                        mm = products(nc, proj[:, w, :], (staged[:, a, 2 * w, at], staged[:, a, 2 * w + 1, at]),
                                      (hT[0][:, k, :], hT[1][:, k, :]), k == 0, k == KD - 1)
                    mm.then_inc(qk_done.sem, 1)

            def project_v(r, p, first):
                pe.wait_ge(w_split.sem, w_split.after(p, 4))
                for t in range(TILES):
                    if t % 2 == 0 and not first:
                        pe.wait_ge(qk_low.sem, qk_low.after(r * 2 + 1, t // 2 + 1))
                    for k in range(KD):
                        at = slice(t * P, (t + 1) * P)
                        mv_ = tuple(w_v[i][:, bass.ds(p, 1), k, :].rearrange("p o n -> p (o n)") for i in range(2))
                        mm = products(nc, proj[:, t // 2, (t % 2) * D:(t % 2 + 1) * D],
                                      (hT[0][:, k, at], hT[1][:, k, at]), mv_, k == 0, k == KD - 1)
                    if t % 2:
                        mm.then_inc(v_done.sem, 1)

            def scores(g):
                pe.wait_ge(qk_low.sem, qk_low.after(g, 2))
                for i in range(TILES):
                    bank, col = s_place[i]
                    if i != 1:
                        pe.wait_ge(pt_low.sem, pt_low.before(g, bank + 1))
                    at = slice(i * P, (i + 1) * P)
                    keys = slice(0, (i + 1) * P)
                    mm = products(nc, work[:, bank, col:col + (i + 1) * P], (qkT[0][:, 0, at], qkT[1][:, 0, at]),
                                  (qkT[0][:, 1, keys], qkT[1][:, 1, keys]), True, True)
                    if i:
                        mm.then_inc(s_done.sem, 1)

            def transpose_probs(g):
                pe.wait_ge(probs_ready.sem, probs_ready.after(g, 1))
                for j in range(TILES):
                    bank, col = pt_bank[j]
                    for i in range(j, TILES):
                        c = col + (i - j) * P
                        mm = nc.tensor.transpose(work[:, bank, c:c + P], probs[:, off[i] + j * P:off[i] + (j + 1) * P], ident[:])
                    if j != 2:
                        mm.then_inc(pt_done.sem, 1)

            def times_v(g, r, a):
                pe.wait_ge(v_low.sem, v_low.after(r, 2))
                pe.wait_ge(pt_low.sem, pt_low.after(g, 3))
                for j in range(TILES):
                    at = slice(pt_off[j], pt_off[j] + S - j * P)
                    head = slice(a * DH, (a + 1) * DH)
                    mm = products(nc, z_ps[:, j * P:S], (v[0][:, j, head], v[1][:, j, head]),
                                  (probs_t[0][:, at], probs_t[1][:, at]), j == 0, j == TILES - 1, skip_group_check=True)
                mm.then_inc(z_done.sem, 1)

            def project_out(g, h, first):
                pe.wait_ge(z_low.sem, z_low.after(g, 1))
                for t in range(TILES):
                    at = slice(t * P, (t + 1) * P)
                    for c, (i, j) in enumerate(((0, 0), (0, 1), (1, 0))):
                        mm = nc.tensor.matmul(o_ps[:, t, :], zT[i][:, at], w_o[j][:, bass.ds(h, 1), :].rearrange("p o n -> p (o n)"),
                                              start=(first and t % 2 == 0 and c == 0), stop=True, skip_group_check=True)
                return mm

            def pair(b, p, first, last):
                r = b * PAIRS + p
                for a in range(2):
                    g = r * 2 + a
                    scores(g)
                    if a == 0:
                        if first:
                            project_v(r, p, True)
                        project_qk(r, 1, r if first else None)
                    elif not last:
                        project_qk(r + 1, 0, r)
                    if not (first and a == 0):
                        times_v(g - 1, r - 1 + a, 1 - a)
                    transpose_probs(g)
                    if first and a == 1:
                        pe.wait_ge(y_done.sem, y_done.before(b, 1))
                    if not (first and a == 0):
                        project_out(g - 1, p * 2 + a - 1, first)
                    if a == 0 and not first:
                        project_v(r, p, False)

            def batch(b, more):
                pairs(pe, pair, b)
                if more:
                    pe.wait_ge(ln_done.sem, ln_done.after(b + 1, 1))
                    transpose_x()
                times_v(b * NH + NH - 1, b * PAIRS + PAIRS - 1, 1)
                project_out(b * NH + NH - 1, NH - 1, False).then_inc(o_done.sem, 1)
                if more:
                    pe.wait_ge(ht_ready.sem, ht_ready.done(b + 1))
                    project_qk((b + 1) * PAIRS, 0)

            pe.wait_ge(ln_done.sem, ln_done.after(0, 1))
            transpose_x()
            pe.wait_ge(ht_ready.sem, ht_ready.done(0))
            project_qk(0, 0)
            batches(pe, batch)

        @block.scalar
        def _(act):
            def modulate(b):
                for k in range(KD):
                    mod = [keep["mod"][:, 0, n * KD + k, bass.ds(b, 1)] for n in (CA, SA)]
                    act.wait_ge(ht_in_psum.sem, ht_in_psum.after(b, k + 1))
                    nc.scalar.activation(whole_hT[:, k, :], proj[:, k, :], ACT.Identity, bias=mod[1], scale=mod[0]).then_inc(ht_whole.sem, 1)

            def qk_halves(g):
                for w in range(2):
                    act.wait_ge(qk_done.sem, qk_done.after(g, w + 1))
                    nc.scalar.activation(qkT[0][:, w], proj[:, w], ACT.Copy).then_inc(qk_high.sem, 1)

            def v_halves(r):
                for w in range(2):
                    act.wait_ge(v_done.sem, v_done.after(r, w + 1))
                    nc.scalar.activation(v[0][:, 2 * w:2 * w + 2], proj[:, w].rearrange("p (t n) -> p t n", t=2), ACT.Copy).then_inc(v_high.sem, 1)

            def z_halves(g):
                act.wait_ge(z_done.sem, z_done.after(g, 1))
                nc.scalar.activation(zT[0][:], z_ps[:], ACT.Copy).then_inc(z_high.sem, 1)

            def pair(b, p, first, last):
                r = b * PAIRS + p
                for a in range(2):
                    g = r * 2 + a
                    act.wait_ge(top_ready.sem, top_ready.after(g, 1))
                    for i in range(TILES):
                        row = probs[:, off[i]:off[i + 1]]
                        last_exp = nc.scalar.activation(row, row, ACT.Exp, bias=neg_top[:, i:i + 1], scale=scale,
                                                        accum_out=total[:, i:i + 1])
                    last_exp.then_inc(exp_done.sem, 1)
                    if first and a == 0:
                        v_halves(r)
                    if not (last and a == 1):
                        qk_halves(g + 1)
                    if not (first and a == 0):
                        z_halves(g - 1)
                    for n, (bank, lo, hi) in enumerate(pt_groups):
                        act.wait_ge(pt_done.sem, pt_done.after(g, n + 1))
                        nc.scalar.activation(probs_t[0][:, lo:hi], work[:, bank, 0:hi - lo], ACT.Copy).then_inc(pt_high.sem, 1)
                    if a == 0 and not first:
                        v_halves(r)

            def batch(b, more):
                pairs(act, pair, b)
                if more:
                    modulate(b + 1)
                z_halves(b * NH + NH - 1)
                if more:
                    qk_halves((b + 1) * NH)

            modulate(0)
            qk_halves(0)
            batches(act, batch)

        @block.vector
        def _(dve):
            def normalise(b):
                count = [0]

                def link(ins, wait=wait_on):
                    count[0] += 1
                    ins.then_inc(link_n.sem, 1)
                    wait(dve, link_n.sem, link_n.after(b, count[0]))

                dve.wait_ge(x_loaded.sem, x_loaded.after(b, 16))
                link(moments_of_rows(nc, link, x_in, stats, mv, var_eps))
                root_by_halving(nc, link, var_eps, root_tmp, rstd)
                norm_rows(nc, x_in, x_in, mv, rstd).then_inc(ln_done.sem, 1)
                assert count[0] == link_n.per, count[0]

            def ht_halves(b):
                for k in range(KD):
                    dve.wait_ge(ht_whole.sem, ht_whole.after(b, k + 1))
                    nc.vector.tensor_copy(hT[0][:, k], whole_hT[:, k]).then_inc(ht_high.sem, 1)
                    dve.wait_ge(ht_high.sem, ht_high.after(b, k + 1))
                    low(nc, hT[1][:, k], whole_hT[:, k], hT[0][:, k]).then_inc(ht_ready.sem, 1)

            def qk_halves(g):
                for w in range(2):
                    dve.wait_ge(qk_high.sem, qk_high.after(g, w + 1))
                    low(nc, qkT[1][:, w], proj[:, w], qkT[0][:, w]).then_inc(qk_low.sem, 1)

            def v_halves(r):
                for w in range(2):
                    dve.wait_ge(v_high.sem, v_high.after(r, w + 1))
                    low(nc, v[1][:, 2 * w:2 * w + 2], proj[:, w].rearrange("p (t n) -> p t n", t=2), v[0][:, 2 * w:2 * w + 2]).then_inc(v_low.sem, 1)

            def z_halves(g):
                dve.wait_ge(z_high.sem, z_high.after(g, 1))
                low(nc, zT[1][:], z_ps[:], zT[0][:]).then_inc(z_low.sem, 1)

            def pair(b, p, first, last):
                r = b * PAIRS + p
                for a in range(2):
                    g = r * 2 + a
                    for i in range(TILES):
                        bank, col = s_place[i]
                        if i != 1:
                            wait_apart(dve, s_done.sem, s_done.after(g, max(i, 1)))
                        n = (i + 1) * P
                        ins = nc.vector.tensor_tensor_reduce(
                            out=probs[:, off[i]:off[i + 1]], in0=work[:, bank, col:col + n], in1=keep["causal"][:, S - n:S],
                            scale=1.0, scalar=-3.0e38, op0=ALU.add, op1=ALU.max, accum_out=top[:, i:i + 1])
                    ins.then_inc(link_h.sem, 1)
                    dve.wait_ge(link_h.sem, link_h.after(g, 1))
                    nc.vector.tensor_scalar(neg_top[:], top[:], -scale, None, ALU.mult).then_inc(top_ready.sem, 1)
                    dve.wait_ge(exp_done.sem, exp_done.after(g, 1))
                    nc.vector.reciprocal(inv_total[:], total[:]).then_inc(link_h.sem, 1)
                    dve.wait_ge(link_h.sem, link_h.after(g, 2))
                    for i in range(TILES):
                        row = probs[:, off[i]:off[i + 1]]
                        ins = nc.vector.tensor_scalar(row, row, inv_total[:, i:i + 1], None, ALU.mult)
                    ins.then_inc(probs_ready.sem, 1)
                    if first and a == 0:
                        v_halves(r)
                    if not (last and a == 1):
                        qk_halves(g + 1)
                    if not (first and a == 0):
                        z_halves(g - 1)
                    for n, (bank, lo, hi) in enumerate(pt_groups):
                        dve.wait_ge(pt_high.sem, pt_high.after(g, n + 1))
                        low(nc, probs_t[1][:, lo:hi], work[:, bank, 0:hi - lo], probs_t[0][:, lo:hi]).then_inc(pt_low.sem, 1)
                    if a == 0 and not first:
                        v_halves(r)

            def add_residual(b):
                dve.wait_ge(o_done.sem, o_done.after(b, 1))
                dve.wait_ge(res_loaded.sem, res_loaded.after(b, 32))
                dve.wait_ge(w_split.sem, w_split.done(PAIRS - 1))
                dve.wait_ge(y_stored.sem, y_stored.before(b, 16))
                gate_rows = gate[:].rearrange("p (o d) -> p o d", o=1).to_broadcast([P, TILES, D])
                nc.vector.tensor_tensor(y, o_ps[:], gate_rows, ALU.mult).then_inc(link_y.sem, 1)
                dve.wait_ge(link_y.sem, link_y.after(b, 1))
                nc.vector.tensor_tensor(y, y, x_res[:], ALU.add).then_inc(y_done.sem, 1)

            def batch(b, more):
                pair(b, 0, True, False)
                with dve.Fori(1, PAIRS - 1) as p:
                    pair(b, p, False, False)
                if more:
                    normalise(b + 1)
                pair(b, PAIRS - 1, False, True)
                if more:
                    ht_halves(b + 1)
                z_halves(b * NH + NH - 1)
                add_residual(b)
                if more:
                    qk_halves((b + 1) * NH)

            normalise(0)
            ht_halves(0)
            qk_halves(0)
            batches(dve, batch)
        m.end()


class SplitWeights:

    def __init__(self, nc, m, io, entries, raw):
        self.nc, self.io, self.entries, self.raw = nc, io, entries, raw
        self.at = {}
        n = 0
        for name, width in entries:
            self.at[name] = slice(n, n + width)
            n += width
        self.halves = [m.sb(f"weights{i}", [P, n], F32R) for i in "hl"]
        self.loaded = [m.sem(f"{name}_loaded") for name, _ in entries]
        self.high = m.sem("weights_high")
        self.ready = m.sem("weights_ready")

    def load(self, sp):
        for (name, _), sem in zip(self.entries, self.loaded):
            sp.dma_start(self.raw[:, self.at[name]], self.io[name]).then_inc(sem, 16)

    def split(self, dve):
        for n, (name, _) in enumerate(self.entries):
            at = self.at[name]
            dve.wait_ge(self.loaded[n], 16)
            self.nc.vector.tensor_copy(self.halves[0][:, at], self.raw[:, at]).then_inc(self.high, 1)
            dve.wait_ge(self.high, n + 1)
            low(self.nc, self.halves[1][:, at], self.raw[:, at], self.halves[0][:, at]).then_inc(self.ready, 1)

    def count(self, name):
        return [n for n, _ in self.entries].index(name) + 1

    def part(self, name, lo, hi):
        start = self.at[name].start
        return tuple(h[:, start + lo:start + hi] for h in self.halves)


def in_batches(eng, body):
    body(0, 0, True, False)
    with eng.Fori(0, B // 2 - 1) as i:
        body(i * 2 + 1, 1, False, False)
        body(i * 2 + 2, 0, False, False)
    body(B - 1, 1, False, True)


class NormedInput:

    def __init__(self, nc, m, io, keep, source, layer, scale, shift, ps, ps_free):
        self.nc, self.io, self.keep, self.source = nc, io, keep, source
        self.layer, self.scale, self.shift, self.ps, self.ps_free = layer, scale, shift, ps, ps_free
        self.x = m.sb("x", [P, TILES, D])
        self.residual = m.sb("residual", [P, TILES, D])
        self.xn = m.sb("xn", [P, TILES, D])
        self.hT = [[m.sb(f"hT{i}{q}", [P, KD, S], F32R) for i in "hl"] for q in range(2)]
        self.stats = m.sb("stats", [P, TILES, 6])
        self.mv = m.sb("mv", [P, TILES, 2])
        self.rstd, self.var_eps, self.root_tmp = (m.sb(n, [P, TILES]) for n in ("rstd", "var_eps", "root_tmp"))
        self.gate_row = m.sb("gate_row", [P, 1, D])
        self.x_loaded = m.counted("x_loaded", 16)
        self.residual_loaded = m.counted("residual_loaded", 32)
        self.link_n = m.counted("link_n", 14)
        self.normed = m.counted("normed", 1, credit=1)
        self.in_psum = m.counted("in_psum", 1)
        self.whole = m.counted("whole", 1)
        self.ready = m.counted("ready", 1)
        self.whole_hT = self.xn[:].rearrange("p t d -> p (t d)").rearrange("p (k s) -> p k s", k=KD)

    def tokens(self, b):
        return self.io[self.source][bass.ds(b * S, S), :].rearrange("(t p) d -> p t d", p=P)

    def load(self, sp, b):
        wait_apart(sp, self.normed.sem, self.normed.before(b, 1))
        sp.dma_start(self.x[:], self.tokens(b)).then_inc(self.x_loaded.sem, 16)

    def load_residual(self, sp, b, gate):
        sp.dma_start(self.residual[:], self.tokens(b)).then_inc(self.residual_loaded.sem, 16)
        row = self.io["mod_rows"][self.layer, bass.ds(b, 1), gate * D:(gate + 1) * D].to_broadcast([P, D])
        sp.dma_start(self.gate_row[:, 0], row).then_inc(self.residual_loaded.sem, 16)

    def norm(self, dve, b):
        nc, count = self.nc, [0]

        def link(ins, wait=wait_on):
            count[0] += 1
            ins.then_inc(self.link_n.sem, 1)
            wait(dve, self.link_n.sem, self.link_n.after(b, count[0]))

        dve.wait_ge(self.x_loaded.sem, self.x_loaded.after(b, 16))
        link(moments_of_rows(nc, link, self.x, self.stats, self.mv, self.var_eps))
        root_by_halving(nc, link, self.var_eps, self.root_tmp, self.rstd)
        norm_rows(nc, self.x, self.xn, self.mv, self.rstd).then_inc(self.normed.sem, 1)

    def transpose(self, pe, b):
        pe.wait_ge(self.normed.sem, self.normed.after(b, 1))
        self.ps_free(pe, b)
        transpose_rows(self.nc, self.ps, self.xn, self.keep["ident"]).then_inc(self.in_psum.sem, 1)

    def modulate(self, act, b):
        act.wait_ge(self.in_psum.sem, self.in_psum.after(b, 1))
        for k in range(KD):
            mod = [self.keep["mod"][:, self.layer, n * KD + k, bass.ds(b, 1)] for n in (self.scale, self.shift)]
            last = self.nc.scalar.activation(self.whole_hT[:, k, :], self.ps[:, k, :], ACT.Identity, bias=mod[1], scale=mod[0])
        last.then_inc(self.whole.sem, 1)

    def halve(self, dve, b, q):
        dve.wait_ge(self.whole.sem, self.whole.after(b, 1))
        self.nc.vector.tensor_copy(self.hT[q][0][:], self.whole_hT).then_inc(self.link_n.sem, 1)
        dve.wait_ge(self.link_n.sem, self.link_n.done(b))
        low(self.nc, self.hT[q][1][:], self.whole_hT, self.hT[q][0][:]).then_inc(self.ready.sem, 1)


def moe_stage(nc, io, keep):
    experts, basis, inner = 128, 8, 128
    wide = basis * inner
    shared = 2 * inner
    row = experts + 8
    top = 4
    with ExitStack() as ctx:
        m = Alloc(nc, ctx, "moe")
        entries = [("router", KD * experts), ("sh_gate", KD * shared), ("sh_up", KD * shared),
                   ("ex_gate", KD * wide), ("ex_up", KD * wide), ("ex_down", D), ("sh_down", 2 * D)]
        raw = m.sb("raw", [P, sum(n for _, n in entries)])
        w = SplitWeights(nc, m, io, entries, raw)
        amp = m.sb("amp", [P, basis, 2])
        e_scale = m.sb("e_scale", [P, 1])
        mix = m.sb("mix", [P, basis])
        mix_sum = m.sb("mix_sum", [P, 1])
        top_logit = m.sb("top_logit", [P, TILES])
        neg_top = m.sb("neg_top", [P, TILES])
        probs = m.sb("probs", [P, TILES, row])
        rest = m.sb("rest", [P, TILES, row])
        total = m.sb("total", [P, TILES])
        best = m.sb("best", [P, TILES, 8])
        best_sum = m.sb("best_sum", [P, TILES])
        route_t = m.sb("route_t", [P, S])
        coeff = m.sb("coeff", [P, 2, TILES, basis])
        silu = m.sb("silu", [P, 2, wide])
        base = m.sb("base", [P, 2, wide])
        tree = m.sb("tree", [P, wide // 2])
        mixed = m.sb("mixed", [P, 2, inner])
        mixedT = [m.sb(f"mixedT{i}", [P, S], F32R) for i in "hl"]
        sh_silu = m.sb("sh_silu", [P, 2, S])
        sh_hid = m.sb("sh_hid", [P, 2, S])
        sh_hT = [m.sb(f"sh_hT{i}", [P, 2, S], F32R) for i in "hl"]
        y = m.sb("y", [P, TILES, D])
        gu = m.ps("gu", [P, 2, 2, 512])
        route_ps = m.ps("route_ps", [P, 512])
        mixed_ps = m.ps("mixed_ps", [P, 512])
        o_ps = m.ps("o_ps", [P, TILES, D])

        amp_loaded = m.sem("amp_loaded")
        mix_link = m.sem("mix_link")
        mix_ready = m.sem("mix_ready")
        link_r = m.counted("link_r", 9)
        logits_done = m.counted("logits_done", 1)
        neg_ready = m.counted("neg_ready", 1)
        exp_done = m.counted("exp_done", 1)
        routed = m.counted("routed", 1)
        rt_done = m.counted("rt_done", 1)
        rt_copied = m.counted("rt_copied", 1)
        coeff_done = m.counted("coeff_done", 1)
        coeff_ready = m.counted("coeff_ready", 1)
        gu_done = m.counted("gu_done", 2)
        silu_done = m.counted("silu_done", 2)
        base_done = m.counted("base_done", 2, credit=2)
        link_m = m.counted("link_m", 1)
        weighed = m.counted("weighed", 1)
        link_p = m.counted("link_p", 2)
        mixed_done = m.counted("mixed_done", 1, credit=2)
        sh_done = m.counted("sh_done", 2)
        sh_silu_done = m.counted("sh_silu_done", 2)
        sh_hid_done = m.counted("sh_hid_done", 2)
        sh_high = m.counted("sh_high", 1)
        sh_low = m.counted("sh_low", 1)
        mt_done = m.counted("mt_done", 4, credit=2)
        mt_high = m.counted("mt_high", 1)
        mt_low = m.counted("mt_low", 1)
        o_done = m.counted("o_done", 1)
        link_y = m.counted("link_y", 1)
        y_done = m.counted("y_done", 1, credit=1)
        y_stored = m.counted("y_stored", 16, credit=16)
        xin = NormedInput(nc, m, io, keep, "x1", 0, CB, SB, o_ps[:].rearrange("p t d -> p (t d)").rearrange("p (k s) -> p k s", k=KD), lambda pe, b: None)
        block = m.begin()

        @block.sync
        def _(sp):
            for s in (xin.normed, base_done, mixed_done, mt_done, y_done, y_stored):
                sp.sem_inc(s.sem, s.credit)
            xin.load(sp, 0)
            sp.dma_start(amp[:], io["amplitudes"]).then_inc(amp_loaded, 16)
            sp.dma_start(e_scale[:], io["expert_scale"]).then_inc(amp_loaded, 16)
            w.load(sp)

            def store(b):
                wait_apart(sp, y_done.sem, y_done.after(b, 1))
                sp.dma_start(io["x2"][bass.ds(b * S, S), :].rearrange("(t p) d -> p t d", p=P), y[:]).then_inc(y_stored.sem, 16)

            def body(b, q, first, last):
                if not last:
                    xin.load(sp, b + 1)
                if not first:
                    store(b - 1)
                xin.load_residual(sp, b, GB)

            in_batches(sp, body)
            store(B - 1)
            sp.wait_ge(y_stored.sem, y_stored.after(B - 1, 16))

        @block.gpsimd
        def _(pool):
            def body(b, q, first, last):
                for t in range(TILES):
                    n = b * TILES + t
                    pool.wait_ge(mixed_done.sem, mixed_done.before(n, 1))
                    pool.wait_ge(weighed.sem, weighed.after(n, 1))
                    s = t % 2
                    half = wide // 2
                    nc.gpsimd.tensor_tensor(tree[:], base[:, s, 0:half], base[:, s, half:wide], ALU.add).then_inc(link_p.sem, 1)
                    pool.wait_ge(link_p.sem, link_p.after(n, 1))
                    nc.gpsimd.tensor_tensor(tree[:, 0:half // 2], tree[:, 0:half // 2], tree[:, half // 2:half], ALU.add).then_inc(link_p.sem, 1)
                    pool.wait_ge(link_p.sem, link_p.after(n, 2))
                    pool.wait_ge(mt_done.sem, mt_done.after(b, t - 1))
                    nc.gpsimd.tensor_tensor(mixed[:, s], tree[:, 0:inner], tree[:, inner:2 * inner], ALU.add).then_inc(mixed_done.sem, 1)

            in_batches(pool, body)

        @block.tensor
        def _(pe):
            def gate_up(b, t, q, c):
                if t:
                    pe.wait_ge(base_done.sem, base_done.after(b * TILES + t - 1, c + 1))
                else:
                    pe.wait_ge(sh_hid_done.sem, sh_hid_done.after(b, c + 1))
                for g, name in enumerate(("ex_gate", "ex_up")):
                    for k in range(KD):
                        at = slice(t * P, (t + 1) * P)
                        col = k * wide + c * 512
                        mm = products(nc, gu[:, c, g, :], (xin.hT[q][0][:, k, at], xin.hT[q][1][:, k, at]),
                                      w.part(name, col, col + 512), k == 0, k == KD - 1)
                mm.then_inc(gu_done.sem, 1)

            def route(b, q):
                pe.wait_ge(xin.ready.sem, xin.ready.after(b, 1))
                for t in range(TILES):
                    for k in range(KD):
                        at = slice(t * P, (t + 1) * P)
                        mm = products(nc, route_ps[:, t * P:(t + 1) * P], (xin.hT[q][0][:, k, at], xin.hT[q][1][:, k, at]),
                                      w.part("router", k * experts, (k + 1) * experts), k == 0, k == KD - 1)
                mm.then_inc(logits_done.sem, 1)

            def turn_routes(b):
                pe.wait_ge(routed.sem, routed.after(b, 1))
                for t in range(TILES):
                    mm = nc.tensor.transpose(route_ps[:, t * P:(t + 1) * P], rest[:, t, 0:experts], keep["ident"][:])
                mm.then_inc(rt_done.sem, 1)

            def mix_coefficients(b):
                pe.wait_ge(rt_copied.sem, rt_copied.after(b, 1))
                for t in range(TILES):
                    mm = nc.tensor.matmul(route_ps[:, t * basis:(t + 1) * basis], route_t[:, t * P:(t + 1) * P], mix[:], start=True, stop=True)
                mm.then_inc(coeff_done.sem, 1)

            def shared_up(b, q, after_tile):
                for i in range(2):
                    if after_tile:
                        pe.wait_ge(base_done.sem, after_tile(i))
                    for g, name in enumerate(("sh_gate", "sh_up")):
                        for k in range(KD):
                            col = k * shared + i * P
                            mm = products(nc, gu[:, i, g, :], w.part(name, col, col + P),
                                          (xin.hT[q][0][:, k, :], xin.hT[q][1][:, k, :]), k == 0, k == KD - 1)
                    mm.then_inc(sh_done.sem, 1)

            def turn_mixed(b, t):
                pe.wait_ge(mixed_done.sem, mixed_done.after(b * TILES + t, 1))
                nc.tensor.transpose(mixed_ps[:, t * P:(t + 1) * P], mixed[:, t % 2], keep["ident"][:]).then_inc(mt_done.sem, 1)

            def down(b):
                pe.wait_ge(mt_low.sem, mt_low.after(b, 1))
                pe.wait_ge(sh_low.sem, sh_low.after(b, 1))
                for t in range(TILES):
                    at = slice(t * P, (t + 1) * P)
                    products(nc, o_ps[:, t, :], (mixedT[0][:, at], mixedT[1][:, at]), w.part("ex_down", 0, D), True, False)
                    for i in range(2):
                        mm = products(nc, o_ps[:, t, :], (sh_hT[0][:, i, at], sh_hT[1][:, i, at]),
                                      w.part("sh_down", i * D, (i + 1) * D), False, i == 1)
                mm.then_inc(o_done.sem, 1)

            def body(b, q, first, last):
                for t in range(TILES):
                    gate_up(b, t, q, 0)
                    if t == 0:
                        turn_routes(b)
                    gate_up(b, t, q, 1)
                    if t == 0:
                        mix_coefficients(b)
                        if not first:
                            turn_mixed(b - 1, TILES - 1)
                        if not last:
                            if not first:
                                pe.wait_ge(y_done.sem, y_done.before(b, 1, back=2))
                            xin.transpose(pe, b + 1)
                    if t == 1 and not first:
                        if not last:
                            pe.wait_ge(xin.whole.sem, xin.whole.after(b + 1, 1))
                        else:
                            pe.wait_ge(y_done.sem, y_done.before(b, 1, back=2))
                        down(b - 1)
                    if t:
                        turn_mixed(b, t - 1)
                    if t == 2 and not last:
                        pe.wait_ge(coeff_ready.sem, coeff_ready.after(b, 1))
                        route(b + 1, 1 - q)
                if not last:
                    shared_up(b + 1, 1 - q, lambda i: base_done.after(b * TILES + TILES - 1, i + 1))

            xin.transpose(pe, 0)
            pe.wait_ge(w.ready, w.count("sh_down"))
            route(0, 0)
            shared_up(0, 0, None)
            pe.wait_ge(mix_ready, 1)
            in_batches(pe, body)
            turn_mixed(B - 1, TILES - 1)
            down(B - 1)

        @block.scalar
        def _(act):
            def exponentials(b):
                act.wait_ge(neg_ready.sem, neg_ready.after(b, 1))
                for t in range(TILES):
                    ins = nc.scalar.activation(probs[:, t, 0:experts], route_ps[:, t * P:(t + 1) * P], ACT.Exp,
                                               bias=neg_top[:, t:t + 1], accum_out=total[:, t:t + 1])
                ins.then_inc(exp_done.sem, 1)

            def copy_routes(b):
                act.wait_ge(rt_done.sem, rt_done.after(b, 1))
                nc.scalar.activation(route_t[:], route_ps[:], ACT.Copy).then_inc(rt_copied.sem, 1)

            def shared_silu(b):
                for i in range(2):
                    act.wait_ge(sh_done.sem, sh_done.after(b, i + 1))
                    nc.scalar.activation(sh_silu[:, i, :], gu[:, i, 0, :], ACT.Silu).then_inc(sh_silu_done.sem, 1)

            def shared_high(b):
                if not isinstance(b, int) or b:
                    act.wait_ge(o_done.sem, o_done.after(b - 1, 1))
                act.wait_ge(sh_hid_done.sem, sh_hid_done.after(b, 2))
                nc.scalar.activation(sh_hT[0][:], sh_hid[:], ACT.Copy).then_inc(sh_high.sem, 1)

            def mixed_high(b):
                act.wait_ge(mt_done.sem, mt_done.after(b, TILES))
                nc.scalar.activation(mixedT[0][:], mixed_ps[:], ACT.Copy).then_inc(mt_high.sem, 1)

            def body(b, q, first, last):
                for t in range(TILES):
                    n = b * TILES + t
                    if t == 3 and not last:
                        exponentials(b + 1)
                    for c in range(2):
                        act.wait_ge(gu_done.sem, gu_done.after(n, c + 1))
                        nc.scalar.activation(silu[:, t % 2, c * 512:(c + 1) * 512], gu[:, c, 0, :], ACT.Silu).then_inc(silu_done.sem, 1)
                        if t == 0 and c == 0:
                            copy_routes(b)
                    if t == 0:
                        if not first:
                            mixed_high(b - 1)
                        if not last:
                            xin.modulate(act, b + 1)
                    if t == 2:
                        shared_high(b)
                if not last:
                    shared_silu(b + 1)

            xin.modulate(act, 0)
            exponentials(0)
            shared_silu(0)
            in_batches(act, body)
            mixed_high(B - 1)

        @block.vector
        def _(dve):
            def route_tops(b, link):
                dve.wait_ge(logits_done.sem, logits_done.after(b, 1))
                link(nc.vector.tensor_reduce(top_logit[:], route_ps[:].rearrange("p (t e) -> p t e", t=TILES), AX.X, ALU.max))
                nc.vector.tensor_scalar(neg_top[:], top_logit[:], -1.0, None, ALU.mult).then_inc(neg_ready.sem, 1)

            def route_weights(b, link):
                dve.wait_ge(exp_done.sem, exp_done.after(b, 1))
                link(nc.vector.reciprocal(total[:], total[:]))
                for t in range(TILES):
                    ins = nc.vector.tensor_scalar(probs[:, t, 0:experts], probs[:, t, 0:experts], total[:, t:t + 1], None, ALU.mult)
                link(ins, wait_apart)
                for t in range(TILES):
                    ins = nc.vector.max(best[:, t, :], probs[:, t, 0:experts])
                link(ins)
                nc.vector.memset(best[:, :, top:8], -1.0)
                link(nc.vector.tensor_reduce(best_sum[:], best[:, :, 0:top], AX.X, ALU.add), wait_apart)
                for t in range(TILES):
                    ins = nc.vector.match_replace(rest[:, t, :], best[:, t, :], probs[:, t, :], 0.0)
                link(ins)
                link(nc.vector.tensor_scalar(best_sum[:], best_sum[:], 1e-8, None, ALU.add))
                link(nc.vector.reciprocal(best_sum[:], best_sum[:]))
                link(nc.vector.tensor_tensor(rest[:], probs[:], rest[:], ALU.subtract))
                for t in range(TILES):
                    ins = nc.vector.tensor_scalar(rest[:, t, :], rest[:, t, :], best_sum[:, t:t + 1], None, ALU.mult)
                ins.then_inc(routed.sem, 1)

            def copy_coefficients(b, q):
                dve.wait_ge(coeff_done.sem, coeff_done.after(b, 1))
                nc.vector.tensor_copy(coeff[:, q], route_ps[:, 0:TILES * basis].rearrange("p (t k) -> p t k", t=TILES)).then_inc(coeff_ready.sem, 1)

            def shared_hidden(b):
                for i in range(2):
                    dve.wait_ge(sh_silu_done.sem, sh_silu_done.after(b, i + 1))
                    nc.vector.tensor_tensor(sh_hid[:, i, :], sh_silu[:, i, :], gu[:, i, 1, :], ALU.mult).then_inc(sh_hid_done.sem, 1)

            def shared_low(b):
                dve.wait_ge(sh_high.sem, sh_high.after(b, 1))
                low(nc, sh_hT[1][:], sh_hid[:], sh_hT[0][:]).then_inc(sh_low.sem, 1)

            def mixed_low(b):
                dve.wait_ge(mt_high.sem, mt_high.after(b, 1))
                low(nc, mixedT[1][:], mixed_ps[:], mixedT[0][:]).then_inc(mt_low.sem, 1)

            def residual(b):
                dve.wait_ge(o_done.sem, o_done.after(b, 1))
                dve.wait_ge(xin.residual_loaded.sem, xin.residual_loaded.after(b, 32))
                dve.wait_ge(y_stored.sem, y_stored.before(b, 16))
                rows = xin.gate_row[:].to_broadcast([P, TILES, D])
                nc.vector.tensor_tensor(y[:], o_ps[:], rows, ALU.mult).then_inc(link_y.sem, 1)
                dve.wait_ge(link_y.sem, link_y.after(b, 1))
                nc.vector.tensor_tensor(y[:], y[:], xin.residual[:], ALU.add).then_inc(y_done.sem, 1)

            def linker(b):
                count = [0]

                def link(ins, wait=wait_on):
                    count[0] += 1
                    ins.then_inc(link_r.sem, 1)
                    wait(dve, link_r.sem, link_r.after(b, count[0]))
                return link, count

            def body(b, q, first, last):
                link, count = linker(b + 1)
                for t in range(TILES):
                    n = b * TILES + t
                    s = t % 2
                    if t == 0 and not last:
                        xin.norm(dve, b + 1)
                    if t == 1 and not last:
                        xin.halve(dve, b + 1, 1 - q)
                    if t == 3 and not last:
                        route_tops(b + 1, link)
                    dve.wait_ge(mixed_done.sem, mixed_done.before(n, 1, back=2))
                    for c in range(2):
                        at = slice(c * 512, (c + 1) * 512)
                        dve.wait_ge(silu_done.sem, silu_done.after(n, c + 1))
                        nc.vector.tensor_tensor(base[:, s, at], silu[:, s, at], gu[:, c, 1, :], ALU.mult).then_inc(base_done.sem, 1)
                        if t == 3 and c == 0 and not last:
                            route_weights(b + 1, link)
                    if t == 0:
                        copy_coefficients(b, q)
                        dve.wait_ge(coeff_ready.sem, coeff_ready.after(b, 1))
                    dve.wait_ge(base_done.sem, base_done.after(n, 2))
                    grid = base[:, s].rearrange("p (k i) -> p k i", k=basis)
                    by = coeff[:, q, t, :].rearrange("p (k o) -> p k o", o=1).to_broadcast([P, basis, inner])
                    nc.vector.tensor_tensor(grid, grid, by, ALU.mult).then_inc(weighed.sem, 1)
                    if t == 0 and not first:
                        mixed_low(b - 1)
                    if t == 1 and not first:
                        residual(b - 1)
                    if t == 2:
                        shared_low(b)
                if not last:
                    shared_hidden(b + 1)
                    assert count[0] == link_r.per, count[0]

            nc.vector.memset(probs[:], -1.0)
            xin.norm(dve, 0)
            xin.halve(dve, 0, 0)
            dve.wait_ge(amp_loaded, 32)
            links = [0]

            def link(ins):
                links[0] += 1
                ins.then_inc(mix_link, 1)
                dve.wait_ge(mix_link, links[0])

            link(nc.vector.tensor_tensor(amp[:], amp[:], amp[:], ALU.mult))
            link(nc.vector.tensor_tensor(mix[:], amp[:, :, 0], amp[:, :, 1], ALU.add))
            link(nc.vector.tensor_reduce(mix_sum[:], mix[:], AX.X, ALU.add))
            link(nc.vector.tensor_scalar(mix_sum[:], mix_sum[:], 1e-8, None, ALU.add))
            link(nc.vector.reciprocal(mix_sum[:], mix_sum[:]))
            nc.vector.tensor_scalar(mix[:], mix[:], mix_sum[:, 0:1], e_scale[:, 0:1], ALU.mult, ALU.mult).then_inc(mix_ready, 1)
            w.split(dve)
            link, _ = linker(0)
            route_tops(0, link)
            route_weights(0, link)
            shared_hidden(0)
            in_batches(dve, body)
            mixed_low(B - 1)
            residual(B - 1)
        m.end()


class Root:

    def __init__(self, nc, m, name, width):
        self.nc = nc
        self.v, self.tmp, self.root = (m.sb(f"{name}_{n}", [P, 2, width]) for n in ("v", "tmp", "root"))

    def solve(self, link):
        root_by_halving(self.nc, link, self.v, self.tmp, self.root)


def gla_stage(nc, io, keep):
    heads, hk, hv, chunk, rank = 8, 16, 32, 64, 16
    keys, vals = heads * hk, heads * hv
    chunks = S // chunk
    inner = 768
    ki = inner // P
    gate_norm = 16.0
    rms_eps = 1e-6
    with ExitStack() as ctx:
        m = Alloc(nc, ctx, "gla")
        entries = [("g_q", KD * keys), ("g_k", KD * keys), ("g_vg", KD * 2 * vals), ("g_o", KD * D),
                   ("g_gate", KD * inner), ("g_up", KD * inner), ("g_down", ki * D)]
        low1 = m.sb("low1", [P, KD, rank])
        low2 = m.sb("low2", [rank, keys])
        low_bias = m.sb("low_bias", [P, 1])
        norm_cols = m.sb("norm_cols", [P, 2, KD])
        gnorm = m.sb("gnorm", [P, hv])
        own_head = m.sb("own_head", [P, heads])
        state_mask = m.sb("state_mask", [P, vals])
        tri = m.sb("tri", [P, chunk])
        carry = m.sb("carry", [P, S])
        one = m.sb("one", [P, 1])

        class Lane:

            def __init__(self, q):
                n = f"{q}_"
                self.q = q
                self.pre, self.h0, self.t1 = (m.sb(n + k, [P, TILES, D]) for k in ("pre", "h0", "t1"))
                self.rows = m.sb(n + "rows", [P, 2, D])
                self.gate = m.sb(n + "gate", [P, 1, D])
                self.t2 = m.sb(n + "t2", [P, 1024])
                self.t3 = m.sb(n + "t3", [P, 1024])
                self.hT = [m.sb(f"{n}hT{i}", [P, KD, S], F32R) for i in "hl"]
                self.act = [m.sb(f"{n}act{i}", [P, 2, S], F32R) for i in "hl"]
                area = self.area = m.sb(n + "area", [P, 8192])
                cut = [area[:, i * 512:(i + 1) * 512] for i in range(16)]
                self.eb, self.enb, self.g, self.bs = cut[0:4]
                self.low = area[0:rank, 0:512]
                self.a = area[:, 0:2048].rearrange("p (t n) -> p t n", t=TILES)
                self.hn = area[:, 0:1024].rearrange("p (t d) -> p t d", t=TILES)
                self.turned = area[:, 1024:2048].rearrange("p (k s) -> p k s", k=KD)
                self.qe, self.ke, self.kd = cut[4:7]
                self.kd_tok = area[:, 3584:4096].rearrange("p (t n) -> p t n", t=TILES)
                self.v = area[:, 4096:5120].rearrange("p (t n) -> p t n", t=TILES)
                self.x = self.v
                self.gs = area[:, 5120:6144].rearrange("p (t n) -> p t n", t=TILES)
                self.state = area[:, 6144:8192].rearrange("p (c n) -> p c n", c=chunks)
                self.ebl = m.sb(n + "ebl", [P, chunks])
                self.stats = m.sb(n + "stats", [P, TILES, 6])
                self.mv = m.sb(n + "mv", [P, TILES, 2])
                self.sq = m.sb(n + "sq", [P, TILES])
                self.X = m.ps(n + "X", [P, 2, 512])
                self.Y = m.ps(n + "Y", [P, 2, 512])
                self.Yt = self.Y[:].rearrange("p w n -> p (w n)").rearrange("p (t d) -> p t d", t=TILES)
                self.whole = self.t1[:].rearrange("p t d -> p (t d)").rearrange("p (k s) -> p k s", k=KD)
                self.qx = [t[:].rearrange("p (c h n) -> p c h n", c=2, h=heads) for t in (self.t2, self.t3)]
                self.pre_loaded = m.counted(n + "pre_loaded", 32)
                self.x_loaded = m.counted(n + "x_loaded", 32)
                self.front_link = m.counted(n + "front_link", 4)
                self.link = m.counted(n + "link", 8)
                self.alink = m.counted(n + "alink", 1)
                self.h0_done = m.counted(n + "h0_done", 1)
                self.sq1 = m.counted(n + "sq1", 1)
                self.hn_done = m.counted(n + "hn_done", 1)
                self.in_psum = m.counted(n + "in_psum", 3)
                self.whole_done = m.counted(n + "whole_done", 2)
                self.ht_link = m.counted(n + "ht_link", 2)
                self.ht_ready = m.counted(n + "ht_ready", 2)
                self.low_done = m.counted(n + "low_done", 1)
                self.low_copied = m.counted(n + "low_copied", 1)
                self.qk_done = m.counted(n + "qk_done", 1)
                self.gk_done = m.counted(n + "gk_done", 1)
                self.abs_done = m.counted(n + "abs_done", 1)
                self.min_done = m.counted(n + "min_done", 1)
                self.zl_done = m.counted(n + "zl_done", 1)
                self.scan_done = m.counted(n + "scan_done", 1)
                self.exps_done = m.counted(n + "exps_done", 1)
                self.qk_used = m.counted(n + "qk_used", 1)
                self.qx_done = m.counted(n + "qx_done", 4)
                self.vg_done = m.counted(n + "vg_done", 4)
                self.vg_used = m.counted(n + "vg_used", 4)
                self.gs_done = m.counted(n + "gs_done", 1)
                self.kd_done = m.counted(n + "kd_done", 1)
                self.kd_copied = m.counted(n + "kd_copied", 1)
                self.a_done = m.counted(n + "a_done", 4)
                self.a_used = m.counted(n + "a_used", 4)
                self.u_done = m.counted(n + "u_done", 2)
                self.u_used = m.counted(n + "u_used", 2)
                self.state_done = m.counted(n + "state_done", 1)
                self.o_done = m.counted(n + "o_done", 1)
                self.sq2 = m.counted(n + "sq2", 1)
                self.o_used = m.counted(n + "o_used", 1)
                self.on_done = m.counted(n + "on_done", 1)
                self.ot_high = m.counted(n + "ot_high", 1)
                self.ot_ready = m.counted(n + "ot_ready", 1)
                self.wo_done = m.counted(n + "wo_done", 1)
                self.x1_done = m.counted(n + "x1_done", 1)
                self.sq3 = m.counted(n + "sq3", 1)
                self.h2_done = m.counted(n + "h2_done", 1)
                self.gu_done = m.counted(n + "gu_done", ki)
                self.sg_done = m.counted(n + "sg_done", ki)
                self.f_done = m.counted(n + "f_done", ki)
                self.fh_done = m.counted(n + "fh_done", ki)
                self.fl_done = m.counted(n + "fl_done", ki)
                self.down_done = m.counted(n + "down_done", ki)
                self.sum_done = m.counted(n + "sum_done", 1, credit=1)
                self.plink = m.counted(n + "plink", 1)
                self.y_done = m.counted(n + "y_done", 1, credit=1)
                self.y_stored = m.counted(n + "y_stored", 16, credit=16)

        lanes = [Lane(q) for q in range(2)]
        w = SplitWeights(nc, m, io, entries, lanes[1].area)
        ln_root, rms1_root, rms2_root = (Root(nc, m, k, TILES) for k in ("ln", "rms1", "rms2"))
        head_root = Root(nc, m, "head", TILES * heads)
        front_root_link = m.counted("front_root_link", 22)
        root_link = m.counted("root_link", 22)
        small_loaded = m.sem("small_loaded")
        zeroed = m.sem("zeroed")
        masks_made = m.sem("masks_made")
        block = m.begin()
        ident = keep["ident"]

        def rounds(eng, body):
            with eng.Fori(0, B // 2 - 1) as i:
                body(i, True)
            body(B // 2 - 1, False)

        @block.sync
        def _(sp):
            for ln in lanes:
                for signal in (ln.sum_done, ln.y_done, ln.y_stored):
                    sp.sem_inc(signal.sem, signal.credit)

            def tokens(name, i, ln):
                return io[name][bass.ds((i * 2 + ln.q) * S, S), :].rearrange("(t p) d -> p t d", p=P)

            def load_input(ln, i):
                sp.dma_start(ln.pre[:], tokens("x2", i, ln)).then_inc(ln.pre_loaded.sem, 16)
                sp.dma_start(ln.rows[:], io["mod_rows"][1, bass.ds(i * 2 + ln.q, 1), 0:2 * D].rearrange("o (r d) -> o r d", r=2).to_broadcast([P, 2, D])
                             ).then_inc(ln.pre_loaded.sem, 16)

            def body(i, more):
                for ln in lanes:
                    wait_apart(sp, ln.y_done.sem, ln.y_done.before(i, 1))
                    wait_apart(sp, ln.o_done.sem, ln.o_done.done(i))
                    sp.dma_start(ln.x[:], tokens("x2", i, ln)).then_inc(ln.x_loaded.sem, 16)
                    sp.dma_start(ln.gate[:, 0], io["mod_rows"][1, bass.ds(i * 2 + ln.q, 1), GA * D:(GA + 1) * D].to_broadcast([P, D])
                                 ).then_inc(ln.x_loaded.sem, 16)
                if more:
                    for ln in lanes:
                        wait_apart(sp, ln.x1_done.sem, ln.x1_done.done(i))
                        load_input(ln, i + 1)
                for ln in lanes:
                    wait_apart(sp, ln.y_done.sem, ln.y_done.after(i, 1))
                    sp.dma_start(tokens("x3", i, ln), ln.t1[:]).then_inc(ln.y_stored.sem, 16)

            for ln in lanes:
                load_input(ln, 0)
            for dst, name in ((low1[:], "gk_w1"), (low2[:], "gk_w2"), (low_bias[:], "gk_b"), (norm_cols[:], "norm_cols")):
                sp.dma_start(dst, io[name]).then_inc(small_loaded, 16)
            sp.dma_start(gnorm[:], io["gnorm"].to_broadcast([P, hv])).then_inc(small_loaded, 16)
            w.load(sp)
            rounds(sp, body)
            for ln in lanes:
                sp.wait_ge(ln.y_stored.sem, ln.y_stored.done(B // 2 - 1))

        @block.gpsimd
        def _(pool):
            for t in (own_head, state_mask, tri, carry, one):
                nc.gpsimd.memset(t[:], 1.0).then_inc(zeroed, 1)
            pool.wait_ge(zeroed, 5)
            nc.gpsimd.memset(carry[:].rearrange("p (c n) -> p c n", c=chunks)[:, :, 0:1], 0.0).then_inc(masks_made, 1)
            for t, pattern in ((own_head[:], [[-hk, heads]]), (state_mask[:].rearrange("p (h n) -> p h n", h=heads), [[-hk, heads], [0, hv]])):
                nc.gpsimd.affine_select(out=t, in_=t, compare_op=ALU.is_ge, fill=0.0, base=0, pattern=pattern,
                                        channel_multiplier=1).then_inc(masks_made, 1)
            pool.wait_ge(masks_made, 3)
            for t, pattern in ((own_head[:], [[hk, heads]]), (state_mask[:].rearrange("p (h n) -> p h n", h=heads), [[hk, heads], [0, hv]])):
                nc.gpsimd.affine_select(out=t, in_=t, compare_op=ALU.is_ge, fill=0.0, base=hk - 1, pattern=pattern,
                                        channel_multiplier=-1).then_inc(masks_made, 1)
            for n in range(2):
                t = tri[n * chunk:(n + 1) * chunk, :]
                pool.wait_ge(masks_made, 5 + n)
                nc.gpsimd.affine_select(out=t, in_=t, compare_op=ALU.is_ge, fill=0.0, base=0, pattern=[[1, chunk]],
                                        channel_multiplier=-1).then_inc(masks_made, 1)
            pool.wait_ge(masks_made, 7)
            pool.wait_ge(small_loaded, 80)

            def spread_queries(ln, i, t):
                if t == 0:
                    pool.wait_ge(ln.qk_used.sem, ln.qk_used.done(i))
                if t >= 2:
                    pool.wait_ge(ln.a_done.sem, ln.a_done.after(i, t - 1))
                for c in range(2):
                    at = slice(t * P + c * chunk, t * P + (c + 1) * chunk)
                    src = ln.qe[:, at].rearrange("p (o n) -> p o n", o=1).to_broadcast([P, heads, chunk])
                    own = own_head[:].rearrange("p (h o) -> p h o", o=1).to_broadcast([P, heads, chunk])
                    ins = nc.gpsimd.tensor_tensor(ln.qx[t % 2][:, c], src, own, ALU.mult)
                ins.then_inc(ln.qx_done.sem, 1)

            def scale_gate(ln, i):
                pool.wait_ge(ln.vg_used.sem, ln.vg_used.done(i))
                g = ln.gs.rearrange("p t n -> p (t n)").rearrange("p (a v) -> p a v", v=hv)
                by = gnorm[:].rearrange("p (o v) -> p o v", o=1).to_broadcast([P, TILES * heads, hv])
                nc.gpsimd.tensor_tensor(g, g, by, ALU.mult).then_inc(ln.gs_done.sem, 1)

            def act_low(ln, i, c):
                pool.wait_ge(ln.fh_done.sem, ln.fh_done.after(i, c + 1))
                src = ln.t1[:].rearrange("p t d -> p (t d)")[:, (c % 2) * 512:(c % 2 + 1) * 512]
                nc.gpsimd.tensor_tensor(ln.act[1][:, c % 2, :], src, ln.act[0][:, c % 2, :].bitcast(F32), ALU.subtract).then_inc(ln.fl_done.sem, 1)

            def last_sum(ln, i):
                pool.wait_ge(ln.sum_done.sem, ln.sum_done.done(i))
                pool.wait_ge(ln.x_loaded.sem, ln.x_loaded.done(i))
                gate = ln.gate[:].to_broadcast([P, TILES, D])
                nc.gpsimd.tensor_tensor(ln.t1[:], ln.t1[:], gate, ALU.mult).then_inc(ln.plink.sem, 1)
                pool.wait_ge(ln.plink.sem, ln.plink.done(i))
                nc.gpsimd.tensor_tensor(ln.t1[:], ln.t1[:], ln.x[:], ALU.add).then_inc(ln.y_done.sem, 1)

            def body(i, more):
                for t in range(TILES):
                    for ln in lanes:
                        spread_queries(ln, i, t)
                for ln in lanes:
                    scale_gate(ln, i)
                for c in range(ki):
                    for ln in lanes:
                        act_low(ln, i, c)
                for ln in lanes:
                    last_sum(ln, i)

            rounds(pool, body)

        @block.tensor
        def _(pe):
            def turn(ln, src):
                return transpose_rows(nc, ln.X, src, ident)

            def inputs(ln, i, ready, src=None):
                pe.wait_ge(ready.sem, ready.done(i))
                turn(ln, src or ln.t1).then_inc(ln.in_psum.sem, 1)

            def projections(ln, i):
                pe.wait_ge(ln.whole_done.sem, ln.whole_done.after(i, 1))
                for k in range(KD):
                    mm = nc.tensor.matmul(ln.X[0:rank, 0, :], low1[:, k, :], ln.turned[:, k, :], start=(k == 0), stop=(k == KD - 1))
                mm.then_inc(ln.low_done.sem, 1)
                pe.wait_ge(ln.ht_ready.sem, ln.ht_ready.after(i, 1))
                pe.wait_ge(ln.sum_done.sem, ln.sum_done.before(i, 1))
                for n, name in enumerate(("g_q", "g_k")):
                    for k in range(KD):
                        mm = products(nc, ln.Y[:, n, :], w.part(name, k * keys, (k + 1) * keys),
                                      (ln.hT[0][:, k, :], ln.hT[1][:, k, :]), k == 0, k == KD - 1)
                mm.then_inc(ln.qk_done.sem, 1)

            def decay_logits(ln, i):
                pe.wait_ge(ln.low_copied.sem, ln.low_copied.done(i))
                nc.tensor.matmul(ln.X[:, 1, :], low2[:], ln.low, start=True, stop=True).then_inc(ln.gk_done.sem, 1)

            def values_gates(ln, i, t):
                if t == 0:
                    pe.wait_ge(ln.min_done.sem, ln.min_done.done(i))
                if t >= 2:
                    pe.wait_ge(ln.vg_used.sem, ln.vg_used.after(i, t - 1))
                at = slice(t * P, (t + 1) * P)
                for k in range(KD):
                    mm = products(nc, ln.X[:, t % 2, :], (ln.hT[0][:, k, at], ln.hT[1][:, k, at]),
                                  w.part("g_vg", k * 512, (k + 1) * 512), k == 0, k == KD - 1)
                mm.then_inc(ln.vg_done.sem, 1)

            def keys_by_token(ln, i):
                pe.wait_ge(ln.qk_used.sem, ln.qk_used.done(i))
                pe.wait_ge(ln.vg_used.sem, ln.vg_used.done(i))
                for t in range(TILES):
                    mm = nc.tensor.transpose(ln.X[:, 0, t * P:(t + 1) * P], ln.kd[:, t * P:(t + 1) * P], ident[:])
                mm.then_inc(ln.kd_done.sem, 1)

            def chunk_products(ln, i, t):
                pe.wait_ge(ln.qx_done.sem, ln.qx_done.after(i, t + 1))
                if t >= 2:
                    pe.wait_ge(ln.a_used.sem, ln.a_used.after(i, t - 1))
                elif t == 1:
                    pe.wait_ge(ln.kd_copied.sem, ln.kd_copied.done(i))
                for c in range(2):
                    at = slice(t * P + c * chunk, t * P + (c + 1) * chunk)
                    mm = nc.tensor.matmul(ln.X[c * chunk:(c + 1) * chunk, 1 - t % 2, :], ln.ke[:, at],
                                          ln.qx[t % 2][:, c].rearrange("p h n -> p (h n)"), start=True, stop=True, skip_group_check=True)
                mm.then_inc(ln.a_done.sem, 1)

            def state_updates(ln, i, n):
                if n == 0:
                    pe.wait_ge(ln.kd_copied.sem, ln.kd_copied.done(i))
                else:
                    pe.wait_ge(ln.u_used.sem, ln.u_used.after(i, 1))
                for c in range(4 * n, min(4 * n + 4, chunks - 1)):
                    at = slice((c % 2) * chunk, (c % 2 + 1) * chunk)
                    mm = nc.tensor.matmul(ln.Yt[:, (c % 2) * 2 + c // 2 % 2, :], ln.kd_tok[at, c // 2, :], ln.v[at, c // 2, :], start=True, stop=True)
                mm.then_inc(ln.u_done.sem, 1)

            def outputs(ln, i):
                pe.wait_ge(ln.state_done.sem, ln.state_done.done(i))
                pe.wait_ge(ln.a_used.sem, ln.a_used.done(i))
                for c in range(chunks):
                    t = c // 2
                    at = slice((c % 2) * chunk, (c % 2 + 1) * chunk)
                    nc.tensor.matmul(ln.Yt[at, t, :], ln.qe[:, c * chunk:(c + 1) * chunk], ln.state[:, c, :],
                                     start=True, stop=False, skip_group_check=True)
                    for h in range(heads):
                        mm = nc.tensor.matmul(ln.Yt[at, t, h * hv:(h + 1) * hv], ln.a[at, t, h * chunk:(h + 1) * chunk],
                                              ln.v[at, t, h * hv:(h + 1) * hv], start=False, stop=(h == heads - 1), skip_group_check=True)
                mm.then_inc(ln.o_done.sem, 1)

            def project_out(ln, i):
                pe.wait_ge(ln.ot_ready.sem, ln.ot_ready.done(i))
                for t in range(TILES):
                    at = slice(t * P, (t + 1) * P)
                    for k in range(KD):
                        mm = products(nc, ln.Yt[:, t, :], (ln.hT[0][:, k, at], ln.hT[1][:, k, at]),
                                      w.part("g_o", k * D, (k + 1) * D), k == 0, k == KD - 1)
                mm.then_inc(ln.wo_done.sem, 1)

            def gate_up(ln, i, c):
                if c == 0:
                    pe.wait_ge(ln.ht_ready.sem, ln.ht_ready.done(i))
                else:
                    pe.wait_ge(ln.f_done.sem, ln.f_done.after(i, c))
                for g, name in enumerate(("g_gate", "g_up")):
                    for k in range(KD):
                        col = k * inner + c * P
                        mm = products(nc, ln.X[:, g, :], w.part(name, col, col + P),
                                      (ln.hT[0][:, k, :], ln.hT[1][:, k, :]), k == 0, k == KD - 1)
                mm.then_inc(ln.gu_done.sem, 1)

            def down(ln, i, c):
                pe.wait_ge(ln.fl_done.sem, ln.fl_done.after(i, c + 1))
                for t in range(TILES):
                    at = slice(t * P, (t + 1) * P)
                    for n, (x, y) in enumerate(((0, 0), (0, 1), (1, 0))):
                        mm = nc.tensor.matmul(ln.Yt[:, t, :], ln.act[x][:, c % 2, at], w.part("g_down", c * D, (c + 1) * D)[y],
                                              start=(c == 0 and t % 2 == 0 and n == 0), stop=(c == ki - 1 and n == 2), skip_group_check=True)
                mm.then_inc(ln.down_done.sem, 1)

            pe.wait_ge(small_loaded, 80)
            pe.wait_ge(w.ready, w.count("g_down"))
            for ln in lanes:
                inputs(ln, 0, ln.hn_done, ln.hn)

            def body(i, more):
                for ln in lanes:
                    projections(ln, i)
                for ln in lanes:
                    decay_logits(ln, i)
                for t in range(TILES):
                    for ln in lanes:
                        values_gates(ln, i, t)
                for ln in lanes:
                    keys_by_token(ln, i)
                for ln in lanes:
                    chunk_products(ln, i, 0)
                for ln in lanes:
                    state_updates(ln, i, 0)
                for ln in lanes:
                    chunk_products(ln, i, 1)
                for ln in lanes:
                    state_updates(ln, i, 1)
                for t in range(2, TILES):
                    for ln in lanes:
                        chunk_products(ln, i, t)
                for ln in lanes:
                    outputs(ln, i)
                for ln in lanes:
                    inputs(ln, i, ln.on_done)
                for ln in lanes:
                    project_out(ln, i)
                for ln in lanes:
                    inputs(ln, i, ln.h2_done)
                for c in range(ki):
                    for ln in lanes:
                        gate_up(ln, i, c)
                        if c:
                            down(ln, i, c - 1)
                for ln in lanes:
                    if more:
                        pe.wait_ge(ln.f_done.sem, ln.f_done.done(i))
                        inputs(ln, i + 1, ln.hn_done, ln.hn)
                for ln in lanes:
                    down(ln, i, ki - 1)

            rounds(pe, body)

        @block.scalar
        def _(act):
            def squares(ln, i, src, ready, done):
                act.wait_ge(ready.sem, ready.done(i))
                for t in range(TILES):
                    ins = nc.scalar.activation(ln.t3[:, t * D:(t + 1) * D], src[:, t, :], ACT.Square, accum_out=ln.sq[:, t:t + 1])
                ins.then_inc(done.sem, 1)

            def whole(ln, i, n):
                act.wait_ge(ln.in_psum.sem, ln.in_psum.after(i, n))
                out = ln.turned if n == 1 else ln.whole
                for k in range(KD):
                    ins = nc.scalar.activation(out[:, k, :], ln.X[:, k, :], ACT.Copy, scale=norm_cols[:, n // 2, k:k + 1])
                ins.then_inc(ln.whole_done.sem, 1)

            def copy_low(ln, i):
                act.wait_ge(ln.low_done.sem, ln.low_done.done(i))
                nc.scalar.activation(ln.low, ln.X[0:rank, 0, :], ACT.Copy).then_inc(ln.low_copied.sem, 1)

            def decay_logs(ln, i):
                act.wait_ge(ln.gk_done.sem, ln.gk_done.done(i))
                ins = nc.scalar.activation(ln.enb, ln.X[:, 1, :], ACT.Abs, bias=low_bias[:])
                ins.then_inc(ln.abs_done.sem, 1)

            def decay_exps(ln, i):
                act.wait_ge(ln.abs_done.sem, ln.abs_done.done(i))
                nc.scalar.activation(ln.enb, ln.enb, ACT.Exp, scale=-1.0).then_inc(ln.alink.sem, 1)

            def decay_lns(ln, i):
                act.wait_ge(ln.alink.sem, ln.alink.done(i))
                nc.scalar.activation(ln.enb, ln.enb, ACT.Ln, bias=one[:]).then_inc(ln.zl_done.sem, 1)

            def decays(ln, i):
                act.wait_ge(ln.scan_done.sem, ln.scan_done.done(i))
                nc.scalar.activation(ln.eb, ln.bs, ACT.Exp, scale=1.0 / gate_norm)
                nc.scalar.activation(ln.enb, ln.bs, ACT.Exp, scale=-1.0 / gate_norm)
                nc.scalar.activation(ln.g, ln.g, ACT.Exp, scale=1.0 / gate_norm).then_inc(ln.exps_done.sem, 1)

            def values_gates(ln, i, t):
                act.wait_ge(ln.vg_done.sem, ln.vg_done.after(i, t + 1))
                if t == 0:
                    act.wait_ge(ln.y_done.sem, ln.y_done.before(i, 1))
                nc.scalar.activation(ln.v[:, t, :], ln.X[:, t % 2, 0:vals], ACT.Copy)
                nc.scalar.activation(ln.gs[:, t, :], ln.X[:, t % 2, vals:2 * vals], ACT.Silu).then_inc(ln.vg_used.sem, 1)

            def copy_keys(ln, i):
                act.wait_ge(ln.kd_done.sem, ln.kd_done.done(i))
                nc.scalar.activation(ln.kd_tok, ln.X[:, 0, :].rearrange("p (t n) -> p t n", t=TILES), ACT.Copy).then_inc(ln.kd_copied.sem, 1)

            def head_squares(ln, i):
                act.wait_ge(ln.o_done.sem, ln.o_done.done(i))
                nc.scalar.activation(ln.t2[:].rearrange("p (w n) -> p w n", w=2), ln.Y[:], ACT.Square).then_inc(ln.sq2.sem, 1)

            def out_high(ln, i):
                act.wait_ge(ln.in_psum.sem, ln.in_psum.after(i, 2))
                nc.scalar.activation(ln.hT[0][:], ln.X[:], ACT.Copy).then_inc(ln.ot_high.sem, 1)

            def activate(ln, i, c):
                act.wait_ge(ln.gu_done.sem, ln.gu_done.after(i, c + 1))
                at = slice((c % 2) * 512, (c % 2 + 1) * 512)
                nc.scalar.activation(ln.t2[:, at], ln.X[:, 0, :], ACT.Silu).then_inc(ln.sg_done.sem, 1)

            def act_high(ln, i, c):
                act.wait_ge(ln.f_done.sem, ln.f_done.after(i, c + 1))
                if c >= 2:
                    act.wait_ge(ln.down_done.sem, ln.down_done.after(i, c - 1))
                src = ln.t1[:].rearrange("p t d -> p (t d)")[:, (c % 2) * 512:(c % 2 + 1) * 512]
                nc.scalar.activation(ln.act[0][:, c % 2, :], src, ACT.Copy).then_inc(ln.fh_done.sem, 1)

            act.wait_ge(small_loaded, 80)
            act.wait_ge(masks_made, 7)
            for ln in lanes:
                squares(ln, 0, ln.pre, ln.h0_done, ln.sq1)

            def body(i, more):
                for ln in lanes:
                    whole(ln, i, 1)
                for ln in lanes:
                    copy_low(ln, i)
                for step in (decay_logs, decay_exps, decay_lns, decays):
                    for ln in lanes:
                        step(ln, i)
                for t in range(TILES):
                    for ln in lanes:
                        values_gates(ln, i, t)
                for ln in lanes:
                    copy_keys(ln, i)
                for ln in lanes:
                    head_squares(ln, i)
                for ln in lanes:
                    out_high(ln, i)
                for ln in lanes:
                    squares(ln, i, ln.h0, ln.x1_done, ln.sq3)
                for ln in lanes:
                    whole(ln, i, 3)
                for c in range(ki):
                    for ln in lanes:
                        activate(ln, i, c)
                    for ln in lanes:
                        act_high(ln, i, c)
                    if c == 2 and more:
                        for ln in lanes:
                            squares(ln, i + 1, ln.pre, ln.h0_done, ln.sq1)

            rounds(act, body)

        @block.vector
        def _(dve):
            def links_of(signal, i):
                count = [0]

                def link(ins, wait=wait_on):
                    count[0] += 1
                    ins.then_inc(signal.sem, 1)
                    wait(dve, signal.sem, signal.after(i, count[0]))
                return link, count

            def norm(ln, i, link):
                dve.wait_ge(ln.pre_loaded.sem, ln.pre_loaded.done(i))
                return moments_of_rows(nc, link, ln.pre, ln.stats, ln.mv, ln_root.v[:, ln.q])

            def modulate(ln, i, link):
                link(norm_rows(nc, ln.pre, ln.pre, ln.mv, ln_root.root[:, ln.q]))
                link(nc.vector.tensor_tensor(ln.pre[:], ln.pre[:], ln.rows[:, 1:2, :].to_broadcast([P, TILES, D]), ALU.mult))
                nc.vector.tensor_tensor(ln.pre[:], ln.pre[:], ln.rows[:, 0:1, :].to_broadcast([P, TILES, D]), ALU.add).then_inc(ln.h0_done.sem, 1)

            def root_norm(ln, out, src, root, done):
                for t in range(TILES):
                    ins = nc.vector.tensor_scalar(out[:, t, :], src[:, t, :], root.root[:, ln.q, t:t + 1], None, ALU.mult)
                ins.then_inc(done.sem, 1)

            class Front:

                def __init__(self, i):
                    self.i = i
                    self.links = [links_of(ln.front_link, i) for ln in lanes]
                    self.root_links = links_of(front_root_link, i)

                def normalise(self):
                    for ln, (link, _) in zip(lanes, self.links):
                        ins = norm(ln, self.i, link)
                    self.root_links[0](ins)

                def modulate(self):
                    ln_root.solve(self.root_links[0])
                    for ln, (link, _) in zip(lanes, self.links):
                        modulate(ln, self.i, link)

                def root_norm(self):
                    for ln in lanes:
                        dve.wait_ge(ln.sq1.sem, ln.sq1.done(self.i))
                        ins = nc.vector.tensor_scalar(rms1_root.v[:, ln.q], ln.sq[:], 1.0 / D, rms_eps, ALU.mult, ALU.add)
                    self.root_links[0](ins)
                    rms1_root.solve(self.root_links[0])
                    for ln in lanes:
                        root_norm(ln, ln.hn, ln.pre, rms1_root, ln.hn_done)
                    for _, count in self.links + [self.root_links]:
                        assert count[0] in (ln.front_link.per, front_root_link.per), count[0]

            def halve(ln, i, n):
                src = ln.turned if n == 1 else ln.whole
                dve.wait_ge(ln.whole_done.sem, ln.whole_done.after(i, n))
                nc.vector.tensor_copy(ln.hT[0][:], src).then_inc(ln.ht_link.sem, 1)
                dve.wait_ge(ln.ht_link.sem, ln.ht_link.after(i, n))
                low(nc, ln.hT[1][:], src, ln.hT[0][:]).then_inc(ln.ht_ready.sem, 1)

            def decay_sums(ln, i, link):
                dve.wait_ge(ln.abs_done.sem, ln.abs_done.done(i))
                nc.vector.tensor_scalar(ln.g, ln.X[:, 1, :], low_bias[:, 0:1], 0.0, ALU.add, ALU.min).then_inc(ln.min_done.sem, 1)
                dve.wait_ge(ln.min_done.sem, ln.min_done.done(i))
                dve.wait_ge(ln.zl_done.sem, ln.zl_done.done(i))
                link(nc.vector.tensor_tensor(ln.g, ln.g, ln.enb, ALU.subtract))
                link(nc.vector.tensor_tensor_scan(ln.bs, carry[:], ln.g, 0.0, ALU.mult, ALU.add))
                b3 = ln.bs.rearrange("p (c n) -> p c n", c=chunks)
                ends = b3[:, :, chunk - 1:chunk].to_broadcast([P, chunks, chunk])
                nc.vector.tensor_tensor(ln.g.rearrange("p (c n) -> p c n", c=chunks), ends, b3, ALU.subtract).then_inc(ln.scan_done.sem, 1)

            def decay_queries_keys(ln, i):
                dve.wait_ge(ln.exps_done.sem, ln.exps_done.done(i))
                dve.wait_ge(ln.qk_done.sem, ln.qk_done.done(i))
                nc.vector.scalar_tensor_tensor(ln.qe, ln.Y[:, 0, :], hk ** -0.5, ln.eb, ALU.mult, ALU.mult)
                nc.vector.tensor_tensor(ln.ke, ln.Y[:, 1, :], ln.enb, ALU.mult)
                nc.vector.tensor_tensor(ln.kd, ln.Y[:, 1, :], ln.g, ALU.mult)
                nc.vector.tensor_copy(ln.ebl[:], ln.eb.rearrange("p (c n) -> p c n", c=chunks)[:, :, chunk - 1]).then_inc(ln.qk_used.sem, 1)

            def masked(ln, i, t):
                if t == 0:
                    dve.wait_ge(ln.qk_used.sem, ln.qk_used.done(i))
                dve.wait_ge(ln.a_done.sem, ln.a_done.after(i, t + 1))
                src = ln.X[:, 1 - t % 2, :].rearrange("p (h n) -> p h n", h=heads)
                by = tri[:].rearrange("p (o n) -> p o n", o=1).to_broadcast([P, heads, chunk])
                nc.vector.tensor_tensor(ln.a[:, t, :].rearrange("p (h n) -> p h n", h=heads), src, by, ALU.mult).then_inc(ln.a_used.sem, 1)

            def own_blocks(ln, i, n):
                dve.wait_ge(ln.u_done.sem, ln.u_done.after(i, n + 1))
                for a in range(2):
                    lo = 4 * n + 2 * a
                    hi = min(lo + 2, chunks - 1)
                    by = state_mask[:].rearrange("p (o n) -> p o n", o=1).to_broadcast([P, hi - lo, vals])
                    src = ln.Y[:, 0:hi - lo, a * vals:(a + 1) * vals]
                    ins = nc.vector.tensor_tensor(ln.state[:, lo + 1:hi + 1, :], src, by, ALU.mult)
                ins.then_inc(ln.u_used.sem, 1)

            def states(ln, i, link, c):
                if c == 1:
                    dve.wait_ge(ln.u_used.sem, ln.u_used.after(i, 2))
                ins = nc.vector.scalar_tensor_tensor(ln.state[:, c + 1, :], ln.state[:, c, :], ln.ebl[:, c:c + 1],
                                                     ln.state[:, c + 1, :], ALU.mult, ALU.add)
                if c < chunks - 2:
                    link(ins)
                else:
                    ins.then_inc(ln.state_done.sem, 1)

            def head_sums(ln, i, link):
                dve.wait_ge(ln.sq2.sem, ln.sq2.done(i))
                link(nc.vector.tensor_reduce(head_root.tmp[:, ln.q], ln.t2[:].rearrange("p (a v) -> p a v", v=hv), AX.X, ALU.add))
                return nc.vector.tensor_scalar(head_root.v[:, ln.q], head_root.tmp[:, ln.q], 1.0 / hv, rms_eps, ALU.mult, ALU.add)

            def gated(ln, i):
                dve.wait_ge(ln.y_stored.sem, ln.y_stored.before(i, 16))
                t1 = ln.t1[:].rearrange("p t d -> p (t d)").rearrange("p (a v) -> p a v", v=hv)
                y = ln.Y[:].rearrange("p w n -> p (w n)").rearrange("p (a v) -> p a v", v=hv)
                by = head_root.root[:, ln.q].rearrange("p (a o) -> p a o", o=1).to_broadcast([P, TILES * heads, hv])
                nc.vector.tensor_tensor(t1, y, by, ALU.mult).then_inc(ln.o_used.sem, 1)
                dve.wait_ge(ln.o_used.sem, ln.o_used.done(i))
                dve.wait_ge(ln.gs_done.sem, ln.gs_done.done(i))
                nc.vector.tensor_tensor(ln.t1[:], ln.t1[:], ln.gs, ALU.mult).then_inc(ln.on_done.sem, 1)

            def out_low(ln, i):
                dve.wait_ge(ln.ot_high.sem, ln.ot_high.done(i))
                low(nc, ln.hT[1][:], ln.X[:], ln.hT[0][:]).then_inc(ln.ot_ready.sem, 1)

            def add_out(ln, i):
                dve.wait_ge(ln.wo_done.sem, ln.wo_done.done(i))
                nc.vector.tensor_tensor(ln.h0[:], ln.Yt, ln.pre[:], ALU.add).then_inc(ln.x1_done.sem, 1)

            def hidden(ln, i, c):
                dve.wait_ge(ln.sg_done.sem, ln.sg_done.after(i, c + 1))
                if c >= 2:
                    dve.wait_ge(ln.fl_done.sem, ln.fl_done.after(i, c - 1))
                elif c == 0:
                    dve.wait_ge(ln.ht_ready.sem, ln.ht_ready.after(i, 2))
                at = slice((c % 2) * 512, (c % 2 + 1) * 512)
                nc.vector.tensor_tensor(ln.t1[:].rearrange("p t d -> p (t d)")[:, at], ln.t2[:, at], ln.X[:, 1, :], ALU.mult).then_inc(ln.f_done.sem, 1)

            def sum_up(ln, i):
                dve.wait_ge(ln.down_done.sem, ln.down_done.done(i))
                dve.wait_ge(ln.fl_done.sem, ln.fl_done.done(i))
                nc.vector.tensor_tensor(ln.t1[:], ln.Yt, ln.h0[:], ALU.add).then_inc(ln.sum_done.sem, 1)

            front = Front(0)
            front.normalise()
            front.modulate()
            w.split(dve)
            dve.wait_ge(w.ready, w.count("g_down"))
            front.root_norm()
            dve.wait_ge(small_loaded, 80)
            dve.wait_ge(masks_made, 7)
            for ln in lanes:
                nc.vector.memset(ln.state[:, 0, :], 0.0)

            def body(i, more):
                made = [links_of(ln.link, i) for ln in lanes]
                both = [(ln, made[ln.q][0]) for ln in lanes]
                root_link_of, root_count = links_of(root_link, i)
                for ln in lanes:
                    halve(ln, i, 1)
                for ln, link in both:
                    decay_sums(ln, i, link)
                for ln in lanes:
                    decay_queries_keys(ln, i)
                for ln in lanes:
                    masked(ln, i, 0)
                for ln in lanes:
                    own_blocks(ln, i, 0)
                for ln in lanes:
                    masked(ln, i, 1)
                for ln in lanes:
                    own_blocks(ln, i, 1)
                for c in range(1, chunks - 1):
                    for ln, link in both:
                        states(ln, i, link, c)
                for t in range(2, TILES):
                    for ln in lanes:
                        masked(ln, i, t)
                for ln, link in both:
                    ins = head_sums(ln, i, link)
                root_link_of(ins)
                head_root.solve(root_link_of)
                for ln in lanes:
                    gated(ln, i)
                for ln in lanes:
                    out_low(ln, i)
                for ln in lanes:
                    add_out(ln, i)
                for ln in lanes:
                    dve.wait_ge(ln.sq3.sem, ln.sq3.done(i))
                    ins = nc.vector.tensor_scalar(rms2_root.v[:, ln.q], ln.sq[:], 1.0 / D, rms_eps, ALU.mult, ALU.add)
                root_link_of(ins)
                rms2_root.solve(root_link_of)
                for ln in lanes:
                    root_norm(ln, ln.t1, ln.h0, rms2_root, ln.h2_done)
                for ln in lanes:
                    halve(ln, i, 2)
                if more:
                    front = Front(i + 1)
                for c in range(ki):
                    for ln in lanes:
                        hidden(ln, i, c)
                    if more and c == 1:
                        front.normalise()
                    if more and c == 2:
                        front.modulate()
                    if more and c == 3:
                        front.root_norm()
                for ln in lanes:
                    sum_up(ln, i)
                for ln in lanes:
                    assert made[ln.q][1][0] == ln.link.per, made[ln.q][1][0]
                assert root_count[0] == root_link.per, root_count[0]

            rounds(dve, body)
        m.end()


def sparse_ffn_stage(nc, io, keep):
    inner = 1024
    halves = inner // 512
    groups = inner // 4
    ki = inner // P
    with ExitStack() as ctx:
        m = Alloc(nc, ctx, "spf")
        entries = [("sp_gate", KD * inner), ("sp_up", KD * inner), ("sp_down", ki * D)]
        raw = m.sb("raw", [P, sum(n for _, n in entries)])
        w = SplitWeights(nc, m, io, entries, raw)
        silu = m.sb("silu", [P, 2, inner])
        hid = m.sb("hid", [P, TILES, inner])
        mag = m.sb("mag", [P, 2, inner])
        lead = m.sb("lead", [P, 2, 3, 2, groups])
        wins = m.sb("wins", [P, 3, 2, groups], BF16)
        sums = m.sb("sums", [P, 4, groups], BF16)
        margin = m.sb("margin", [P, 4, groups], BF16)
        kept = m.sb("kept", [P, inner])
        keptT = [m.sb(f"keptT{i}", [P, ki, P], F32R) for i in "hl"]
        y = m.sb("y", [P, TILES, D])
        gu = m.ps("gu", [P, 2, 2, 512])
        tp = m.ps("tp", [P, 2, 512])
        o_ps = m.ps("o_ps", [P, TILES, D])
        link_t = m.counted("link_t", 2)
        gu_done = m.counted("gu_done", 2)
        silu_done = m.counted("silu_done", 2)
        hid_done = m.counted("hid_done", 2, credit=2)
        mag_done = m.counted("mag_done", 1)
        looked = m.counted("looked", 1, credit=2)
        compared = m.counted("compared", 1, credit=2)
        kept_done = m.counted("kept_done", 1)
        kt_done = m.counted("kt_done", 2)
        kt_high = m.counted("kt_high", 2)
        kt_low = m.counted("kt_low", 2, credit=2)
        o_done = m.counted("o_done", 1)
        link_y = m.counted("link_y", 1)
        y_done = m.counted("y_done", 1, credit=1)
        y_stored = m.counted("y_stored", 16, credit=16)

        xin = NormedInput(nc, m, io, keep, "x3", 1, CB, SB, tp, lambda pe, b: None)
        block = m.begin()

        @block.sync
        def _(sp):
            sp.sem_inc(xin.normed.sem, xin.normed.credit)
            sp.sem_inc(hid_done.sem, hid_done.credit)
            sp.sem_inc(compared.sem, compared.credit)
            sp.sem_inc(looked.sem, looked.credit)
            sp.sem_inc(kt_low.sem, kt_low.credit)
            sp.sem_inc(y_done.sem, y_done.credit)
            sp.sem_inc(y_stored.sem, y_stored.credit)
            xin.load(sp, 0)
            w.load(sp)

            def body(b, q, first, last):
                if not last:
                    xin.load(sp, b + 1)
                if not first:
                    store(b - 1)
                xin.load_residual(sp, b, GB)

            def store(b):
                wait_apart(sp, y_done.sem, y_done.after(b, 1))
                sp.dma_start(io["out_rows"][bass.ds(b * S, S), :].rearrange("(t p) d -> p t d", p=P), y[:]).then_inc(y_stored.sem, 16)

            in_batches(sp, body)
            store(B - 1)
            sp.wait_ge(y_stored.sem, y_stored.after(B - 1, 16))

        @block.gpsimd
        def _(pool):
            def body(b, q, first, last):
                for t in range(TILES):
                    n = b * TILES + t
                    pool.wait_ge(mag_done.sem, mag_done.after(n, 1))
                    pool.wait_ge(looked.sem, looked.before(n, 1, back=2))
                    s = t % 2
                    a = mag[:, s].rearrange("p (g e) -> p e g", e=4)
                    nc.gpsimd.tensor_tensor(lead[:, s, 0], a[:, 0:4:2, :], a[:, 1:4:2, :], ALU.subtract)
                    nc.gpsimd.tensor_tensor(lead[:, s, 1], a[:, 0:2, :], a[:, 2:4, :], ALU.subtract)
                    nc.gpsimd.tensor_tensor(lead[:, s, 2, 0, :], a[:, 0, :], a[:, 3, :], ALU.subtract)
                    ins = nc.gpsimd.tensor_tensor(lead[:, s, 2, 1, :], a[:, 1, :], a[:, 2, :], ALU.subtract)
                    ins.then_inc(compared.sem, 1)

            in_batches(pool, body)

        @block.tensor
        def _(pe):
            def gate_up(n, t, q, c):
                pe.wait_ge(hid_done.sem, hid_done.before(n, c + 1))
                for g, name in enumerate(("sp_gate", "sp_up")):
                    for k in range(KD):
                        at = slice(t * P, (t + 1) * P)
                        col = k * inner + c * 512
                        mm = products(nc, gu[:, c, g, :], (xin.hT[q][0][:, k, at], xin.hT[q][1][:, k, at]),
                                      w.part(name, col, col + 512), k == 0, k == KD - 1)
                mm.then_inc(gu_done.sem, 1)

            def turn_kept(n):
                pe.wait_ge(kept_done.sem, kept_done.after(n, 1))
                for c in range(2):
                    for j in range(4):
                        at = (c * 4 + j) * P
                        mm = nc.tensor.transpose(tp[:, c, j * P:(j + 1) * P], kept[:, at:at + P], keep["ident"][:])
                    mm.then_inc(kt_done.sem, 1)

            def down(n, t):
                for k in range(ki):
                    if k % 4 == 0:
                        pe.wait_ge(kt_low.sem, kt_low.after(n, k // 4 + 1))
                    mm = products(nc, o_ps[:, t, :], (keptT[0][:, k, :], keptT[1][:, k, :]),
                                  w.part("sp_down", k * D, (k + 1) * D), k == 0, k == ki - 1)
                if t == TILES - 1:
                    mm.then_inc(o_done.sem, 1)

            def body(b, q, first, last):
                for t in range(TILES):
                    n = b * TILES + t
                    if t == 0:
                        pe.wait_ge(xin.ready.sem, xin.ready.after(b, 1))
                    gate_up(n, t, q, 0)
                    if t == 3:
                        pe.wait_ge(y_done.sem, y_done.before(b, 1))
                    if t == 3 or not first:
                        down(n - 3, (t + 1) % TILES)
                    if t == 1 and not last:
                        xin.transpose(pe, b + 1)
                    gate_up(n, t, q, 1)
                    if t == 1 and not last:
                        pe.wait_ge(xin.whole.sem, xin.whole.after(b + 1, 1))
                    if t >= 2 or not first:
                        turn_kept(n - 2)

            xin.transpose(pe, 0)
            pe.wait_ge(w.ready, w.count("sp_down"))
            in_batches(pe, body)
            for n in range(B * TILES, B * TILES + 3):
                down(n - 3, (n - 3) % TILES)
                if n - 2 < B * TILES:
                    turn_kept(n - 2)

        @block.scalar
        def _(act):
            def activate(n, c, t):
                act.wait_ge(gu_done.sem, gu_done.after(n, c + 1))
                nc.scalar.activation(silu[:, t % 2, c * 512:(c + 1) * 512], gu[:, c, 0, :], ACT.Silu).then_inc(silu_done.sem, 1)

            def magnitudes(n, t):
                act.wait_ge(hid_done.sem, hid_done.after(n, 2))
                act.wait_ge(compared.sem, compared.before(n, 1, back=2))
                nc.scalar.activation(mag[:, t % 2], hid[:, t, :], ACT.Abs).then_inc(mag_done.sem, 1)

            def kept_high(n):
                for c in range(2):
                    act.wait_ge(kt_done.sem, kt_done.after(n, c + 1))
                    nc.scalar.activation(keptT[0][:, c * 4:(c + 1) * 4, :], tp[:, c, :].rearrange("p (j n) -> p j n", j=4),
                                         ACT.Copy).then_inc(kt_high.sem, 1)

            def body(b, q, first, last):
                for t in range(TILES):
                    n = b * TILES + t
                    activate(n, 0, t)
                    if t == 1 and not last:
                        xin.modulate(act, b + 1)
                    activate(n, 1, t)
                    if t >= 2 or not first:
                        kept_high(n - 2)
                    magnitudes(n, t)

            xin.modulate(act, 0)
            in_batches(act, body)
            for n in range(B * TILES - 2, B * TILES):
                kept_high(n)

        @block.vector
        def _(dve):
            def hidden(n, c, t):
                dve.wait_ge(silu_done.sem, silu_done.after(n, c + 1))
                at = slice(c * 512, (c + 1) * 512)
                nc.vector.tensor_tensor(hid[:, t, at], silu[:, t % 2, at], gu[:, c, 1, :], ALU.mult).then_inc(hid_done.sem, 1)

            def kept_low(n):
                for c in range(2):
                    dve.wait_ge(kt_high.sem, kt_high.after(n, c + 1))
                    at = slice(c * 4, (c + 1) * 4)
                    low(nc, keptT[1][:, at, :], tp[:, c, :].rearrange("p (j n) -> p j n", j=4), keptT[0][:, at, :]).then_inc(kt_low.sem, 1)

            def choose(n, t):
                dve.wait_ge(compared.sem, compared.after(n, 1))
                nc.vector.tensor_scalar(wins[:], lead[:, t % 2], 0.0, None, ALU.is_ge).then_inc(looked.sem, 1)
                dve.wait_ge(looked.sem, looked.after(n, 1))
                x, y_, z = (wins[:, i] for i in range(3))
                nc.vector.tensor_tensor(sums[:, 0:2, :], y_, z, ALU.add)
                nc.vector.tensor_tensor(sums[:, 2, :], y_[:, 0, :], z[:, 1, :], ALU.add)
                nc.vector.scalar_tensor_tensor(sums[:, 3, :], y_[:, 1, :], -1.0, z[:, 0, :], ALU.mult, ALU.subtract).then_inc(link_t.sem, 1)
                dve.wait_ge(link_t.sem, link_t.after(n, 1))
                nc.vector.scalar_tensor_tensor(margin[:, 0, :], sums[:, 0, :], -2.0, x[:, 0, :], ALU.add, ALU.add)
                nc.vector.scalar_tensor_tensor(margin[:, 1, :], sums[:, 1, :], -1.0, x[:, 0, :], ALU.add, ALU.subtract)
                nc.vector.tensor_tensor(margin[:, 2, :], x[:, 1, :], sums[:, 2, :], ALU.subtract)
                nc.vector.scalar_tensor_tensor(margin[:, 3, :], sums[:, 3, :], 1.0, x[:, 1, :], ALU.add, ALU.subtract).then_inc(link_t.sem, 1)
                dve.wait_ge(link_t.sem, link_t.after(n, 2))
                nc.vector.scalar_tensor_tensor(kept[:].rearrange("p (g e) -> p e g", e=4), margin[:], 0.0,
                                               hid[:, t, :].rearrange("p (g e) -> p e g", e=4), ALU.is_ge, ALU.mult).then_inc(kept_done.sem, 1)

            def residual(b):
                dve.wait_ge(o_done.sem, o_done.after(b, 1))
                dve.wait_ge(xin.residual_loaded.sem, xin.residual_loaded.after(b, 32))
                dve.wait_ge(y_stored.sem, y_stored.before(b, 16))
                rows = xin.gate_row[:].to_broadcast([P, TILES, D])
                nc.vector.tensor_tensor(y[:], o_ps[:], rows, ALU.mult).then_inc(link_y.sem, 1)
                dve.wait_ge(link_y.sem, link_y.after(b, 1))
                nc.vector.tensor_tensor(y[:], y[:], xin.residual[:], ALU.add).then_inc(y_done.sem, 1)

            def body(b, q, first, last):
                for t in range(TILES):
                    n = b * TILES + t
                    hidden(n, 0, t)
                    if t >= 2 or not first:
                        choose(n - 2, (t + 2) % TILES)
                    hidden(n, 1, t)
                    if t >= 2 or not first:
                        kept_low(n - 2)
                    if t == 0 and not last:
                        xin.norm(dve, b + 1)
                    if t == 1 and not last:
                        xin.halve(dve, b + 1, 1 - q)
                    if t == 2 and not first:
                        residual(b - 1)

            xin.norm(dve, 0)
            xin.halve(dve, 0, 0)
            w.split(dve)
            in_batches(dve, body)
            for n in range(B * TILES - 2, B * TILES):
                choose(n, n % TILES)
                kept_low(n)
            residual(B - 1)
        m.end()


def build(nc, io, stages="full"):
    with ExitStack() as ctx:
        k = Alloc(nc, ctx, "keep")
        keep = {"ident": k.sb("ident", [P, P]), "causal": k.sb("causal", [P, S]),
                "mod": k.sb("mod", [P, 2, MODS * KD, B])}
        Apart.passed = k.sem("passed")
        keep["raw_loaded"] = [k.counted(f"raw_loaded{n}", 16) for n in range(4)]
        modulation_stage(nc, io, keep)
        if stages in ("full", "a"):
            attention_stage(nc, io, keep)
        if stages in ("full", "b"):
            moe_stage(nc, io, keep)
        if stages in ("full", "c"):
            gla_stage(nc, io, keep)
        if stages in ("full", "d"):
            sparse_ffn_stage(nc, io, keep)


def layout(i):
    import numpy as np
    f = {}
    f["x"] = i["L0_attn_x"].reshape(B * S, D)

    def feature_major(w):
        return w.reshape(NH, DH, KD, P).transpose(3, 0, 2, 1).reshape(P, NH, KD * DH)

    f["wqk"] = np.stack([feature_major(i["L0_attn_W_Q"]), feature_major(i["L0_attn_W_K"])], axis=2)
    f["wv"] = i["L0_attn_W_V"].reshape(PAIRS, 2, DH, KD, P).transpose(4, 0, 3, 1, 2).reshape(P, PAIRS, KD * 2 * DH)
    f["wo"] = i["L0_attn_W_O"].transpose(2, 0, 1).reshape(P, PAIRS, 2 * D)
    for l in range(2):
        f[f"c{l}"] = i[f"L{l}_c"].T.reshape(KD, P, B).transpose(1, 0, 2).reshape(P, KD * B)
        f[f"wmod{l}"] = i[f"L{l}_wmod"]

    def rows(w):
        return w.reshape(-1, P, w.shape[1]).transpose(1, 0, 2).reshape(P, -1)

    for n in ("gate", "up", "down"):
        f[f"sp_{n}"] = rows(i[f"L1_ffn_w_{n}"])
        f[f"ex_{n}"] = rows(i[f"L0_ffn_w_{n}"])
        f[f"sh_{n}"] = rows(i[f"L0_ffn_shared_w_{n}"])
    f["g_q"], f["g_k"], f["g_o"] = (rows(i[f"L1_attn_w{n}"]) for n in "qko")
    f["g_vg"] = rows(np.concatenate([i["L1_attn_wv"], i["L1_attn_wg"]], axis=1))
    wide = 768
    for n in ("gate", "up"):
        f[f"g_{n}"] = rows(np.pad(i[f"L1_attn_w_{n}"], ((0, 0), (0, wide - 704))))
    f["g_down"] = rows(np.pad(i["L1_attn_w_down"], ((0, wide - 704), (0, 0))))
    f["gk_w1"] = rows(i["L1_attn_gk_w1"]).reshape(P, KD, 16)
    f["gk_w2"] = i["L1_attn_gk_w2"]
    f["gk_b"] = i["L1_attn_gk_b"].reshape(P, 1)
    f["norm_cols"] = np.stack([i["L1_attn_norm1_w"].reshape(KD, P).T, i["L1_attn_ffn_norm_w"].reshape(KD, P).T], axis=1)
    f["gnorm"] = i["L1_attn_gnorm_w"].reshape(1, 32)
    f["router"] = rows(i["L0_ffn_w_router"])
    f["amplitudes"] = i["L0_ffn_amplitudes"]
    f["expert_scale"] = i["L0_ffn_expert_scale"].reshape(P, 1)
    return {n: np.ascontiguousarray(a) for n, a in f.items()}


def declare(nc, arrays):
    io = {n: nc.dram_tensor(f"in_{n}_dram", a.shape, F32, kind="ExternalInput").ap() for n, a in arrays.items()}
    for n in ("x1", "x2", "x3"):
        io[n] = nc.dram_tensor(n, (B * S, D), F32, kind="Internal").ap()
    io["mod_rows"] = nc.dram_tensor("scratch_mod_rows", (2, B, MODS * D), F32, kind="Internal").ap()
    io["out"] = nc.dram_tensor("out_0_dram", (B, S, D), F32, kind="ExternalOutput").ap()
    io["out_rows"] = io["out"].rearrange("b s d -> (b s) d")
    return io, ["out_0_dram"]


def kernel(**inputs):
    import numpy as np
    import concourse.bacc as bacc
    from concourse.bass_utils import run_bass_kernel_spmd

    nc = bacc.Bacc("TRN2", target_bir_lowering=False, num_devices=1)
    arrays = layout({n: np.asarray(a) for n, a in inputs.items()})
    io, outs = declare(nc, arrays)
    build(nc, io)
    r = run_bass_kernel_spmd(nc, [{f"in_{n}_dram": a for n, a in arrays.items()}], core_ids=[0])
    return r.results[0][outs[0]]
```

```python
from contextlib import ExitStack

import concourse.bass as bass
from concourse import mybir

ALU = mybir.AluOpType
ACT = mybir.ActivationFunctionType
AX = mybir.AxisListType
F32 = mybir.dt.float32
F32R = mybir.dt.float32r
BF16 = mybir.dt.bfloat16
I32 = mybir.dt.int32

P = 128
B, S, D = 8, 512, 256
TILES = S // P
KD = D // P
NH, DH = 16, 128
PAIRS = NH // 2
LN_EPS = 1e-5
MODS = 6
SA, CA, GA, SB, CB, GB = range(MODS)
MASKED = -1.0e30
ROOT_MAGIC = 1597463007.0


class Signal:

    def __init__(self, sem, per, credit=0):
        self.sem, self.per, self.credit = sem, per, credit

    def done(self, r):
        return self.after(r, self.per)

    def after(self, r, k):
        return r * self.per + (self.credit + k)

    def before(self, r, k, back=1):
        return r * self.per + (self.credit + k - back * self.per)


def wait_on(eng, sem, value):
    eng.wait_ge(sem, value)


class Apart:
    passed = None


def wait_apart(eng, sem, value):
    eng.wait_ge(sem, value)
    eng.sem_inc(Apart.passed, 1)


def products(nc, out, still, moving, start, stop, **kw):
    nc.tensor.matmul(out, still[0], moving[0], start=start, stop=False, **kw)
    nc.tensor.matmul(out, still[0], moving[1], start=False, stop=False, **kw)
    return nc.tensor.matmul(out, still[1], moving[0], start=False, stop=stop, **kw)


def low(nc, out, whole, high):
    return nc.vector.tensor_tensor(out, whole, high.bitcast(F32), ALU.subtract)


class Alloc:
    def __init__(self, nc, ctx, prefix):
        self.nc, self.ctx, self.prefix, self.sems = nc, ctx, prefix, []

    def sb(self, name, shape, dt=F32):
        return self.ctx.enter_context(self.nc.sbuf_tensor(f"{self.prefix}_{name}", shape, dt))

    def ps(self, name, shape, dt=F32):
        return self.ctx.enter_context(self.nc.psum_tensor(f"{self.prefix}_{name}", shape, dt))

    def sem(self, name):
        self.sems.append(self.ctx.enter_context(self.nc.semaphore(f"{self.prefix}_{name}")))
        return self.sems[-1]

    def begin(self):
        self.body = ExitStack()
        return self.body.enter_context(self.nc.Block())

    def end(self):
        self.body.close()
        with self.nc.Block() as block:
            @block.sync
            def _(sp):
                for s in self.sems:
                    sp.sem_clear(s)

    def counted(self, name, per, credit=0):
        return Signal(self.sem(name), per, credit)


def modulation_stage(nc, io, keep):
    with ExitStack() as ctx:
        m = Alloc(nc, ctx, "mod")
        c_in = m.sb("c_in", [P, 2, KD, B])
        c_act = m.sb("c_act", [P, 2, KD, B])
        wmod = m.sb("wmod", [P, 2, KD, MODS * D])
        rows = m.sb("rows", [B, 2, MODS * D])
        gates = m.sb("gates", [B, 2, 2, D])
        signs = m.sb("signs", [B, 2, 2, D])
        col_banks = m.ps("col_ps", [P, 2, 512])
        col_ps = [col_banks[:, l, 0:MODS * KD * B].rearrange("p (n b) -> p n b", b=B) for l in range(2)]
        row_ps = m.ps("row_ps", [B, 2, MODS * D])
        pieces = [slice(n, n + 512) for n in range(0, MODS * D, 512)]
        c_loaded = m.sem("c_loaded")
        w_loaded = [[m.sem(f"w_loaded{l}{n}") for n in range(len(pieces))] for l in range(2)]
        zeroed = m.sem("zeroed")
        consts_made = m.sem("consts_made")
        c_ready = m.sem("c_ready")
        cols_done = m.sem("cols_done")
        rows_done = m.sem("rows_done")
        rows_copied = m.sem("rows_copied")
        chain = m.sem("chain")
        rows_final = m.sem("rows_final")
        stored = m.sem("stored")
        block = m.begin()

        @block.sync
        def _(sp):
            for l in range(2):
                sp.dma_start(c_in[:, l], io[f"c{l}"].rearrange("p (k b) -> p k b", k=KD)).then_inc(c_loaded, 16)
            for l in range(2):
                for at, sem in zip(pieces, w_loaded[l]):
                    sp.dma_start(wmod[:, l, :, at], io[f"wmod{l}"][:, at].rearrange("(k p) n -> p k n", p=P)).then_inc(sem, 16)
            for l in range(2):
                sp.wait_ge(rows_final, l + 1)
                sp.dma_start(io["mod_rows"][l], rows[:, l]).then_inc(stored, 16)
            sp.wait_ge(stored, 32)

        @block.gpsimd
        def _(pool):
            nc.gpsimd.memset(keep["ident"][:], 0.0).then_inc(zeroed, 1)
            nc.gpsimd.memset(keep["causal"][:], 0.0).then_inc(zeroed, 1)
            pool.wait_ge(zeroed, 2)
            nc.gpsimd.affine_select(out=keep["ident"][:], in_=keep["ident"][:], compare_op=ALU.not_equal, fill=1.0,
                                    base=0, pattern=[[-1, P]], channel_multiplier=1).then_inc(consts_made, 1)
            last = keep["causal"][:, S - P:S]
            nc.gpsimd.affine_select(out=last, in_=last, compare_op=ALU.is_ge, fill=MASKED,
                                    base=0, pattern=[[-1, P]], channel_multiplier=1).then_inc(consts_made, 1)

        @block.scalar
        def _(act):
            act.wait_ge(c_loaded, 32)
            nc.scalar.activation(c_act[:], c_in[:], ACT.Silu).then_inc(c_ready, 1)

        @block.tensor
        def _(pe):
            pe.wait_ge(c_ready, 1)
            for l in range(2):
                for at, sem in zip(pieces, w_loaded[l]):
                    pe.wait_ge(sem, 16)
                    for k in range(KD):
                        mm = nc.tensor.matmul(row_ps[:, l, at], c_act[:, l, k, :], wmod[:, l, k, at],
                                              start=(k == 0), stop=(k == KD - 1))
                mm.then_inc(rows_done, 1)
            pe.wait_ge(consts_made, 2)
            for l in range(2):
                pe.wait_ge(rows_final, l + 1)
                for n in (SA, CA, SB, CB):
                    for k in range(KD):
                        at = slice(n * D + k * P, n * D + (k + 1) * P)
                        mm = nc.tensor.transpose(col_ps[l][:, n * KD + k, :], rows[:, l, at], keep["ident"][0:B, 0:B])
                mm.then_inc(cols_done, 1)

        @block.vector
        def _(dve):
            for l in range(2):
                dve.wait_ge(rows_done, l + 1)
                nc.vector.tensor_copy(rows[:, l], row_ps[:, l]).then_inc(rows_copied, 1)
                dve.wait_ge(rows_copied, l + 1)
                g = rows[:, l].rearrange("b (h m d) -> b h m d", h=2, m=3)
                nc.vector.tensor_scalar(signs[:, l], g[:, :, 2, :], 0.0, 2.0, ALU.is_ge, ALU.mult)
                nc.vector.scalar_tensor_tensor(gates[:, l], g[:, :, 2, :], -1.0, g[:, :, 2, :], ALU.mult, ALU.max)
                nc.vector.tensor_scalar(g[:, :, 1, :], g[:, :, 1, :], 1.0, None, ALU.add).then_inc(chain, 1)
                dve.wait_ge(chain, 2 * l + 1)
                nc.vector.tensor_scalar(gates[:, l], gates[:, l], 0.25, None, ALU.max).then_inc(chain, 1)
                dve.wait_ge(chain, 2 * l + 2)
                nc.vector.scalar_tensor_tensor(g[:, :, 2, :], signs[:, l], -1.0, gates[:, l], ALU.add, ALU.mult).then_inc(rows_final, 1)
            for l in range(2):
                dve.wait_ge(cols_done, l + 1)
                for n in (SA, SB):
                    at = slice(n * KD, (n + 2) * KD)
                    nc.vector.tensor_copy(keep["mod"][:, l, at, :], col_ps[l][:, at, :])
        m.end()


def moments_of_rows(nc, link, x, stats, mv, var_eps):
    for t in range(TILES):
        last = nc.vector.bn_stats(stats[:, t, :], x[:, t, :])
    link(last, wait_apart)
    for t in range(TILES):
        last = nc.vector.bn_aggr(mv[:, t, :], stats[:, t, :])
    link(last)
    return nc.vector.tensor_scalar(var_eps[:], mv[:, :, 1], LN_EPS, None, ALU.add)


def refine_root(nc, link, var_eps, tmp, rstd):
    link(nc.vector.tensor_tensor(tmp[:], rstd[:], rstd[:], ALU.mult))
    link(nc.vector.scalar_tensor_tensor(tmp[:], tmp[:], -0.5, var_eps[:], ALU.mult, ALU.mult))
    link(nc.vector.scalar_tensor_tensor(rstd[:], tmp[:], 1.5, rstd[:], ALU.add, ALU.mult))


def root_by_halving(nc, link, var_eps, tmp, rstd):
    link(nc.vector.tensor_scalar(rstd[:].bitcast(I32), var_eps[:].bitcast(I32), -0.5, ROOT_MAGIC, ALU.mult, ALU.add))
    for _ in range(3):
        refine_root(nc, link, var_eps, tmp, rstd)


def norm_rows(nc, x, xn, mv, rstd):
    for t in range(TILES):
        last = nc.vector.tensor_scalar(xn[:, t, :], x[:, t, :], mv[:, t, 0:1], rstd[:, t:t + 1],
                                       ALU.subtract, ALU.mult)
    return last


def transpose_rows(nc, out, xn, ident):
    for k in range(KD):
        for t in range(TILES):
            mm = nc.tensor.transpose(out[:, k, t * P:(t + 1) * P], xn[:, t, k * P:(k + 1) * P], ident[:])
    return mm


def attention_stage(nc, io, keep):
    scale = DH ** -0.5
    off = [P * (i * (i + 1) // 2) for i in range(TILES + 1)]
    pt_off = [0, 512, 896, 1152]
    pt_bank = [(0, 0), (1, 0), (2, 0), (2, 256)]
    pt_groups = [(0, 0, 512), (1, 512, 896), (2, 896, 1280)]
    s_place = [(0, 0), (0, P), (1, 0), (2, 0)]
    ident = keep["ident"]
    with ExitStack() as ctx:
        m = Alloc(nc, ctx, "att")
        w_qk = m.sb("w_qk", [P, NH, 4, KD * P], F32R)
        w_v = [m.sb(f"w_v{i}", [P, PAIRS, KD, 2 * DH], F32R) for i in "hl"]
        w_o = [m.sb(f"w_o{i}", [P, NH, D], F32R) for i in "hl"]
        raw = m.sb("raw", [P, 4, 512])
        staged = m.sb("staged", [P, 2, 4, KD * P], F32R)
        x_in = m.sb("x_in", [P, TILES, D])
        x_res = m.sb("x_res", [P, TILES, D])
        whole_hT = m.sb("whole_hT", [P, KD, S])
        gate = m.sb("gate", [P, D])
        hT = [m.sb(f"hT{i}", [P, KD, S], F32R) for i in "hl"]
        qkT = [m.sb(f"qkT{i}", [P, 2, S], F32R) for i in "hl"]
        v = [m.sb(f"v{i}", [P, TILES, 2 * DH], F32R) for i in "hl"]
        probs = m.sb("probs", [P, off[TILES]])
        probs_t = [m.sb(f"probs_t{i}", [P, off[TILES]], F32R) for i in "hl"]
        zT = [m.sb(f"zT{i}", [P, S], F32R) for i in "hl"]
        stats = m.sb("stats", [P, TILES, 6])
        mv = m.sb("mv", [P, TILES, 2])
        rstd = m.sb("rstd", [P, TILES])
        var_eps = m.sb("var_eps", [P, TILES])
        root_tmp = m.sb("root_tmp", [P, TILES])
        neg_top = m.sb("neg_top", [P, TILES])
        total = m.sb("total", [P, TILES])
        inv_total = m.sb("inv_total", [P, TILES])
        proj = m.ps("proj", [P, 2, 512])
        work = m.ps("work", [P, 3, 512])
        z_ps = m.ps("z_ps", [P, 512])
        o_ps = m.ps("o_ps", [P, TILES, D])

        x_loaded = m.counted("x_loaded", 16)
        res_loaded = m.counted("res_loaded", 32)
        raw_loaded = keep["raw_loaded"]
        w_high = m.counted("w_high", 4)
        w_split = m.counted("w_split", 4)
        stage_loaded = [m.counted(f"stage_loaded{a}", 16) for a in range(2)]
        link_n = m.counted("link_n", 13)
        o_used = m.counted("o_used", 1)
        link_h = m.counted("link_h", 1)
        ln_done = m.counted("ln_done", 1)
        ht_in_psum = m.counted("ht_in_psum", KD)
        ht_whole = m.counted("ht_whole", KD)
        ht_high = m.counted("ht_high", KD)
        ht_ready = m.counted("ht_ready", KD)
        qk_done = m.counted("qk_done", 2, credit=4)
        qk_high = m.counted("qk_high", 2)
        qk_low = m.counted("qk_low", 2)
        v_done = m.counted("v_done", 2)
        v_high = m.counted("v_high", 2)
        v_low = m.counted("v_low", 2)
        s_done = m.counted("s_done", 3)
        top_ready = m.counted("top_ready", TILES)
        exp_done = m.counted("exp_done", TILES)
        probs_ready = m.counted("probs_ready", 1)
        pt_done = m.counted("pt_done", 3)
        pt_high = m.counted("pt_high", 3)
        pt_low = m.counted("pt_low", 3, credit=3)
        z_done = m.counted("z_done", 1)
        z_high = m.counted("z_high", 1)
        z_low = m.counted("z_low", 1)
        o_done = m.counted("o_done", 1)
        y_done = m.counted("y_done", 1, credit=1)
        y_stored = m.counted("y_stored", 16, credit=16)
        y = raw[:, 0:2, :].rearrange("p w (t d) -> p (w t) d", t=2)
        block = m.begin()

        def batches(eng, batch):
            batch(0, True)
            with eng.Fori(1, B - 1) as b:
                batch(b, True)
            batch(B - 1, False)

        def pairs(eng, pair, b, more):
            pair(b, 0, "first")
            with eng.Fori(1, PAIRS - 1) as p:
                pair(b, p, "middle")
            pair(b, PAIRS - 1, "next" if more else "last")

        @block.sync
        def _(sp):
            for signal in (qk_done, pt_low, y_done, y_stored):
                sp.sem_inc(signal.sem, signal.credit)

            def stage_weights(b, p):
                for a in range(2):
                    g = b * NH + p * 2 + a
                    wait_apart(sp, w_split.sem, w_split.after(p, 2))
                    wait_apart(sp, qk_done.sem, qk_done.before(g, 2, back=2))
                    sp.dma_start(staged[:, a].bitcast(F32), w_qk[:, bass.ds(p * 2 + a, 1)].rearrange("p o m n -> p (o m) n").bitcast(F32)).then_inc(stage_loaded[a].sem, 16)

            def tokens(ap, b):
                return ap[bass.ds(b * S, S), :].rearrange("(t p) d -> p t d", p=P)

            def batch(b, first, last):
                stage_weights(b, 0)
                stage_weights(b, 1)
                if not first:
                    wait_apart(sp, y_done.sem, y_done.before(b, 1))
                    sp.dma_start(tokens(io["x1"], b - 1), y).then_inc(y_stored.sem, 16)
                sp.dma_start(x_res[:], tokens(io["x"], b)).then_inc(res_loaded.sem, 16)
                sp.dma_start(gate[:], io["mod_rows"][0, bass.ds(b, 1), GA * D:(GA + 1) * D].to_broadcast([P, D])).then_inc(res_loaded.sem, 16)
                if not last:
                    wait_apart(sp, ht_in_psum.sem, ht_in_psum.done(b))
                    sp.dma_start(x_in[:], tokens(io["x"], b + 1)).then_inc(x_loaded.sem, 16)
                with sp.Fori(2, PAIRS) as p:
                    stage_weights(b, p)

            sp.dma_start(x_in[:], tokens(io["x"], 0)).then_inc(x_loaded.sem, 16)
            batch(0, True, False)
            with sp.Fori(1, B - 1) as b:
                batch(b, False, False)
            batch(B - 1, False, True)
            sp.wait_ge(y_done.sem, y_done.done(B - 1))
            sp.dma_start(tokens(io["x1"], B - 1), y).then_inc(y_stored.sem, 16)
            sp.wait_ge(y_stored.sem, y_stored.done(B - 1))

        @block.gpsimd
        def _(pool):
            def fetch(n, p):
                if n < 2:
                    src = io["wqk"][:, bass.ds(p * 2, 2), n, :]
                    dst = raw[:, n].rearrange("p (h n) -> p h n", h=2)
                elif n == 2:
                    src, dst = io["wv"][:, bass.ds(p, 1), :].rearrange("p o n -> p (o n)"), raw[:, n]
                else:
                    src, dst = io["wo"][:, bass.ds(p, 1), :].rearrange("p o n -> p (o n)"), raw[:, n]
                pool.dma_start(dst, src).then_inc(raw_loaded[n].sem, 16)

            def place(n, p, half):
                if n < 2:
                    return w_qk[:, bass.ds(p * 2, 2), 2 * n + half, :], raw[:, n].rearrange("p (h n) -> p h n", h=2)
                if n == 2:
                    return w_v[half][:, bass.ds(p, 1)].rearrange("p o k n -> p (o k n)"), raw[:, n]
                return w_o[half][:, bass.ds(p * 2, 2)].rearrange("p h n -> p (h n)"), raw[:, n]

            def split(p, more):
                for n in range(4):
                    pool.wait_ge(raw_loaded[n].sem, raw_loaded[n].after(p, 16))
                    dst, src = place(n, p, 0)
                    nc.gpsimd.tensor_copy(dst, src).then_inc(w_high.sem, 1)
                    pool.wait_ge(w_high.sem, w_high.after(p, n + 1))
                    dst, src = place(n, p, 1)
                    nc.gpsimd.tensor_tensor(dst, src, place(n, p, 0)[0].bitcast(F32), ALU.subtract).then_inc(w_split.sem, 1)
                    if more:
                        wait_apart(pool, w_split.sem, w_split.after(p, n + 1))
                        fetch(n, p + 1)

            for n in range(4):
                fetch(n, 0)
            with pool.Fori(0, PAIRS - 1) as p:
                split(p, True)
            split(PAIRS - 1, False)

        @block.tensor
        def _(pe):
            def transpose_x():
                for k in range(KD):
                    for t in range(TILES):
                        mm = nc.tensor.transpose(proj[:, k, t * P:(t + 1) * P], x_in[:, t, k * P:(k + 1) * P], ident[:])
                    mm.then_inc(ht_in_psum.sem, 1)

            def project_qk(r, a, v_before=None):
                pe.wait_ge(stage_loaded[a].sem, stage_loaded[a].after(r, 16))
                for w in range(2):
                    if v_before is not None:
                        pe.wait_ge(v_low.sem, v_low.after(v_before, w + 1))
                    for k in range(KD):
                        at = slice(k * P, (k + 1) * P)
                        mm = products(nc, proj[:, w, :], (staged[:, a, 2 * w, at], staged[:, a, 2 * w + 1, at]),
                                      (hT[0][:, k, :], hT[1][:, k, :]), k == 0, k == KD - 1)
                    mm.then_inc(qk_done.sem, 1)

            def project_v(r, p, first):
                pe.wait_ge(w_split.sem, w_split.after(p, 4))
                for t in range(TILES):
                    if t % 2 == 0 and not first:
                        pe.wait_ge(qk_low.sem, qk_low.after(r * 2 + 1, t // 2 + 1))
                    for k in range(KD):
                        at = slice(t * P, (t + 1) * P)
                        mv_ = tuple(w_v[i][:, bass.ds(p, 1), k, :].rearrange("p o n -> p (o n)") for i in range(2))
                        mm = products(nc, proj[:, t // 2, (t % 2) * D:(t % 2 + 1) * D],
                                      (hT[0][:, k, at], hT[1][:, k, at]), mv_, k == 0, k == KD - 1)
                    if t % 2:
                        mm.then_inc(v_done.sem, 1)

            def scores(g):
                pe.wait_ge(qk_low.sem, qk_low.after(g, 2))
                for i in range(TILES):
                    bank, col = s_place[i]
                    if i != 1:
                        pe.wait_ge(pt_low.sem, pt_low.before(g, bank + 1))
                    at = slice(i * P, (i + 1) * P)
                    keys = slice(0, (i + 1) * P)
                    mm = products(nc, work[:, bank, col:col + (i + 1) * P], (qkT[0][:, 0, at], qkT[1][:, 0, at]),
                                  (qkT[0][:, 1, keys], qkT[1][:, 1, keys]), True, True)
                    if i:
                        mm.then_inc(s_done.sem, 1)

            def transpose_probs(g):
                pe.wait_ge(probs_ready.sem, probs_ready.after(g, 1))
                for j in range(TILES):
                    bank, col = pt_bank[j]
                    for i in range(j, TILES):
                        c = col + (i - j) * P
                        mm = nc.tensor.transpose(work[:, bank, c:c + P], probs[:, off[i] + j * P:off[i] + (j + 1) * P], ident[:])
                    if j != 2:
                        mm.then_inc(pt_done.sem, 1)

            def times_v(g, r, a):
                pe.wait_ge(v_low.sem, v_low.after(r, 2))
                pe.wait_ge(pt_low.sem, pt_low.after(g, 3))
                for j in range(TILES):
                    at = slice(pt_off[j], pt_off[j] + S - j * P)
                    head = slice(a * DH, (a + 1) * DH)
                    mm = products(nc, z_ps[:, j * P:S], (v[0][:, j, head], v[1][:, j, head]),
                                  (probs_t[0][:, at], probs_t[1][:, at]), j == 0, j == TILES - 1, skip_group_check=True)
                mm.then_inc(z_done.sem, 1)

            def project_out(g, h, first):
                pe.wait_ge(z_low.sem, z_low.after(g, 1))
                for t in range(TILES):
                    at = slice(t * P, (t + 1) * P)
                    for c, (i, j) in enumerate(((0, 0), (0, 1), (1, 0))):
                        mm = nc.tensor.matmul(o_ps[:, t, :], zT[i][:, at], w_o[j][:, bass.ds(h, 1), :].rearrange("p o n -> p (o n)"),
                                              start=(first and t % 2 == 0 and c == 0), stop=True, skip_group_check=True)
                return mm

            def pair(b, p, place):
                r = b * PAIRS + p
                first = place == "first"
                start = first and isinstance(b, int) and b == 0
                for a in range(2):
                    g = r * 2 + a
                    scores(g)
                    if a == 0:
                        if start:
                            project_v(r, p, True)
                        project_qk(r, 1, r if start else None)
                    elif place == "next":
                        pe.wait_ge(ln_done.sem, ln_done.after(b + 1, 1))
                        pe.wait_ge(v_low.sem, v_low.after(r, 2))
                        transpose_x()
                    elif place != "last":
                        project_qk(r + 1, 0, r)
                    if not (start and a == 0):
                        times_v(g - 1, r - 1 + a, 1 - a)
                    transpose_probs(g)
                    if a == 0 and not start:
                        project_v(r, p, False)
                    if first and a == 0 and not start:
                        project_out(g - 1, NH - 1, False).then_inc(o_done.sem, 1)
                    elif first and a == 1:
                        if not (isinstance(b, int) and b == 0):
                            pe.wait_ge(o_used.sem, o_used.after(b - 1, 1))
                        project_out(g - 1, 0, True)
                    elif not start:
                        project_out(g - 1, p * 2 + a - 1, False)

            def batch(b, more):
                pairs(pe, pair, b, more)
                if more:
                    pe.wait_ge(ht_ready.sem, ht_ready.done(b + 1))
                    project_qk((b + 1) * PAIRS, 0)
                else:
                    times_v(b * NH + NH - 1, b * PAIRS + PAIRS - 1, 1)
                    project_out(b * NH + NH - 1, NH - 1, False).then_inc(o_done.sem, 1)

            pe.wait_ge(ln_done.sem, ln_done.after(0, 1))
            transpose_x()
            pe.wait_ge(ht_ready.sem, ht_ready.done(0))
            project_qk(0, 0)
            batches(pe, batch)

        @block.scalar
        def _(act):
            def modulate(b):
                for k in range(KD):
                    mod = [keep["mod"][:, 0, n * KD + k, bass.ds(b, 1)] for n in (CA, SA)]
                    act.wait_ge(ht_in_psum.sem, ht_in_psum.after(b, k + 1))
                    nc.scalar.activation(whole_hT[:, k, :], proj[:, k, :], ACT.Identity, bias=mod[1], scale=mod[0]).then_inc(ht_whole.sem, 1)

            def qk_halves(g):
                for w in range(2):
                    act.wait_ge(qk_done.sem, qk_done.after(g, w + 1))
                    nc.scalar.activation(qkT[0][:, w], proj[:, w], ACT.Copy).then_inc(qk_high.sem, 1)

            def v_halves(r):
                for w in range(2):
                    act.wait_ge(v_done.sem, v_done.after(r, w + 1))
                    nc.scalar.activation(v[0][:, 2 * w:2 * w + 2], proj[:, w].rearrange("p (t n) -> p t n", t=2), ACT.Copy).then_inc(v_high.sem, 1)

            def z_halves(g):
                act.wait_ge(z_done.sem, z_done.after(g, 1))
                nc.scalar.activation(zT[0][:], z_ps[:], ACT.Copy).then_inc(z_high.sem, 1)

            def pair(b, p, place):
                r = b * PAIRS + p
                start = place == "first" and isinstance(b, int) and b == 0
                for a in range(2):
                    g = r * 2 + a
                    for i in range(TILES):
                        act.wait_ge(top_ready.sem, top_ready.after(g, i + 1))
                        row = probs[:, off[i]:off[i + 1]]
                        nc.scalar.activation(row, row, ACT.Exp, bias=neg_top[:, i:i + 1], scale=-1.0,
                                             accum_out=total[:, i:i + 1]).then_inc(exp_done.sem, 1)
                    if start and a == 0:
                        v_halves(r)
                    if not (place in ("next", "last") and a == 1):
                        qk_halves(g + 1)
                    if not (start and a == 0):
                        z_halves(g - 1)
                    if place == "next" and a == 1:
                        modulate(b + 1)
                    for n, (bank, lo, hi) in enumerate(pt_groups):
                        act.wait_ge(pt_done.sem, pt_done.after(g, n + 1))
                        nc.scalar.activation(probs_t[0][:, lo:hi], work[:, bank, 0:hi - lo], ACT.Copy).then_inc(pt_high.sem, 1)
                    if a == 0 and not start:
                        v_halves(r)

            def batch(b, more):
                pairs(act, pair, b, more)
                if more:
                    qk_halves((b + 1) * NH)
                else:
                    z_halves(b * NH + NH - 1)

            modulate(0)
            qk_halves(0)
            batches(act, batch)

        @block.vector
        def _(dve):
            moments_links = 3

            def linker(b, passed):
                count = [passed]

                def link(ins, wait=wait_on):
                    count[0] += 1
                    ins.then_inc(link_n.sem, 1)
                    wait(dve, link_n.sem, link_n.after(b, count[0]))
                return link, count

            def moments(b):
                link, count = linker(b, 0)
                dve.wait_ge(x_loaded.sem, x_loaded.after(b, 16))
                moments_of_rows(nc, link, x_in, stats, mv, var_eps).then_inc(link_n.sem, 1)
                assert count[0] == moments_links - 1, count[0]

            def normalise(b):
                link, count = linker(b, moments_links)
                dve.wait_ge(link_n.sem, link_n.after(b, moments_links))
                root_by_halving(nc, link, var_eps, root_tmp, rstd)
                assert count[0] == link_n.per, count[0]
                norm_rows(nc, x_in, x_in, mv, rstd).then_inc(ln_done.sem, 1)

            def ht_halves(b):
                for k in range(KD):
                    dve.wait_ge(ht_whole.sem, ht_whole.after(b, k + 1))
                    nc.vector.tensor_copy(hT[0][:, k], whole_hT[:, k]).then_inc(ht_high.sem, 1)
                    dve.wait_ge(ht_high.sem, ht_high.after(b, k + 1))
                    low(nc, hT[1][:, k], whole_hT[:, k], hT[0][:, k]).then_inc(ht_ready.sem, 1)

            def qk_halves(g):
                for w in range(2):
                    dve.wait_ge(qk_high.sem, qk_high.after(g, w + 1))
                    low(nc, qkT[1][:, w], proj[:, w], qkT[0][:, w]).then_inc(qk_low.sem, 1)

            def v_halves(r):
                for w in range(2):
                    dve.wait_ge(v_high.sem, v_high.after(r, w + 1))
                    low(nc, v[1][:, 2 * w:2 * w + 2], proj[:, w].rearrange("p (t n) -> p t n", t=2), v[0][:, 2 * w:2 * w + 2]).then_inc(v_low.sem, 1)

            def z_halves(g):
                dve.wait_ge(z_high.sem, z_high.after(g, 1))
                low(nc, zT[1][:], z_ps[:], zT[0][:]).then_inc(z_low.sem, 1)

            def pair(b, p, place):
                r = b * PAIRS + p
                start = place == "first" and isinstance(b, int) and b == 0
                for a in range(2):
                    g = r * 2 + a
                    for i in range(TILES):
                        bank, col = s_place[i]
                        if i != 1:
                            wait_apart(dve, s_done.sem, s_done.after(g, max(i, 1)))
                        n = (i + 1) * P
                        nc.vector.tensor_tensor_reduce(
                            out=probs[:, off[i]:off[i + 1]], in0=work[:, bank, col:col + n], in1=keep["causal"][:, S - n:S],
                            scale=-scale, scalar=3.0e38, op0=ALU.add, op1=ALU.min, accum_out=neg_top[:, i:i + 1]).then_inc(top_ready.sem, 1)
                    dve.wait_ge(exp_done.sem, exp_done.after(g, TILES))
                    nc.vector.reciprocal(inv_total[:], total[:]).then_inc(link_h.sem, 1)
                    dve.wait_ge(link_h.sem, link_h.after(g, 1))
                    for i in range(TILES):
                        row = probs[:, off[i]:off[i + 1]]
                        ins = nc.vector.tensor_scalar(row, row, inv_total[:, i:i + 1], None, ALU.mult)
                    ins.then_inc(probs_ready.sem, 1)
                    if start and a == 0:
                        v_halves(r)
                    if not (place in ("next", "last") and a == 1):
                        qk_halves(g + 1)
                    if not (start and a == 0):
                        z_halves(g - 1)
                    if place == "next" and a == 1:
                        ht_halves(b + 1)
                    for n, (bank, lo, hi) in enumerate(pt_groups):
                        dve.wait_ge(pt_high.sem, pt_high.after(g, n + 1))
                        low(nc, probs_t[1][:, lo:hi], work[:, bank, 0:hi - lo], probs_t[0][:, lo:hi]).then_inc(pt_low.sem, 1)
                    if a == 0 and not start:
                        v_halves(r)
                    if place == "first" and a == 0 and not start:
                        add_residual(b - 1)

            def add_residual(b):
                dve.wait_ge(o_done.sem, o_done.after(b, 1))
                dve.wait_ge(res_loaded.sem, res_loaded.after(b, 32))
                dve.wait_ge(w_split.sem, w_split.done(PAIRS - 1))
                dve.wait_ge(y_stored.sem, y_stored.before(b, 16))
                gate_rows = gate[:].rearrange("p (o d) -> p o d", o=1).to_broadcast([P, TILES, D])
                nc.vector.tensor_tensor(y, o_ps[:], gate_rows, ALU.mult).then_inc(o_used.sem, 1)
                dve.wait_ge(o_used.sem, o_used.after(b, 1))
                nc.vector.tensor_tensor(y, y, x_res[:], ALU.add).then_inc(y_done.sem, 1)

            def batch(b, more):
                pair(b, 0, "first")
                if more:
                    moments(b + 1)
                with dve.Fori(1, PAIRS - 1) as p:
                    pair(b, p, "middle")
                if more:
                    normalise(b + 1)
                pair(b, PAIRS - 1, "next" if more else "last")
                if more:
                    qk_halves((b + 1) * NH)
                else:
                    z_halves(b * NH + NH - 1)
                    add_residual(b)

            moments(0)
            normalise(0)
            ht_halves(0)
            qk_halves(0)
            batches(dve, batch)
        m.end()


class SplitWeights:

    def __init__(self, nc, m, io, entries, raw, by_pool):
        self.nc, self.io, self.entries, self.raw, self.by_pool = nc, io, entries, raw, by_pool
        self.at = {}
        n = 0
        for name, width in entries:
            self.at[name] = slice(n, n + width)
            n += width
        self.halves = [m.sb(f"weights{i}", [P, n], F32R) for i in "hl"]
        self.loaded = [m.sem(f"{name}_loaded") for name, _ in entries]
        self.high = m.sem("weights_high")
        self.ready = m.sem("weights_ready")
        self.ready_by_pool = m.sem("weights_ready_by_pool")

    def load(self, sp):
        for (name, _), sem in zip(self.entries, self.loaded):
            sp.dma_start(self.raw[:, self.at[name]], self.io[name]).then_inc(sem, 16)

    def span(self, first, last):
        names = [name for name, _ in self.entries]
        return [(n, names[n], self.at[names[n]]) for n in range(names.index(first), names.index(last) + 1)]

    def split_high(self, act, first, last):
        for n, name, at in self.span(first, last):
            act.wait_ge(self.loaded[n], 16)
            self.nc.scalar.activation(self.halves[0][:, at], self.raw[:, at], ACT.Copy).then_inc(self.high, 1)

    def split_low(self, dve, first, last):
        for n, name, at in self.span(first, last):
            if name in self.by_pool:
                continue
            dve.wait_ge(self.high, n + 1)
            low(self.nc, self.halves[1][:, at], self.raw[:, at], self.halves[0][:, at]).then_inc(self.ready, 1)

    def split_low_by_pool(self, pool):
        for n, (name, _) in enumerate(self.entries):
            if name in self.by_pool:
                at = self.at[name]
                pool.wait_ge(self.high, n + 1)
                self.nc.gpsimd.tensor_tensor(self.halves[1][:, at], self.raw[:, at], self.halves[0][:, at].bitcast(F32),
                                             ALU.subtract).then_inc(self.ready_by_pool, 1)

    def count(self, name):
        pool = name in self.by_pool
        return [n for n, _ in self.entries if (n in self.by_pool) == pool].index(name) + 1

    def part(self, name, lo, hi):
        start = self.at[name].start
        return tuple(h[:, start + lo:start + hi] for h in self.halves)


def in_batches(eng, body):
    body(0, 0, True, False)
    with eng.Fori(0, B // 2 - 1) as i:
        body(i * 2 + 1, 1, False, False)
        body(i * 2 + 2, 0, False, False)
    body(B - 1, 1, False, True)


class NormedInput:

    def __init__(self, nc, m, io, keep, source, layer, scale, shift, ps, ps_free):
        self.nc, self.io, self.keep, self.source = nc, io, keep, source
        self.layer, self.scale, self.shift, self.ps, self.ps_free = layer, scale, shift, ps, ps_free
        self.x = m.sb("x", [P, TILES, D])
        self.residual = m.sb("residual", [P, TILES, D])
        self.xn = m.sb("xn", [P, TILES, D])
        self.hT = [[m.sb(f"hT{i}{q}", [P, KD, S], F32R) for i in "hl"] for q in range(2)]
        self.stats = m.sb("stats", [P, TILES, 6])
        self.mv = m.sb("mv", [P, TILES, 2])
        self.rstd, self.var_eps, self.root_tmp = (m.sb(n, [P, TILES]) for n in ("rstd", "var_eps", "root_tmp"))
        self.gate_row = m.sb("gate_row", [P, 1, D])
        self.x_loaded = m.counted("x_loaded", 16)
        self.residual_loaded = m.counted("residual_loaded", 32)
        self.link_n = m.counted("link_n", 14)
        self.normed = m.counted("normed", 1, credit=1)
        self.in_psum = m.counted("in_psum", 1)
        self.whole = m.counted("whole", 1)
        self.ready = m.counted("ready", 1)
        self.whole_hT = self.xn[:].rearrange("p t d -> p (t d)").rearrange("p (k s) -> p k s", k=KD)

    def tokens(self, b):
        return self.io[self.source][bass.ds(b * S, S), :].rearrange("(t p) d -> p t d", p=P)

    def load(self, sp, b):
        wait_apart(sp, self.normed.sem, self.normed.before(b, 1))
        sp.dma_start(self.x[:], self.tokens(b)).then_inc(self.x_loaded.sem, 16)

    def load_residual(self, sp, b, gate):
        sp.dma_start(self.residual[:], self.tokens(b)).then_inc(self.residual_loaded.sem, 16)
        row = self.io["mod_rows"][self.layer, bass.ds(b, 1), gate * D:(gate + 1) * D].to_broadcast([P, D])
        sp.dma_start(self.gate_row[:, 0], row).then_inc(self.residual_loaded.sem, 16)

    def linker(self, dve, b, passed):
        count = [passed]

        def link(ins, wait=wait_on):
            count[0] += 1
            ins.then_inc(self.link_n.sem, 1)
            wait(dve, self.link_n.sem, self.link_n.after(b, count[0]))
        return link

    def moments(self, dve, b):
        nc, link = self.nc, self.linker(dve, b, 0)
        dve.wait_ge(self.x_loaded.sem, self.x_loaded.after(b, 16))
        moments_of_rows(nc, link, self.x, self.stats, self.mv, self.var_eps).then_inc(self.link_n.sem, 1)

    def norm(self, dve, b):
        nc, link = self.nc, self.linker(dve, b, 3)
        dve.wait_ge(self.link_n.sem, self.link_n.after(b, 3))
        root_by_halving(nc, link, self.var_eps, self.root_tmp, self.rstd)
        norm_rows(nc, self.x, self.xn, self.mv, self.rstd).then_inc(self.normed.sem, 1)

    def transpose(self, pe, b):
        pe.wait_ge(self.normed.sem, self.normed.after(b, 1))
        self.ps_free(pe, b)
        transpose_rows(self.nc, self.ps, self.xn, self.keep["ident"]).then_inc(self.in_psum.sem, 1)

    def modulate(self, act, b):
        act.wait_ge(self.in_psum.sem, self.in_psum.after(b, 1))
        for k in range(KD):
            mod = [self.keep["mod"][:, self.layer, n * KD + k, bass.ds(b, 1)] for n in (self.scale, self.shift)]
            last = self.nc.scalar.activation(self.whole_hT[:, k, :], self.ps[:, k, :], ACT.Identity, bias=mod[1], scale=mod[0])
        last.then_inc(self.whole.sem, 1)

    def halve(self, dve, b, q):
        dve.wait_ge(self.whole.sem, self.whole.after(b, 1))
        self.nc.vector.tensor_copy(self.hT[q][0][:], self.whole_hT).then_inc(self.link_n.sem, 1)
        dve.wait_ge(self.link_n.sem, self.link_n.done(b))
        low(self.nc, self.hT[q][1][:], self.whole_hT, self.hT[q][0][:]).then_inc(self.ready.sem, 1)


def moe_stage(nc, io, keep):
    experts, basis, inner = 128, 8, 128
    wide = basis * inner
    shared = 2 * inner
    row = experts + 8
    top = 4
    with ExitStack() as ctx:
        m = Alloc(nc, ctx, "moe")
        entries = [("router", KD * experts), ("sh_gate", KD * shared), ("sh_up", KD * shared),
                   ("ex_gate", KD * wide), ("ex_up", KD * wide), ("ex_down", D), ("sh_down", 2 * D)]
        raw = m.sb("raw", [P, sum(n for _, n in entries)])
        w = SplitWeights(nc, m, io, entries, raw, ("ex_gate", "ex_up"))
        amp = m.sb("amp", [P, basis, 2])
        e_scale = m.sb("e_scale", [P, 1])
        mix = m.sb("mix", [P, basis])
        mix_sum = m.sb("mix_sum", [P, 1])
        top_logit = m.sb("top_logit", [P, TILES])
        neg_top = m.sb("neg_top", [P, TILES])
        probs = m.sb("probs", [P, TILES, row])
        rest = m.sb("rest", [P, TILES, row])
        total = m.sb("total", [P, TILES])
        best = m.sb("best", [P, TILES, 8])
        best_sum = m.sb("best_sum", [P, TILES])
        route_t = m.sb("route_t", [P, S])
        coeff = m.sb("coeff", [P, 2, TILES, basis])
        silu = m.sb("silu", [P, 2, wide])
        base = m.sb("base", [P, 2, wide])
        tree = m.sb("tree", [P, wide // 2])
        mixed = m.sb("mixed", [P, 2, inner])
        mixedT = [m.sb(f"mixedT{i}", [P, S], F32R) for i in "hl"]
        sh_silu = m.sb("sh_silu", [P, 2, S])
        sh_hid = m.sb("sh_hid", [P, 2, S])
        sh_hT = [m.sb(f"sh_hT{i}", [P, 2, S], F32R) for i in "hl"]
        y = m.sb("y", [P, TILES, D])
        gu = m.ps("gu", [P, 2, 2, 512])
        route_ps = m.ps("route_ps", [P, 512])
        mixed_ps = m.ps("mixed_ps", [P, 512])
        o_ps = m.ps("o_ps", [P, TILES, D])

        amp_loaded = m.sem("amp_loaded")
        mix_link = m.sem("mix_link")
        mix_ready = m.sem("mix_ready")
        link_r = m.counted("link_r", 9)
        logits_done = m.counted("logits_done", 1)
        neg_ready = m.counted("neg_ready", 1)
        exp_done = m.counted("exp_done", 1)
        routed = m.counted("routed", 1)
        rt_done = m.counted("rt_done", 1)
        rt_copied = m.counted("rt_copied", 1)
        coeff_done = m.counted("coeff_done", 1)
        coeff_ready = m.counted("coeff_ready", 1)
        gu_done = m.counted("gu_done", 2)
        silu_done = m.counted("silu_done", 2)
        base_done = m.counted("base_done", 2, credit=2)
        link_m = m.counted("link_m", 1)
        weighed = m.counted("weighed", 1)
        link_p = m.counted("link_p", 2)
        mixed_done = m.counted("mixed_done", 1, credit=2)
        sh_done = m.counted("sh_done", 2)
        sh_silu_done = m.counted("sh_silu_done", 2)
        sh_hid_done = m.counted("sh_hid_done", 2)
        sh_high = m.counted("sh_high", 1)
        sh_low = m.counted("sh_low", 1)
        mt_done = m.counted("mt_done", 4, credit=2)
        mt_high = m.counted("mt_high", 1)
        mt_low = m.counted("mt_low", 1)
        o_done = m.counted("o_done", 1)
        link_y = m.counted("link_y", 1)
        y_done = m.counted("y_done", 1, credit=1)
        y_stored = m.counted("y_stored", 16, credit=16)
        xin = NormedInput(nc, m, io, keep, "x1", 0, CB, SB, o_ps[:].rearrange("p t d -> p (t d)").rearrange("p (k s) -> p k s", k=KD), lambda pe, b: None)
        block = m.begin()

        @block.sync
        def _(sp):
            for s in (xin.normed, base_done, mixed_done, mt_done, y_done, y_stored):
                sp.sem_inc(s.sem, s.credit)
            xin.load(sp, 0)
            sp.dma_start(amp[:], io["amplitudes"]).then_inc(amp_loaded, 16)
            sp.dma_start(e_scale[:], io["expert_scale"]).then_inc(amp_loaded, 16)
            w.load(sp)

            def store(b):
                wait_apart(sp, y_done.sem, y_done.after(b, 1))
                sp.dma_start(io["x2"][bass.ds(b * S, S), :].rearrange("(t p) d -> p t d", p=P), y[:]).then_inc(y_stored.sem, 16)

            def body(b, q, first, last):
                if not last:
                    xin.load(sp, b + 1)
                if not first:
                    store(b - 1)
                xin.load_residual(sp, b, GB)

            in_batches(sp, body)
            store(B - 1)
            sp.wait_ge(y_stored.sem, y_stored.after(B - 1, 16))

        @block.gpsimd
        def _(pool):
            def body(b, q, first, last):
                for t in range(TILES):
                    n = b * TILES + t
                    pool.wait_ge(mixed_done.sem, mixed_done.before(n, 1))
                    pool.wait_ge(weighed.sem, weighed.after(n, 1))
                    s = t % 2
                    half = wide // 2
                    nc.gpsimd.tensor_tensor(tree[:], base[:, s, 0:half], base[:, s, half:wide], ALU.add).then_inc(link_p.sem, 1)
                    pool.wait_ge(link_p.sem, link_p.after(n, 1))
                    nc.gpsimd.tensor_tensor(tree[:, 0:half // 2], tree[:, 0:half // 2], tree[:, half // 2:half], ALU.add).then_inc(link_p.sem, 1)
                    pool.wait_ge(link_p.sem, link_p.after(n, 2))
                    pool.wait_ge(mt_done.sem, mt_done.after(b, t - 1))
                    nc.gpsimd.tensor_tensor(mixed[:, s], tree[:, 0:inner], tree[:, inner:2 * inner], ALU.add).then_inc(mixed_done.sem, 1)

            w.split_low_by_pool(pool)
            in_batches(pool, body)

        @block.tensor
        def _(pe):
            def gate_up(b, t, q, c):
                if t:
                    pe.wait_ge(base_done.sem, base_done.after(b * TILES + t - 1, c + 1))
                else:
                    pe.wait_ge(sh_hid_done.sem, sh_hid_done.after(b, c + 1))
                for g, name in enumerate(("ex_gate", "ex_up")):
                    for k in range(KD):
                        at = slice(t * P, (t + 1) * P)
                        col = k * wide + c * 512
                        mm = products(nc, gu[:, c, g, :], (xin.hT[q][0][:, k, at], xin.hT[q][1][:, k, at]),
                                      w.part(name, col, col + 512), k == 0, k == KD - 1)
                mm.then_inc(gu_done.sem, 1)

            def route(b, q):
                pe.wait_ge(xin.ready.sem, xin.ready.after(b, 1))
                for t in range(TILES):
                    for k in range(KD):
                        at = slice(t * P, (t + 1) * P)
                        mm = products(nc, route_ps[:, t * P:(t + 1) * P], (xin.hT[q][0][:, k, at], xin.hT[q][1][:, k, at]),
                                      w.part("router", k * experts, (k + 1) * experts), k == 0, k == KD - 1)
                mm.then_inc(logits_done.sem, 1)

            def turn_routes(b):
                pe.wait_ge(routed.sem, routed.after(b, 1))
                for t in range(TILES):
                    mm = nc.tensor.transpose(route_ps[:, t * P:(t + 1) * P], rest[:, t, 0:experts], keep["ident"][:])
                mm.then_inc(rt_done.sem, 1)

            def mix_coefficients(b):
                pe.wait_ge(rt_copied.sem, rt_copied.after(b, 1))
                for t in range(TILES):
                    mm = nc.tensor.matmul(route_ps[:, t * basis:(t + 1) * basis], route_t[:, t * P:(t + 1) * P], mix[:], start=True, stop=True)
                mm.then_inc(coeff_done.sem, 1)

            def shared_up(b, q, after_tile):
                for i in range(2):
                    if after_tile:
                        pe.wait_ge(base_done.sem, after_tile(i))
                    for g, name in enumerate(("sh_gate", "sh_up")):
                        for k in range(KD):
                            col = k * shared + i * P
                            mm = products(nc, gu[:, i, g, :], w.part(name, col, col + P),
                                          (xin.hT[q][0][:, k, :], xin.hT[q][1][:, k, :]), k == 0, k == KD - 1)
                    mm.then_inc(sh_done.sem, 1)

            def turn_mixed(b, t):
                pe.wait_ge(mixed_done.sem, mixed_done.after(b * TILES + t, 1))
                nc.tensor.transpose(mixed_ps[:, t * P:(t + 1) * P], mixed[:, t % 2], keep["ident"][:]).then_inc(mt_done.sem, 1)

            def down(b):
                pe.wait_ge(mt_low.sem, mt_low.after(b, 1))
                pe.wait_ge(sh_low.sem, sh_low.after(b, 1))
                for t in range(TILES):
                    at = slice(t * P, (t + 1) * P)
                    products(nc, o_ps[:, t, :], (mixedT[0][:, at], mixedT[1][:, at]), w.part("ex_down", 0, D), True, False)
                    for i in range(2):
                        mm = products(nc, o_ps[:, t, :], (sh_hT[0][:, i, at], sh_hT[1][:, i, at]),
                                      w.part("sh_down", i * D, (i + 1) * D), False, i == 1)
                mm.then_inc(o_done.sem, 1)

            def body(b, q, first, last):
                if first:
                    pe.wait_ge(w.ready, w.count("sh_down"))
                    pe.wait_ge(w.ready_by_pool, w.count("ex_up"))
                for t in range(TILES):
                    if t == 0:
                        turn_routes(b)
                    gate_up(b, t, q, 0)
                    gate_up(b, t, q, 1)
                    if t == 0:
                        mix_coefficients(b)
                        if not first:
                            turn_mixed(b - 1, TILES - 1)
                        if not last:
                            if not first:
                                pe.wait_ge(y_done.sem, y_done.before(b, 1, back=2))
                            xin.transpose(pe, b + 1)
                    if t == 1 and not first:
                        if not last:
                            pe.wait_ge(xin.whole.sem, xin.whole.after(b + 1, 1))
                        else:
                            pe.wait_ge(y_done.sem, y_done.before(b, 1, back=2))
                        down(b - 1)
                    if t:
                        turn_mixed(b, t - 1)
                    if t == 1 and not last:
                        pe.wait_ge(coeff_ready.sem, coeff_ready.after(b, 1))
                        route(b + 1, 1 - q)
                if not last:
                    shared_up(b + 1, 1 - q, lambda i: base_done.after(b * TILES + TILES - 1, i + 1))

            xin.transpose(pe, 0)
            pe.wait_ge(w.ready, w.count("router"))
            route(0, 0)
            pe.wait_ge(w.ready, w.count("sh_up"))
            shared_up(0, 0, None)
            pe.wait_ge(mix_ready, 1)
            in_batches(pe, body)
            turn_mixed(B - 1, TILES - 1)
            down(B - 1)

        @block.scalar
        def _(act):
            def exponentials(b):
                act.wait_ge(neg_ready.sem, neg_ready.after(b, 1))
                for t in range(TILES):
                    ins = nc.scalar.activation(probs[:, t, 0:experts], route_ps[:, t * P:(t + 1) * P], ACT.Exp,
                                               bias=neg_top[:, t:t + 1], accum_out=total[:, t:t + 1])
                ins.then_inc(exp_done.sem, 1)

            def copy_routes(b):
                act.wait_ge(rt_done.sem, rt_done.after(b, 1))
                nc.scalar.activation(route_t[:], route_ps[:], ACT.Copy).then_inc(rt_copied.sem, 1)

            def shared_silu(b):
                for i in range(2):
                    act.wait_ge(sh_done.sem, sh_done.after(b, i + 1))
                    nc.scalar.activation(sh_silu[:, i, :], gu[:, i, 0, :], ACT.Silu).then_inc(sh_silu_done.sem, 1)

            def shared_high(b):
                if not isinstance(b, int) or b:
                    act.wait_ge(o_done.sem, o_done.after(b - 1, 1))
                act.wait_ge(sh_hid_done.sem, sh_hid_done.after(b, 2))
                nc.scalar.activation(sh_hT[0][:], sh_hid[:], ACT.Copy).then_inc(sh_high.sem, 1)

            def mixed_high(b):
                act.wait_ge(mt_done.sem, mt_done.after(b, TILES))
                nc.scalar.activation(mixedT[0][:], mixed_ps[:], ACT.Copy).then_inc(mt_high.sem, 1)

            def body(b, q, first, last):
                for t in range(TILES):
                    n = b * TILES + t
                    if t == 2 and not last:
                        exponentials(b + 1)
                    if t == 0:
                        copy_routes(b)
                    for c in range(2):
                        act.wait_ge(gu_done.sem, gu_done.after(n, c + 1))
                        nc.scalar.activation(silu[:, t % 2, c * 512:(c + 1) * 512], gu[:, c, 0, :], ACT.Silu).then_inc(silu_done.sem, 1)
                    if t == 0:
                        if not first:
                            mixed_high(b - 1)
                        if not last:
                            xin.modulate(act, b + 1)
                    if t == 2:
                        shared_high(b)
                if not last:
                    shared_silu(b + 1)

            xin.modulate(act, 0)
            w.split_high(act, "router", "sh_down")
            exponentials(0)
            shared_silu(0)
            in_batches(act, body)
            mixed_high(B - 1)

        @block.vector
        def _(dve):
            def route_tops(b, link):
                dve.wait_ge(logits_done.sem, logits_done.after(b, 1))
                link(nc.vector.tensor_reduce(top_logit[:], route_ps[:].rearrange("p (t e) -> p t e", t=TILES), AX.X, ALU.max))
                nc.vector.tensor_scalar(neg_top[:], top_logit[:], -1.0, None, ALU.mult).then_inc(neg_ready.sem, 1)

            def route_weights(b, link):
                dve.wait_ge(exp_done.sem, exp_done.after(b, 1))
                link(nc.vector.reciprocal(total[:], total[:]))
                for t in range(TILES):
                    ins = nc.vector.tensor_scalar(probs[:, t, 0:experts], probs[:, t, 0:experts], total[:, t:t + 1], None, ALU.mult)
                link(ins, wait_apart)
                for t in range(TILES):
                    ins = nc.vector.max(best[:, t, :], probs[:, t, 0:experts])
                link(ins)
                nc.vector.memset(best[:, :, top:8], -1.0)
                link(nc.vector.tensor_reduce(best_sum[:], best[:, :, 0:top], AX.X, ALU.add), wait_apart)
                for t in range(TILES):
                    ins = nc.vector.match_replace(rest[:, t, :], best[:, t, :], probs[:, t, :], 0.0)
                link(ins)
                link(nc.vector.tensor_scalar(best_sum[:], best_sum[:], 1e-8, None, ALU.add))
                link(nc.vector.reciprocal(best_sum[:], best_sum[:]))
                link(nc.vector.tensor_tensor(rest[:], probs[:], rest[:], ALU.subtract))
                for t in range(TILES):
                    ins = nc.vector.tensor_scalar(rest[:, t, :], rest[:, t, :], best_sum[:, t:t + 1], None, ALU.mult)
                ins.then_inc(routed.sem, 1)

            def copy_coefficients(b, q):
                dve.wait_ge(coeff_done.sem, coeff_done.after(b, 1))
                nc.vector.tensor_copy(coeff[:, q], route_ps[:, 0:TILES * basis].rearrange("p (t k) -> p t k", t=TILES)).then_inc(coeff_ready.sem, 1)

            def shared_hidden(b):
                for i in range(2):
                    dve.wait_ge(sh_silu_done.sem, sh_silu_done.after(b, i + 1))
                    nc.vector.tensor_tensor(sh_hid[:, i, :], sh_silu[:, i, :], gu[:, i, 1, :], ALU.mult).then_inc(sh_hid_done.sem, 1)

            def shared_low(b):
                dve.wait_ge(sh_high.sem, sh_high.after(b, 1))
                low(nc, sh_hT[1][:], sh_hid[:], sh_hT[0][:]).then_inc(sh_low.sem, 1)

            def mixed_low(b):
                dve.wait_ge(mt_high.sem, mt_high.after(b, 1))
                low(nc, mixedT[1][:], mixed_ps[:], mixedT[0][:]).then_inc(mt_low.sem, 1)

            def residual(b):
                dve.wait_ge(o_done.sem, o_done.after(b, 1))
                dve.wait_ge(xin.residual_loaded.sem, xin.residual_loaded.after(b, 32))
                dve.wait_ge(y_stored.sem, y_stored.before(b, 16))
                rows = xin.gate_row[:].to_broadcast([P, TILES, D])
                nc.vector.tensor_tensor(y[:], o_ps[:], rows, ALU.mult).then_inc(link_y.sem, 1)
                dve.wait_ge(link_y.sem, link_y.after(b, 1))
                nc.vector.tensor_tensor(y[:], y[:], xin.residual[:], ALU.add).then_inc(y_done.sem, 1)

            def linker(b):
                count = [0]

                def link(ins, wait=wait_on):
                    count[0] += 1
                    ins.then_inc(link_r.sem, 1)
                    wait(dve, link_r.sem, link_r.after(b, count[0]))
                return link, count

            def body(b, q, first, last):
                link, count = linker(b + 1)
                for t in range(TILES):
                    n = b * TILES + t
                    s = t % 2
                    if t == 0 and not last:
                        xin.moments(dve, b + 1)
                        xin.norm(dve, b + 1)
                    if t == 1 and not last:
                        xin.halve(dve, b + 1, 1 - q)
                    if t == 2 and not last:
                        route_tops(b + 1, link)
                    dve.wait_ge(mixed_done.sem, mixed_done.before(n, 1, back=2))
                    for c in range(2):
                        at = slice(c * 512, (c + 1) * 512)
                        dve.wait_ge(silu_done.sem, silu_done.after(n, c + 1))
                        nc.vector.tensor_tensor(base[:, s, at], silu[:, s, at], gu[:, c, 1, :], ALU.mult).then_inc(base_done.sem, 1)
                        if t == 2 and c == 0 and not last:
                            route_weights(b + 1, link)
                    if t == 0:
                        copy_coefficients(b, q)
                        dve.wait_ge(coeff_ready.sem, coeff_ready.after(b, 1))
                    dve.wait_ge(base_done.sem, base_done.after(n, 2))
                    grid = base[:, s].rearrange("p (k i) -> p k i", k=basis)
                    by = coeff[:, q, t, :].rearrange("p (k o) -> p k o", o=1).to_broadcast([P, basis, inner])
                    nc.vector.tensor_tensor(grid, grid, by, ALU.mult).then_inc(weighed.sem, 1)
                    if t == 0 and not first:
                        mixed_low(b - 1)
                    if t == 1 and not first:
                        residual(b - 1)
                    if t == 2:
                        shared_low(b)
                if not last:
                    shared_hidden(b + 1)
                    assert count[0] == link_r.per, count[0]

            nc.vector.memset(probs[:], -1.0)
            xin.moments(dve, 0)
            xin.norm(dve, 0)
            xin.halve(dve, 0, 0)
            dve.wait_ge(amp_loaded, 32)
            links = [0]

            def link(ins):
                links[0] += 1
                ins.then_inc(mix_link, 1)
                dve.wait_ge(mix_link, links[0])

            link(nc.vector.tensor_tensor(amp[:], amp[:], amp[:], ALU.mult))
            link(nc.vector.tensor_tensor(mix[:], amp[:, :, 0], amp[:, :, 1], ALU.add))
            link(nc.vector.tensor_reduce(mix_sum[:], mix[:], AX.X, ALU.add))
            link(nc.vector.tensor_scalar(mix_sum[:], mix_sum[:], 1e-8, None, ALU.add))
            link(nc.vector.reciprocal(mix_sum[:], mix_sum[:]))
            nc.vector.tensor_scalar(mix[:], mix[:], mix_sum[:, 0:1], e_scale[:, 0:1], ALU.mult, ALU.mult).then_inc(mix_ready, 1)
            w.split_low(dve, "router", "sh_down")
            link, _ = linker(0)
            route_tops(0, link)
            route_weights(0, link)
            shared_hidden(0)
            in_batches(dve, body)
            mixed_low(B - 1)
            residual(B - 1)
        m.end()


class Root:

    def __init__(self, nc, m, name, width):
        self.nc = nc
        self.v, self.tmp, self.root = (m.sb(f"{name}_{n}", [P, 2, width]) for n in ("v", "tmp", "root"))

    def solve(self, link, lane=slice(0, 2)):
        root_by_halving(self.nc, link, self.v[:, lane], self.tmp[:, lane], self.root[:, lane])


def gla_stage(nc, io, keep):
    heads, hk, hv, chunk, rank = 8, 16, 32, 64, 16
    keys, vals = heads * hk, heads * hv
    chunks = S // chunk
    inner = 768
    ki = inner // P
    gate_norm = 16.0
    rms_eps = 1e-6
    with ExitStack() as ctx:
        m = Alloc(nc, ctx, "gla")
        entries = [("g_q", KD * keys), ("g_k", KD * keys), ("g_vg", KD * 2 * vals), ("g_o", KD * D),
                   ("g_gate", KD * inner), ("g_up", KD * inner), ("g_down", ki * D)]
        low1 = m.sb("low1", [P, KD, rank])
        low2 = m.sb("low2", [rank, keys])
        low_bias = m.sb("low_bias", [P, 1])
        norm_cols = m.sb("norm_cols", [P, 2, KD])
        gnorm = m.sb("gnorm", [P, hv])
        own_head = m.sb("own_head", [P, heads])
        state_mask = m.sb("state_mask", [P, vals])
        tri = m.sb("tri", [P, chunk])
        carry = m.sb("carry", [P, S])
        one = m.sb("one", [P, 1])

        class Lane:

            def __init__(self, q):
                n = f"{q}_"
                self.q = q
                self.pre, self.h0, self.t1 = (m.sb(n + k, [P, TILES, D]) for k in ("pre", "h0", "t1"))
                self.rows = m.sb(n + "rows", [P, 2, D])
                self.gate = m.sb(n + "gate", [P, 1, D])
                self.t2 = m.sb(n + "t2", [P, 1024])
                self.t3 = m.sb(n + "t3", [P, 1024])
                self.hT = [m.sb(f"{n}hT{i}", [P, KD, S], F32R) for i in "hl"]
                self.act = [m.sb(f"{n}act{i}", [P, 2, S], F32R) for i in "hl"]
                area = self.area = m.sb(n + "area", [P, 8192])
                cut = [area[:, i * 512:(i + 1) * 512] for i in range(16)]
                self.eb, self.enb, self.g, self.bs = cut[0:4]
                self.low = area[0:rank, 0:512]
                self.a = area[:, 0:2048].rearrange("p (t n) -> p t n", t=TILES)
                self.hn = area[:, 0:1024].rearrange("p (t d) -> p t d", t=TILES)
                self.turned = area[:, 1024:2048].rearrange("p (k s) -> p k s", k=KD)
                self.qe, self.ke, self.kd = cut[4:7]
                self.kd_tok = area[:, 3584:4096].rearrange("p (t n) -> p t n", t=TILES)
                self.v = area[:, 4096:5120].rearrange("p (t n) -> p t n", t=TILES)
                self.x = self.v
                self.gs = area[:, 5120:6144].rearrange("p (t n) -> p t n", t=TILES)
                self.vg = area[:, 4096:6144].rearrange("p (h t n) -> p h t n", h=2, t=TILES)
                self.state = area[:, 6144:8192].rearrange("p (c n) -> p c n", c=chunks)
                self.ebl = m.sb(n + "ebl", [P, chunks])
                self.stats = m.sb(n + "stats", [P, TILES, 6])
                self.mv = m.sb(n + "mv", [P, TILES, 2])
                self.sq = m.sb(n + "sq", [P, TILES])
                self.X = m.ps(n + "X", [P, 2, 512])
                self.Y = m.ps(n + "Y", [P, 2, 512])
                self.Yt = self.Y[:].rearrange("p w n -> p (w n)").rearrange("p (t d) -> p t d", t=TILES)
                self.whole = self.t1[:].rearrange("p t d -> p (t d)").rearrange("p (k s) -> p k s", k=KD)
                self.qx = [t[:].rearrange("p (c h n) -> p c h n", c=2, h=heads) for t in (self.t2, self.t3)]
                self.pre_loaded = m.counted(n + "pre_loaded", 32)
                self.x_loaded = m.counted(n + "x_loaded", 32)
                self.front_link = m.counted(n + "front_link", 3)
                self.link = m.counted(n + "link", 30)
                self.alink = m.counted(n + "alink", 1)
                self.normed = m.counted(n + "normed", 1)
                self.scaled = m.counted(n + "scaled", 1)
                self.h0_done = m.counted(n + "h0_done", 1)
                self.sq1 = m.counted(n + "sq1", 1)
                self.hn_done = m.counted(n + "hn_done", 1)
                self.in_psum = m.counted(n + "in_psum", 3)
                self.whole_done = m.counted(n + "whole_done", 2)
                self.ht_link = m.counted(n + "ht_link", 2)
                self.ht_ready = m.counted(n + "ht_ready", 2)
                self.low_done = m.counted(n + "low_done", 1)
                self.low_copied = m.counted(n + "low_copied", 1)
                self.qk_done = m.counted(n + "qk_done", 1)
                self.gk_done = m.counted(n + "gk_done", 1)
                self.abs_done = m.counted(n + "abs_done", 1)
                self.min_done = m.counted(n + "min_done", 1)
                self.zl_done = m.counted(n + "zl_done", 1)
                self.scan_done = m.counted(n + "scan_done", 1)
                self.exps_done = m.counted(n + "exps_done", 1)
                self.qk_used = m.counted(n + "qk_used", 1)
                self.qx_done = m.counted(n + "qx_done", 4)
                self.vg_done = m.counted(n + "vg_done", 4)
                self.vg_used = m.counted(n + "vg_used", 4)
                self.silu_done = m.counted(n + "silu_done", 1)
                self.gs_done = m.counted(n + "gs_done", 1)
                self.kd_done = m.counted(n + "kd_done", 1)
                self.kd_copied = m.counted(n + "kd_copied", 1)
                self.a_done = m.counted(n + "a_done", 4)
                self.a_used = m.counted(n + "a_used", 4)
                self.u_done = m.counted(n + "u_done", 2)
                self.u_used = m.counted(n + "u_used", 2)
                self.state_done = m.counted(n + "state_done", 1)
                self.o_done = m.counted(n + "o_done", 1)
                self.sq2 = m.counted(n + "sq2", 1)
                self.o_used = m.counted(n + "o_used", 1)
                self.on_done = m.counted(n + "on_done", 1)
                self.ot_high = m.counted(n + "ot_high", 1)
                self.ot_ready = m.counted(n + "ot_ready", 1)
                self.wo_done = m.counted(n + "wo_done", 1)
                self.x1_done = m.counted(n + "x1_done", 1)
                self.sq3 = m.counted(n + "sq3", 1)
                self.h2_done = m.counted(n + "h2_done", 1)
                self.gu_done = m.counted(n + "gu_done", ki)
                self.sg_done = m.counted(n + "sg_done", ki)
                self.f_done = m.counted(n + "f_done", ki)
                self.fh_done = m.counted(n + "fh_done", ki)
                self.fl_done = m.counted(n + "fl_done", ki)
                self.down_done = m.counted(n + "down_done", ki)
                self.sum_done = m.counted(n + "sum_done", 1, credit=1)
                self.plink = m.counted(n + "plink", 1)
                self.y_done = m.counted(n + "y_done", 1, credit=1)
                self.y_stored = m.counted(n + "y_stored", 16, credit=16)

        lanes = [Lane(q) for q in range(2)]
        w = SplitWeights(nc, m, io, entries, lanes[1].area[:, 8192 - sum(n for _, n in entries):], ("g_gate", "g_up", "g_down"))
        ln_root, rms1_root, rms2_root = (Root(nc, m, k, TILES) for k in ("ln", "rms1", "rms2"))
        head_root = Root(nc, m, "head", TILES * heads)
        front_root_link = m.counted("front_root_link", 21)
        small_loaded = m.sem("small_loaded")
        zeroed = m.sem("zeroed")
        masks_made = m.sem("masks_made")
        block = m.begin()
        ident = keep["ident"]

        def rounds(eng, body):
            with eng.Fori(0, B // 2 - 1) as i:
                body(i, True)
            body(B // 2 - 1, False)

        @block.sync
        def _(sp):
            for ln in lanes:
                for signal in (ln.sum_done, ln.y_done, ln.y_stored):
                    sp.sem_inc(signal.sem, signal.credit)

            def tokens(name, i, ln):
                return io[name][bass.ds((i * 2 + ln.q) * S, S), :].rearrange("(t p) d -> p t d", p=P)

            def load_input(ln, i):
                sp.dma_start(ln.pre[:], tokens("x2", i, ln)).then_inc(ln.pre_loaded.sem, 16)
                sp.dma_start(ln.rows[:], io["mod_rows"][1, bass.ds(i * 2 + ln.q, 1), 0:2 * D].rearrange("o (r d) -> o r d", r=2).to_broadcast([P, 2, D])
                             ).then_inc(ln.pre_loaded.sem, 16)

            def body(i, more):
                for ln in lanes:
                    wait_apart(sp, ln.y_done.sem, ln.y_done.before(i, 1))
                    wait_apart(sp, ln.o_done.sem, ln.o_done.done(i))
                    sp.dma_start(ln.x[:], tokens("x2", i, ln)).then_inc(ln.x_loaded.sem, 16)
                    sp.dma_start(ln.gate[:, 0], io["mod_rows"][1, bass.ds(i * 2 + ln.q, 1), GA * D:(GA + 1) * D].to_broadcast([P, D])
                                 ).then_inc(ln.x_loaded.sem, 16)
                if more:
                    for ln in lanes:
                        wait_apart(sp, ln.x1_done.sem, ln.x1_done.done(i))
                        load_input(ln, i + 1)
                for ln in lanes:
                    wait_apart(sp, ln.y_done.sem, ln.y_done.after(i, 1))
                    sp.dma_start(tokens("x3", i, ln), ln.t1[:]).then_inc(ln.y_stored.sem, 16)

            for ln in lanes:
                load_input(ln, 0)
            for dst, name in ((low1[:], "gk_w1"), (low2[:], "gk_w2"), (low_bias[:], "gk_b"), (norm_cols[:], "norm_cols")):
                sp.dma_start(dst, io[name]).then_inc(small_loaded, 16)
            sp.dma_start(gnorm[:], io["gnorm"].to_broadcast([P, hv])).then_inc(small_loaded, 16)
            w.load(sp)
            rounds(sp, body)
            for ln in lanes:
                sp.wait_ge(ln.y_stored.sem, ln.y_stored.done(B // 2 - 1))

        @block.gpsimd
        def _(pool):
            for t in (own_head, state_mask, tri, carry, one):
                nc.gpsimd.memset(t[:], 1.0).then_inc(zeroed, 1)
            pool.wait_ge(zeroed, 5)
            nc.gpsimd.memset(carry[:].rearrange("p (c n) -> p c n", c=chunks)[:, :, 0:1], 0.0).then_inc(masks_made, 1)
            for t, pattern in ((own_head[:], [[-hk, heads]]), (state_mask[:].rearrange("p (h n) -> p h n", h=heads), [[-hk, heads], [0, hv]])):
                nc.gpsimd.affine_select(out=t, in_=t, compare_op=ALU.is_ge, fill=0.0, base=0, pattern=pattern,
                                        channel_multiplier=1).then_inc(masks_made, 1)
            pool.wait_ge(masks_made, 3)
            for t, pattern in ((own_head[:], [[hk, heads]]), (state_mask[:].rearrange("p (h n) -> p h n", h=heads), [[hk, heads], [0, hv]])):
                nc.gpsimd.affine_select(out=t, in_=t, compare_op=ALU.is_ge, fill=0.0, base=hk - 1, pattern=pattern,
                                        channel_multiplier=-1).then_inc(masks_made, 1)
            for n in range(2):
                t = tri[n * chunk:(n + 1) * chunk, :]
                pool.wait_ge(masks_made, 5 + n)
                nc.gpsimd.affine_select(out=t, in_=t, compare_op=ALU.is_ge, fill=0.0, base=0, pattern=[[1, chunk]],
                                        channel_multiplier=-1).then_inc(masks_made, 1)
            pool.wait_ge(masks_made, 7)
            pool.wait_ge(small_loaded, 80)

            def spread_queries(ln, i, t):
                if t == 0:
                    pool.wait_ge(ln.qk_used.sem, ln.qk_used.done(i))
                if t >= 2:
                    pool.wait_ge(ln.a_done.sem, ln.a_done.after(i, t - 1))
                for c in range(2):
                    at = slice(t * P + c * chunk, t * P + (c + 1) * chunk)
                    src = ln.qe[:, at].rearrange("p (o n) -> p o n", o=1).to_broadcast([P, heads, chunk])
                    own = own_head[:].rearrange("p (h o) -> p h o", o=1).to_broadcast([P, heads, chunk])
                    ins = nc.gpsimd.tensor_tensor(ln.qx[t % 2][:, c], src, own, ALU.mult)
                ins.then_inc(ln.qx_done.sem, 1)

            def scale_gate(ln, i):
                pool.wait_ge(ln.silu_done.sem, ln.silu_done.done(i))
                g = ln.gs.rearrange("p t n -> p (t n)").rearrange("p (a v) -> p a v", v=hv)
                by = gnorm[:].rearrange("p (o v) -> p o v", o=1).to_broadcast([P, TILES * heads, hv])
                nc.gpsimd.tensor_tensor(g, g, by, ALU.mult).then_inc(ln.gs_done.sem, 1)

            def modulate(ln, i):
                pool.wait_ge(ln.normed.sem, ln.normed.done(i))
                nc.gpsimd.tensor_tensor(ln.pre[:], ln.pre[:], ln.rows[:, 1:2, :].to_broadcast([P, TILES, D]), ALU.mult).then_inc(ln.scaled.sem, 1)
                pool.wait_ge(ln.scaled.sem, ln.scaled.done(i))
                nc.gpsimd.tensor_tensor(ln.pre[:], ln.pre[:], ln.rows[:, 0:1, :].to_broadcast([P, TILES, D]), ALU.add).then_inc(ln.h0_done.sem, 1)

            def act_low(ln, i, c):
                pool.wait_ge(ln.fh_done.sem, ln.fh_done.after(i, c + 1))
                src = ln.t1[:].rearrange("p t d -> p (t d)")[:, (c % 2) * 512:(c % 2 + 1) * 512]
                nc.gpsimd.tensor_tensor(ln.act[1][:, c % 2, :], src, ln.act[0][:, c % 2, :].bitcast(F32), ALU.subtract).then_inc(ln.fl_done.sem, 1)

            def last_sum(ln, i):
                pool.wait_ge(ln.sum_done.sem, ln.sum_done.done(i))
                pool.wait_ge(ln.x_loaded.sem, ln.x_loaded.done(i))
                gate = ln.gate[:].to_broadcast([P, TILES, D])
                nc.gpsimd.tensor_tensor(ln.t1[:], ln.t1[:], gate, ALU.mult).then_inc(ln.plink.sem, 1)
                pool.wait_ge(ln.plink.sem, ln.plink.done(i))
                nc.gpsimd.tensor_tensor(ln.t1[:], ln.t1[:], ln.x[:], ALU.add).then_inc(ln.y_done.sem, 1)

            w.split_low_by_pool(pool)

            def body(i, more):
                for t in range(TILES):
                    for ln in lanes:
                        spread_queries(ln, i, t)
                for ln in lanes:
                    scale_gate(ln, i)
                for c in range(ki):
                    for ln in lanes:
                        act_low(ln, i, c)
                    if more and c in (2, 3):
                        modulate(lanes[c - 2], i + 1)
                for ln in lanes:
                    last_sum(ln, i)

            rounds(pool, body)

        @block.tensor
        def _(pe):
            def turn(ln, src):
                return transpose_rows(nc, ln.X, src, ident)

            def inputs(ln, i, ready, src=None):
                pe.wait_ge(ready.sem, ready.done(i))
                turn(ln, src or ln.t1).then_inc(ln.in_psum.sem, 1)

            def projections(ln, i):
                pe.wait_ge(ln.whole_done.sem, ln.whole_done.after(i, 1))
                for k in range(KD):
                    mm = nc.tensor.matmul(ln.X[0:rank, 0, :], low1[:, k, :], ln.turned[:, k, :], start=(k == 0), stop=(k == KD - 1))
                mm.then_inc(ln.low_done.sem, 1)
                pe.wait_ge(ln.ht_ready.sem, ln.ht_ready.after(i, 1))
                pe.wait_ge(w.ready, w.count("g_k"))
                pe.wait_ge(ln.sum_done.sem, ln.sum_done.before(i, 1))
                for n, name in enumerate(("g_q", "g_k")):
                    for k in range(KD):
                        mm = products(nc, ln.Y[:, n, :], w.part(name, k * keys, (k + 1) * keys),
                                      (ln.hT[0][:, k, :], ln.hT[1][:, k, :]), k == 0, k == KD - 1)
                mm.then_inc(ln.qk_done.sem, 1)

            def decay_logits(ln, i):
                pe.wait_ge(ln.low_copied.sem, ln.low_copied.done(i))
                nc.tensor.matmul(ln.X[:, 1, :], low2[:], ln.low, start=True, stop=True).then_inc(ln.gk_done.sem, 1)

            def values_gates(ln, i, t):
                if t == 0:
                    pe.wait_ge(w.ready, w.count("g_vg"))
                elif t == 1:
                    pe.wait_ge(ln.min_done.sem, ln.min_done.done(i))
                if t >= 2:
                    pe.wait_ge(ln.vg_used.sem, ln.vg_used.after(i, t - 1))
                at = slice(t * P, (t + 1) * P)
                for k in range(KD):
                    mm = products(nc, ln.X[:, t % 2, :], (ln.hT[0][:, k, at], ln.hT[1][:, k, at]),
                                  w.part("g_vg", k * 512, (k + 1) * 512), k == 0, k == KD - 1)
                mm.then_inc(ln.vg_done.sem, 1)

            def keys_by_token(ln, i):
                pe.wait_ge(ln.qk_used.sem, ln.qk_used.done(i))
                pe.wait_ge(ln.vg_used.sem, ln.vg_used.done(i))
                for t in range(TILES):
                    mm = nc.tensor.transpose(ln.X[:, 0, t * P:(t + 1) * P], ln.kd[:, t * P:(t + 1) * P], ident[:])
                mm.then_inc(ln.kd_done.sem, 1)

            def chunk_products(ln, i, t):
                pe.wait_ge(ln.qx_done.sem, ln.qx_done.after(i, t + 1))
                if t >= 2:
                    pe.wait_ge(ln.a_used.sem, ln.a_used.after(i, t - 1))
                elif t == 1:
                    pe.wait_ge(ln.kd_copied.sem, ln.kd_copied.done(i))
                for c in range(2):
                    at = slice(t * P + c * chunk, t * P + (c + 1) * chunk)
                    mm = nc.tensor.matmul(ln.X[c * chunk:(c + 1) * chunk, 1 - t % 2, :], ln.ke[:, at],
                                          ln.qx[t % 2][:, c].rearrange("p h n -> p (h n)"), start=True, stop=True, skip_group_check=True)
                mm.then_inc(ln.a_done.sem, 1)

            def state_updates(ln, i, n):
                if n == 0:
                    pe.wait_ge(ln.kd_copied.sem, ln.kd_copied.done(i))
                else:
                    pe.wait_ge(ln.u_used.sem, ln.u_used.after(i, 1))
                for c in range(4 * n, min(4 * n + 4, chunks - 1)):
                    at = slice((c % 2) * chunk, (c % 2 + 1) * chunk)
                    mm = nc.tensor.matmul(ln.Yt[:, (c % 2) * 2 + c // 2 % 2, :], ln.kd_tok[at, c // 2, :], ln.v[at, c // 2, :], start=True, stop=True)
                mm.then_inc(ln.u_done.sem, 1)

            def outputs(ln, i, lo, hi):
                if lo == 0:
                    pe.wait_ge(ln.state_done.sem, ln.state_done.done(i))
                    pe.wait_ge(ln.a_used.sem, ln.a_used.done(i))
                for c in range(lo, hi):
                    t = c // 2
                    at = slice((c % 2) * chunk, (c % 2 + 1) * chunk)
                    nc.tensor.matmul(ln.Yt[at, t, :], ln.qe[:, c * chunk:(c + 1) * chunk], ln.state[:, c, :],
                                     start=True, stop=False, skip_group_check=True)
                    for h in range(heads):
                        mm = nc.tensor.matmul(ln.Yt[at, t, h * hv:(h + 1) * hv], ln.a[at, t, h * chunk:(h + 1) * chunk],
                                              ln.v[at, t, h * hv:(h + 1) * hv], start=False, stop=(h == heads - 1), skip_group_check=True)
                if hi == chunks:
                    mm.then_inc(ln.o_done.sem, 1)

            def project_out(ln, i):
                pe.wait_ge(ln.ot_ready.sem, ln.ot_ready.done(i))
                pe.wait_ge(w.ready, w.count("g_o"))
                for t in range(TILES):
                    at = slice(t * P, (t + 1) * P)
                    for k in range(KD):
                        mm = products(nc, ln.Yt[:, t, :], (ln.hT[0][:, k, at], ln.hT[1][:, k, at]),
                                      w.part("g_o", k * D, (k + 1) * D), k == 0, k == KD - 1)
                mm.then_inc(ln.wo_done.sem, 1)

            def gate_up(ln, i, c):
                if c == 0:
                    pe.wait_ge(ln.ht_ready.sem, ln.ht_ready.done(i))
                    pe.wait_ge(w.ready_by_pool, w.count("g_up"))
                else:
                    pe.wait_ge(ln.f_done.sem, ln.f_done.after(i, c))
                for g, name in enumerate(("g_gate", "g_up")):
                    for k in range(KD):
                        col = k * inner + c * P
                        mm = products(nc, ln.X[:, g, :], w.part(name, col, col + P),
                                      (ln.hT[0][:, k, :], ln.hT[1][:, k, :]), k == 0, k == KD - 1)
                mm.then_inc(ln.gu_done.sem, 1)

            def down(ln, i, c):
                pe.wait_ge(ln.fl_done.sem, ln.fl_done.after(i, c + 1))
                if c == 0:
                    pe.wait_ge(w.ready_by_pool, w.count("g_down"))
                for t in range(TILES):
                    at = slice(t * P, (t + 1) * P)
                    for n, (x, y) in enumerate(((0, 0), (0, 1), (1, 0))):
                        mm = nc.tensor.matmul(ln.Yt[:, t, :], ln.act[x][:, c % 2, at], w.part("g_down", c * D, (c + 1) * D)[y],
                                              start=(c == 0 and t % 2 == 0 and n == 0), stop=(c == ki - 1 and n == 2), skip_group_check=True)
                mm.then_inc(ln.down_done.sem, 1)

            pe.wait_ge(small_loaded, 80)
            for ln in lanes:
                inputs(ln, 0, ln.hn_done, ln.hn)

            def body(i, more):
                for ln in lanes:
                    projections(ln, i)
                for ln in lanes:
                    decay_logits(ln, i)
                for t in range(TILES):
                    for ln in lanes:
                        values_gates(ln, i, t)
                for ln in lanes:
                    keys_by_token(ln, i)
                for ln in lanes:
                    chunk_products(ln, i, 0)
                for ln in lanes:
                    state_updates(ln, i, 0)
                for ln in lanes:
                    chunk_products(ln, i, 1)
                for ln in lanes:
                    state_updates(ln, i, 1)
                for t in range(2, TILES):
                    for ln in lanes:
                        chunk_products(ln, i, t)
                ahead, behind = lanes
                outputs(ahead, i, 0, chunks)
                outputs(behind, i, 0, chunks // 2)
                inputs(ahead, i, ahead.on_done)
                outputs(behind, i, chunks // 2, chunks // 2 + 2)
                project_out(ahead, i)
                outputs(behind, i, chunks // 2 + 2, chunks)
                inputs(behind, i, behind.on_done)
                inputs(ahead, i, ahead.h2_done)
                project_out(behind, i)
                gate_up(ahead, i, 0)
                inputs(behind, i, behind.h2_done)
                gate_up(behind, i, 0)

                def next_inputs(ln):
                    if more:
                        pe.wait_ge(ln.f_done.sem, ln.f_done.done(i))
                        inputs(ln, i + 1, ln.hn_done, ln.hn)

                for c in range(1, ki):
                    for ln in lanes:
                        gate_up(ln, i, c)
                        if c == ki - 1 and ln.q == 1:
                            next_inputs(lanes[0])
                        down(ln, i, c - 1)
                next_inputs(lanes[1])
                for ln in lanes:
                    down(ln, i, ki - 1)

            rounds(pe, body)

        @block.scalar
        def _(act):
            def squares(ln, i, src, ready, done):
                act.wait_ge(ready.sem, ready.done(i))
                for t in range(TILES):
                    ins = nc.scalar.activation(ln.t3[:, t * D:(t + 1) * D], src[:, t, :], ACT.Square, accum_out=ln.sq[:, t:t + 1])
                ins.then_inc(done.sem, 1)

            def whole(ln, i, n):
                act.wait_ge(ln.in_psum.sem, ln.in_psum.after(i, n))
                out = ln.turned if n == 1 else ln.whole
                for k in range(KD):
                    ins = nc.scalar.activation(out[:, k, :], ln.X[:, k, :], ACT.Copy, scale=norm_cols[:, n // 2, k:k + 1])
                ins.then_inc(ln.whole_done.sem, 1)

            def copy_low(ln, i):
                act.wait_ge(ln.low_done.sem, ln.low_done.done(i))
                nc.scalar.activation(ln.low, ln.X[0:rank, 0, :], ACT.Copy).then_inc(ln.low_copied.sem, 1)

            def decay_logs(ln, i):
                act.wait_ge(ln.gk_done.sem, ln.gk_done.done(i))
                ins = nc.scalar.activation(ln.enb, ln.X[:, 1, :], ACT.Abs, bias=low_bias[:])
                ins.then_inc(ln.abs_done.sem, 1)

            def decay_exps(ln, i):
                act.wait_ge(ln.abs_done.sem, ln.abs_done.done(i))
                nc.scalar.activation(ln.enb, ln.enb, ACT.Exp, scale=-1.0).then_inc(ln.alink.sem, 1)

            def decay_lns(ln, i):
                act.wait_ge(ln.alink.sem, ln.alink.done(i))
                nc.scalar.activation(ln.enb, ln.enb, ACT.Ln, bias=one[:]).then_inc(ln.zl_done.sem, 1)

            def decays(ln, i):
                act.wait_ge(ln.scan_done.sem, ln.scan_done.done(i))
                nc.scalar.activation(ln.eb, ln.bs, ACT.Exp, scale=1.0 / gate_norm)
                nc.scalar.activation(ln.enb, ln.bs, ACT.Exp, scale=-1.0 / gate_norm)
                nc.scalar.activation(ln.g, ln.g, ACT.Exp, scale=1.0 / gate_norm).then_inc(ln.exps_done.sem, 1)

            def values_gates(ln, i, t):
                act.wait_ge(ln.vg_done.sem, ln.vg_done.after(i, t + 1))
                if t == 0:
                    act.wait_ge(w.ready_by_pool, w.count("g_down"))
                    act.wait_ge(ln.y_done.sem, ln.y_done.before(i, 1))
                nc.scalar.activation(ln.vg[:, :, t, :], ln.X[:, t % 2, :].rearrange("p (h n) -> p h n", h=2), ACT.Copy).then_inc(ln.vg_used.sem, 1)

            def silu_of_gates(ln, i):
                act.wait_ge(ln.vg_used.sem, ln.vg_used.done(i))
                nc.scalar.activation(ln.gs, ln.gs, ACT.Silu).then_inc(ln.silu_done.sem, 1)

            def copy_keys(ln, i):
                act.wait_ge(ln.kd_done.sem, ln.kd_done.done(i))
                nc.scalar.activation(ln.kd_tok, ln.X[:, 0, :].rearrange("p (t n) -> p t n", t=TILES), ACT.Copy).then_inc(ln.kd_copied.sem, 1)

            def head_squares(ln, i):
                act.wait_ge(ln.o_done.sem, ln.o_done.done(i))
                nc.scalar.activation(ln.t2[:].rearrange("p (w n) -> p w n", w=2), ln.Y[:], ACT.Square).then_inc(ln.sq2.sem, 1)

            def out_high(ln, i):
                act.wait_ge(ln.in_psum.sem, ln.in_psum.after(i, 2))
                nc.scalar.activation(ln.hT[0][:], ln.X[:], ACT.Copy).then_inc(ln.ot_high.sem, 1)

            def activate(ln, i, c):
                act.wait_ge(ln.gu_done.sem, ln.gu_done.after(i, c + 1))
                at = slice((c % 2) * 512, (c % 2 + 1) * 512)
                nc.scalar.activation(ln.t2[:, at], ln.X[:, 0, :], ACT.Silu).then_inc(ln.sg_done.sem, 1)

            def act_high(ln, i, c):
                act.wait_ge(ln.f_done.sem, ln.f_done.after(i, c + 1))
                if c >= 2:
                    act.wait_ge(ln.down_done.sem, ln.down_done.after(i, c - 1))
                src = ln.t1[:].rearrange("p t d -> p (t d)")[:, (c % 2) * 512:(c % 2 + 1) * 512]
                nc.scalar.activation(ln.act[0][:, c % 2, :], src, ACT.Copy).then_inc(ln.fh_done.sem, 1)

            w.split_high(act, "g_q", "g_vg")
            act.wait_ge(small_loaded, 80)
            act.wait_ge(masks_made, 7)
            for ln in lanes:
                squares(ln, 0, ln.pre, ln.h0_done, ln.sq1)
            w.split_high(act, "g_o", "g_down")

            def body(i, more):
                for ln in lanes:
                    whole(ln, i, 1)
                for ln in lanes:
                    copy_low(ln, i)
                for step in (decay_logs, decay_exps, decay_lns):
                    for ln in lanes:
                        step(ln, i)
                for ln in lanes:
                    values_gates(ln, i, 0)
                for ln in lanes:
                    decays(ln, i)
                for t in range(1, TILES):
                    for ln in lanes:
                        values_gates(ln, i, t)
                for ln in lanes:
                    copy_keys(ln, i)
                for ln in lanes:
                    silu_of_gates(ln, i)
                ahead, behind = lanes
                head_squares(ahead, i)
                out_high(ahead, i)
                head_squares(behind, i)
                squares(ahead, i, ahead.h0, ahead.x1_done, ahead.sq3)
                out_high(behind, i)
                whole(ahead, i, 3)
                squares(behind, i, behind.h0, behind.x1_done, behind.sq3)
                whole(behind, i, 3)
                for c in range(ki):
                    for ln in lanes:
                        activate(ln, i, c)
                    for ln in lanes:
                        act_high(ln, i, c)
                    if c in (3, 4) and more:
                        ln = lanes[c - 3]
                        squares(ln, i + 1, ln.pre, ln.h0_done, ln.sq1)

            rounds(act, body)

        @block.vector
        def _(dve):
            def links_of(signal, i):
                count = [0]

                def link(ins, wait=wait_on):
                    count[0] += 1
                    ins.then_inc(signal.sem, 1)
                    wait(dve, signal.sem, signal.after(i, count[0]))
                return link, count

            def norm(ln, i, link):
                dve.wait_ge(ln.pre_loaded.sem, ln.pre_loaded.done(i))
                return moments_of_rows(nc, link, ln.pre, ln.stats, ln.mv, ln_root.v[:, ln.q])

            def normed_rows(ln):
                norm_rows(nc, ln.pre, ln.pre, ln.mv, ln_root.root[:, ln.q]).then_inc(ln.normed.sem, 1)

            def root_norm(ln, out, src, root, done):
                for t in range(TILES):
                    ins = nc.vector.tensor_scalar(out[:, t, :], src[:, t, :], root.root[:, ln.q, t:t + 1], None, ALU.mult)
                ins.then_inc(done.sem, 1)

            class Front:

                def __init__(self, i):
                    self.i = i
                    self.links = [links_of(ln.front_link, i) for ln in lanes]
                    self.root_links = links_of(front_root_link, i)

                def moments(self, q):
                    self.links[q][0](norm(lanes[q], self.i, self.links[q][0]))

                def norm_root(self):
                    ln_root.solve(self.root_links[0])

                def norms(self):
                    for ln in lanes:
                        normed_rows(ln)

                def root(self):
                    for ln in lanes:
                        dve.wait_ge(ln.sq1.sem, ln.sq1.done(self.i))
                        ins = nc.vector.tensor_scalar(rms1_root.v[:, ln.q], ln.sq[:], 1.0 / D, rms_eps, ALU.mult, ALU.add)
                    self.root_links[0](ins)
                    rms1_root.solve(self.root_links[0])

                def root_norm(self, q):
                    root_norm(lanes[q], lanes[q].hn, lanes[q].pre, rms1_root, lanes[q].hn_done)
                    if q:
                        assert [c[0] for _, c in self.links] == [3, 3] and self.root_links[1][0] == front_root_link.per, self.root_links[1]

            def halve(ln, i, n):
                src = ln.turned if n == 1 else ln.whole
                dve.wait_ge(ln.whole_done.sem, ln.whole_done.after(i, n))
                nc.vector.tensor_copy(ln.hT[0][:], src).then_inc(ln.ht_link.sem, 1)
                dve.wait_ge(ln.ht_link.sem, ln.ht_link.after(i, n))
                low(nc, ln.hT[1][:], src, ln.hT[0][:]).then_inc(ln.ht_ready.sem, 1)

            def decay_minima(ln, i):
                dve.wait_ge(ln.abs_done.sem, ln.abs_done.done(i))
                nc.vector.tensor_scalar(ln.g, ln.X[:, 1, :], low_bias[:, 0:1], 0.0, ALU.add, ALU.min).then_inc(ln.min_done.sem, 1)

            def decay_sums(ln, i, link):
                dve.wait_ge(ln.min_done.sem, ln.min_done.done(i))
                dve.wait_ge(ln.zl_done.sem, ln.zl_done.done(i))
                link(nc.vector.tensor_tensor(ln.g, ln.g, ln.enb, ALU.subtract))
                link(nc.vector.tensor_tensor_scan(ln.bs, carry[:], ln.g, 0.0, ALU.mult, ALU.add))
                b3 = ln.bs.rearrange("p (c n) -> p c n", c=chunks)
                ends = b3[:, :, chunk - 1:chunk].to_broadcast([P, chunks, chunk])
                nc.vector.tensor_tensor(ln.g.rearrange("p (c n) -> p c n", c=chunks), ends, b3, ALU.subtract).then_inc(ln.scan_done.sem, 1)

            def decay_queries_keys(ln, i):
                dve.wait_ge(ln.exps_done.sem, ln.exps_done.done(i))
                dve.wait_ge(w.ready_by_pool, w.count("g_down"))
                dve.wait_ge(ln.qk_done.sem, ln.qk_done.done(i))
                nc.vector.scalar_tensor_tensor(ln.qe, ln.Y[:, 0, :], hk ** -0.5, ln.eb, ALU.mult, ALU.mult)
                nc.vector.tensor_tensor(ln.ke, ln.Y[:, 1, :], ln.enb, ALU.mult)
                nc.vector.tensor_tensor(ln.kd, ln.Y[:, 1, :], ln.g, ALU.mult)
                nc.vector.tensor_copy(ln.ebl[:], ln.eb.rearrange("p (c n) -> p c n", c=chunks)[:, :, chunk - 1]).then_inc(ln.qk_used.sem, 1)

            def masked(ln, i, t):
                if t == 0:
                    dve.wait_ge(ln.qk_used.sem, ln.qk_used.done(i))
                dve.wait_ge(ln.a_done.sem, ln.a_done.after(i, t + 1))
                src = ln.X[:, 1 - t % 2, :].rearrange("p (h n) -> p h n", h=heads)
                by = tri[:].rearrange("p (o n) -> p o n", o=1).to_broadcast([P, heads, chunk])
                nc.vector.tensor_tensor(ln.a[:, t, :].rearrange("p (h n) -> p h n", h=heads), src, by, ALU.mult).then_inc(ln.a_used.sem, 1)

            def own_blocks(ln, i, n):
                if n == 0:
                    nc.vector.memset(ln.state[:, 0, :], 0.0)
                dve.wait_ge(ln.u_done.sem, ln.u_done.after(i, n + 1))
                for a in range(2):
                    lo = 4 * n + 2 * a
                    hi = min(lo + 2, chunks - 1)
                    by = state_mask[:].rearrange("p (o n) -> p o n", o=1).to_broadcast([P, hi - lo, vals])
                    src = ln.Y[:, 0:hi - lo, a * vals:(a + 1) * vals]
                    ins = nc.vector.tensor_tensor(ln.state[:, lo + 1:hi + 1, :], src, by, ALU.mult)
                ins.then_inc(ln.u_used.sem, 1)

            def states(ln, i, link, c):
                if c == 1:
                    dve.wait_ge(ln.u_used.sem, ln.u_used.after(i, 2))
                ins = nc.vector.scalar_tensor_tensor(ln.state[:, c + 1, :], ln.state[:, c, :], ln.ebl[:, c:c + 1],
                                                     ln.state[:, c + 1, :], ALU.mult, ALU.add)
                if c < chunks - 2:
                    link(ins)
                else:
                    ins.then_inc(ln.state_done.sem, 1)

            def head_sums(ln, i, link):
                dve.wait_ge(ln.sq2.sem, ln.sq2.done(i))
                link(nc.vector.tensor_reduce(head_root.tmp[:, ln.q], ln.t2[:].rearrange("p (a v) -> p a v", v=hv), AX.X, ALU.add))
                return nc.vector.tensor_scalar(head_root.v[:, ln.q], head_root.tmp[:, ln.q], 1.0 / hv, rms_eps, ALU.mult, ALU.add)

            def gated(ln, i):
                dve.wait_ge(ln.y_stored.sem, ln.y_stored.before(i, 16))
                t1 = ln.t1[:].rearrange("p t d -> p (t d)").rearrange("p (a v) -> p a v", v=hv)
                y = ln.Y[:].rearrange("p w n -> p (w n)").rearrange("p (a v) -> p a v", v=hv)
                by = head_root.root[:, ln.q].rearrange("p (a o) -> p a o", o=1).to_broadcast([P, TILES * heads, hv])
                nc.vector.tensor_tensor(t1, y, by, ALU.mult).then_inc(ln.o_used.sem, 1)
                dve.wait_ge(ln.o_used.sem, ln.o_used.done(i))
                dve.wait_ge(ln.gs_done.sem, ln.gs_done.done(i))
                nc.vector.tensor_tensor(ln.t1[:], ln.t1[:], ln.gs, ALU.mult).then_inc(ln.on_done.sem, 1)

            def out_low(ln, i):
                dve.wait_ge(ln.ot_high.sem, ln.ot_high.done(i))
                low(nc, ln.hT[1][:], ln.X[:], ln.hT[0][:]).then_inc(ln.ot_ready.sem, 1)

            def add_out(ln, i):
                dve.wait_ge(ln.wo_done.sem, ln.wo_done.done(i))
                nc.vector.tensor_tensor(ln.h0[:], ln.Yt, ln.pre[:], ALU.add).then_inc(ln.x1_done.sem, 1)

            def hidden(ln, i, c):
                dve.wait_ge(ln.sg_done.sem, ln.sg_done.after(i, c + 1))
                if c >= 2:
                    dve.wait_ge(ln.fl_done.sem, ln.fl_done.after(i, c - 1))
                elif c == 0:
                    dve.wait_ge(ln.ht_ready.sem, ln.ht_ready.after(i, 2))
                at = slice((c % 2) * 512, (c % 2 + 1) * 512)
                nc.vector.tensor_tensor(ln.t1[:].rearrange("p t d -> p (t d)")[:, at], ln.t2[:, at], ln.X[:, 1, :], ALU.mult).then_inc(ln.f_done.sem, 1)

            def sum_up(ln, i):
                dve.wait_ge(ln.down_done.sem, ln.down_done.done(i))
                dve.wait_ge(ln.fl_done.sem, ln.fl_done.done(i))
                nc.vector.tensor_tensor(ln.t1[:], ln.Yt, ln.h0[:], ALU.add).then_inc(ln.sum_done.sem, 1)

            front = Front(0)
            for q in range(2):
                front.moments(q)
            front.norm_root()
            front.norms()
            for ln in lanes:
                dve.wait_ge(ln.normed.sem, ln.normed.done(0))
                nc.vector.tensor_tensor(ln.pre[:], ln.pre[:], ln.rows[:, 1:2, :].to_broadcast([P, TILES, D]), ALU.mult).then_inc(ln.scaled.sem, 1)
                dve.wait_ge(ln.scaled.sem, ln.scaled.done(0))
                nc.vector.tensor_tensor(ln.pre[:], ln.pre[:], ln.rows[:, 0:1, :].to_broadcast([P, TILES, D]), ALU.add).then_inc(ln.h0_done.sem, 1)
            w.split_low(dve, "g_q", "g_vg")
            front.root()
            for q in range(2):
                front.root_norm(q)
            w.split_low(dve, "g_o", "g_down")
            dve.wait_ge(small_loaded, 80)
            dve.wait_ge(masks_made, 7)


            def body(i, more):
                made = [links_of(ln.link, i) for ln in lanes]
                both = [(ln, made[ln.q][0]) for ln in lanes]
                for ln in lanes:
                    halve(ln, i, 1)
                for ln in lanes:
                    decay_minima(ln, i)
                for ln, link in both:
                    decay_sums(ln, i, link)
                for ln in lanes:
                    decay_queries_keys(ln, i)
                for ln in lanes:
                    masked(ln, i, 0)
                for ln in lanes:
                    own_blocks(ln, i, 0)
                for ln in lanes:
                    masked(ln, i, 1)
                for ln in lanes:
                    own_blocks(ln, i, 1)
                for ln, link in both:
                    for c in range(1, chunks - 1):
                        states(ln, i, link, c)
                    for t in range(2, TILES):
                        masked(ln, i, t)

                def head_norm(ln, link):
                    link(head_sums(ln, i, link))
                    head_root.solve(link, slice(ln.q, ln.q + 1))
                    gated(ln, i)

                def second_norm(ln, link):
                    dve.wait_ge(ln.sq3.sem, ln.sq3.done(i))
                    link(nc.vector.tensor_scalar(rms2_root.v[:, ln.q], ln.sq[:], 1.0 / D, rms_eps, ALU.mult, ALU.add))
                    rms2_root.solve(link, slice(ln.q, ln.q + 1))
                    root_norm(ln, ln.t1, ln.h0, rms2_root, ln.h2_done)

                ahead, behind = both
                head_norm(*ahead)
                out_low(lanes[0], i)
                add_out(lanes[0], i)
                head_norm(*behind)
                second_norm(*ahead)
                out_low(lanes[1], i)
                add_out(lanes[1], i)
                halve(lanes[0], i, 2)
                second_norm(*behind)
                halve(lanes[1], i, 2)
                if more:
                    front = Front(i + 1)
                for c in range(ki):
                    for ln in lanes:
                        hidden(ln, i, c)
                        if more and c == 1:
                            front.moments(ln.q)
                        if more and (c, ln.q) == (2, 0):
                            front.norm_root()
                        if more and (c, ln.q) == (2, 1):
                            front.norms()
                        if more and (c, ln.q) == (4, 1):
                            front.root()
                        if more and c == ki - 1:
                            front.root_norm(ln.q)
                for ln in lanes:
                    sum_up(ln, i)
                for ln in lanes:
                    assert made[ln.q][1][0] == ln.link.per, made[ln.q][1][0]

            rounds(dve, body)
        m.end()


def sparse_ffn_stage(nc, io, keep):
    inner = 1024
    halves = inner // 512
    groups = inner // 4
    ki = inner // P
    with ExitStack() as ctx:
        m = Alloc(nc, ctx, "spf")
        entries = [("sp_gate", KD * inner), ("sp_up", KD * inner), ("sp_down", ki * D)]
        raw = m.sb("raw", [P, sum(n for _, n in entries)])
        w = SplitWeights(nc, m, io, entries, raw, ())
        silu = m.sb("silu", [P, 2, inner])
        hid = m.sb("hid", [P, TILES, inner])
        mag = m.sb("mag", [P, 2, inner])
        lead = m.sb("lead", [P, 2, 3, 2, groups])
        wins = m.sb("wins", [P, 3, 2, groups], BF16)
        sums = m.sb("sums", [P, 4, groups], BF16)
        margin = m.sb("margin", [P, 4, groups], BF16)
        kept = m.sb("kept", [P, inner])
        keptT = [m.sb(f"keptT{i}", [P, ki, P], F32R) for i in "hl"]
        y = m.sb("y", [P, TILES, D])
        gu = m.ps("gu", [P, 2, 2, 512])
        tp = m.ps("tp", [P, 2, 512])
        o_ps = m.ps("o_ps", [P, TILES, D])
        link_t = m.counted("link_t", 2)
        gu_done = m.counted("gu_done", 2)
        silu_done = m.counted("silu_done", 2)
        hid_done = m.counted("hid_done", 2, credit=2)
        mag_done = m.counted("mag_done", 1)
        looked = m.counted("looked", 1, credit=2)
        compared = m.counted("compared", 1, credit=2)
        kept_done = m.counted("kept_done", 1)
        kt_done = m.counted("kt_done", 2)
        kt_high = m.counted("kt_high", 2)
        kt_low = m.counted("kt_low", 2, credit=2)
        o_done = m.counted("o_done", 1)
        link_y = m.counted("link_y", 1)
        y_done = m.counted("y_done", 1, credit=1)
        y_stored = m.counted("y_stored", 16, credit=16)

        xin = NormedInput(nc, m, io, keep, "x3", 1, CB, SB, tp, lambda pe, b: None)
        block = m.begin()

        @block.sync
        def _(sp):
            sp.sem_inc(xin.normed.sem, xin.normed.credit)
            sp.sem_inc(hid_done.sem, hid_done.credit)
            sp.sem_inc(compared.sem, compared.credit)
            sp.sem_inc(looked.sem, looked.credit)
            sp.sem_inc(kt_low.sem, kt_low.credit)
            sp.sem_inc(y_done.sem, y_done.credit)
            sp.sem_inc(y_stored.sem, y_stored.credit)
            xin.load(sp, 0)
            w.load(sp)

            def body(b, q, first, last):
                if not last:
                    xin.load(sp, b + 1)
                if not first:
                    store(b - 1)
                xin.load_residual(sp, b, GB)

            def store(b):
                wait_apart(sp, y_done.sem, y_done.after(b, 1))
                sp.dma_start(io["out_rows"][bass.ds(b * S, S), :].rearrange("(t p) d -> p t d", p=P), y[:]).then_inc(y_stored.sem, 16)

            in_batches(sp, body)
            store(B - 1)
            sp.wait_ge(y_stored.sem, y_stored.after(B - 1, 16))

        @block.gpsimd
        def _(pool):
            def body(b, q, first, last):
                for t in range(TILES):
                    n = b * TILES + t
                    pool.wait_ge(mag_done.sem, mag_done.after(n, 1))
                    pool.wait_ge(looked.sem, looked.before(n, 1, back=2))
                    s = t % 2
                    a = mag[:, s].rearrange("p (g e) -> p e g", e=4)
                    nc.gpsimd.tensor_tensor(lead[:, s, 0], a[:, 0:4:2, :], a[:, 1:4:2, :], ALU.subtract)
                    nc.gpsimd.tensor_tensor(lead[:, s, 1], a[:, 0:2, :], a[:, 2:4, :], ALU.subtract)
                    nc.gpsimd.tensor_tensor(lead[:, s, 2, 0, :], a[:, 0, :], a[:, 3, :], ALU.subtract)
                    ins = nc.gpsimd.tensor_tensor(lead[:, s, 2, 1, :], a[:, 1, :], a[:, 2, :], ALU.subtract)
                    ins.then_inc(compared.sem, 1)

            in_batches(pool, body)

        @block.tensor
        def _(pe):
            def gate_up(n, t, q, c):
                pe.wait_ge(hid_done.sem, hid_done.before(n, c + 1))
                for g, name in enumerate(("sp_gate", "sp_up")):
                    for k in range(KD):
                        at = slice(t * P, (t + 1) * P)
                        col = k * inner + c * 512
                        mm = products(nc, gu[:, c, g, :], (xin.hT[q][0][:, k, at], xin.hT[q][1][:, k, at]),
                                      w.part(name, col, col + 512), k == 0, k == KD - 1)
                mm.then_inc(gu_done.sem, 1)

            def turn_kept(n):
                pe.wait_ge(kept_done.sem, kept_done.after(n, 1))
                for c in range(2):
                    for j in range(4):
                        at = (c * 4 + j) * P
                        mm = nc.tensor.transpose(tp[:, c, j * P:(j + 1) * P], kept[:, at:at + P], keep["ident"][:])
                    mm.then_inc(kt_done.sem, 1)

            def down(n, t):
                pe.wait_ge(w.ready, w.count("sp_down"))
                for k in range(ki):
                    if k % 4 == 0:
                        pe.wait_ge(kt_low.sem, kt_low.after(n, k // 4 + 1))
                    mm = products(nc, o_ps[:, t, :], (keptT[0][:, k, :], keptT[1][:, k, :]),
                                  w.part("sp_down", k * D, (k + 1) * D), k == 0, k == ki - 1)
                if t == TILES - 1:
                    mm.then_inc(o_done.sem, 1)

            def body(b, q, first, last):
                for t in range(TILES):
                    n = b * TILES + t
                    if t == 0:
                        pe.wait_ge(xin.ready.sem, xin.ready.after(b, 1))
                    gate_up(n, t, q, 0)
                    if t == 3:
                        pe.wait_ge(y_done.sem, y_done.before(b, 1))
                    if t == 3 or not first:
                        down(n - 3, (t + 1) % TILES)
                    if t == 2 and not last:
                        xin.transpose(pe, b + 1)
                    gate_up(n, t, q, 1)
                    if t == 2 and not last:
                        pe.wait_ge(xin.whole.sem, xin.whole.after(b + 1, 1))
                    if t >= 2 or not first:
                        turn_kept(n - 2)

            xin.transpose(pe, 0)
            pe.wait_ge(w.ready, w.count("sp_up"))
            in_batches(pe, body)
            for n in range(B * TILES, B * TILES + 3):
                down(n - 3, (n - 3) % TILES)
                if n - 2 < B * TILES:
                    turn_kept(n - 2)

        @block.scalar
        def _(act):
            def activate(n, c, t):
                act.wait_ge(gu_done.sem, gu_done.after(n, c + 1))
                nc.scalar.activation(silu[:, t % 2, c * 512:(c + 1) * 512], gu[:, c, 0, :], ACT.Silu).then_inc(silu_done.sem, 1)

            def magnitudes(n, t):
                act.wait_ge(hid_done.sem, hid_done.after(n, 2))
                act.wait_ge(compared.sem, compared.before(n, 1, back=2))
                nc.scalar.activation(mag[:, t % 2], hid[:, t, :], ACT.Abs).then_inc(mag_done.sem, 1)

            def kept_high(n):
                for c in range(2):
                    act.wait_ge(kt_done.sem, kt_done.after(n, c + 1))
                    nc.scalar.activation(keptT[0][:, c * 4:(c + 1) * 4, :], tp[:, c, :].rearrange("p (j n) -> p j n", j=4),
                                         ACT.Copy).then_inc(kt_high.sem, 1)

            def body(b, q, first, last):
                for t in range(TILES):
                    n = b * TILES + t
                    activate(n, 0, t)
                    if t == 2 and not last:
                        xin.modulate(act, b + 1)
                    activate(n, 1, t)
                    if t >= 2 or not first:
                        kept_high(n - 2)
                    magnitudes(n, t)

            xin.modulate(act, 0)
            w.split_high(act, "sp_gate", "sp_down")
            in_batches(act, body)
            for n in range(B * TILES - 2, B * TILES):
                kept_high(n)

        @block.vector
        def _(dve):
            def hidden(n, c, t):
                dve.wait_ge(silu_done.sem, silu_done.after(n, c + 1))
                at = slice(c * 512, (c + 1) * 512)
                nc.vector.tensor_tensor(hid[:, t, at], silu[:, t % 2, at], gu[:, c, 1, :], ALU.mult).then_inc(hid_done.sem, 1)

            def kept_low(n):
                for c in range(2):
                    dve.wait_ge(kt_high.sem, kt_high.after(n, c + 1))
                    at = slice(c * 4, (c + 1) * 4)
                    low(nc, keptT[1][:, at, :], tp[:, c, :].rearrange("p (j n) -> p j n", j=4), keptT[0][:, at, :]).then_inc(kt_low.sem, 1)

            def choose(n, t):
                dve.wait_ge(compared.sem, compared.after(n, 1))
                nc.vector.tensor_scalar(wins[:], lead[:, t % 2], 0.0, None, ALU.is_ge).then_inc(looked.sem, 1)
                dve.wait_ge(looked.sem, looked.after(n, 1))
                x, y_, z = (wins[:, i] for i in range(3))
                nc.vector.tensor_tensor(sums[:, 0:2, :], y_, z, ALU.add)
                nc.vector.tensor_tensor(sums[:, 2, :], y_[:, 0, :], z[:, 1, :], ALU.add)
                nc.vector.scalar_tensor_tensor(sums[:, 3, :], y_[:, 1, :], -1.0, z[:, 0, :], ALU.mult, ALU.subtract).then_inc(link_t.sem, 1)
                dve.wait_ge(link_t.sem, link_t.after(n, 1))
                nc.vector.scalar_tensor_tensor(margin[:, 0, :], sums[:, 0, :], -2.0, x[:, 0, :], ALU.add, ALU.add)
                nc.vector.scalar_tensor_tensor(margin[:, 1, :], sums[:, 1, :], -1.0, x[:, 0, :], ALU.add, ALU.subtract)
                nc.vector.tensor_tensor(margin[:, 2, :], x[:, 1, :], sums[:, 2, :], ALU.subtract)
                nc.vector.scalar_tensor_tensor(margin[:, 3, :], sums[:, 3, :], 1.0, x[:, 1, :], ALU.add, ALU.subtract).then_inc(link_t.sem, 1)
                dve.wait_ge(link_t.sem, link_t.after(n, 2))
                nc.vector.scalar_tensor_tensor(kept[:].rearrange("p (g e) -> p e g", e=4), margin[:], 0.0,
                                               hid[:, t, :].rearrange("p (g e) -> p e g", e=4), ALU.is_ge, ALU.mult).then_inc(kept_done.sem, 1)

            def residual(b):
                dve.wait_ge(o_done.sem, o_done.after(b, 1))
                dve.wait_ge(xin.residual_loaded.sem, xin.residual_loaded.after(b, 32))
                dve.wait_ge(y_stored.sem, y_stored.before(b, 16))
                rows = xin.gate_row[:].to_broadcast([P, TILES, D])
                nc.vector.tensor_tensor(y[:], o_ps[:], rows, ALU.mult).then_inc(link_y.sem, 1)
                dve.wait_ge(link_y.sem, link_y.after(b, 1))
                nc.vector.tensor_tensor(y[:], y[:], xin.residual[:], ALU.add).then_inc(y_done.sem, 1)

            def body(b, q, first, last):
                for t in range(TILES):
                    n = b * TILES + t
                    hidden(n, 0, t)
                    if t == 3 and not last:
                        xin.halve(dve, b + 1, 1 - q)
                    if t >= 2 or not first:
                        choose(n - 2, (t + 2) % TILES)
                    hidden(n, 1, t)
                    if t >= 2 or not first:
                        kept_low(n - 2)
                    if t == 0 and not last:
                        xin.moments(dve, b + 1)
                    if t == 1 and not last:
                        xin.norm(dve, b + 1)
                    if t == 2 and not first:
                        residual(b - 1)

            xin.moments(dve, 0)
            xin.norm(dve, 0)
            xin.halve(dve, 0, 0)
            w.split_low(dve, "sp_gate", "sp_down")
            in_batches(dve, body)
            for n in range(B * TILES - 2, B * TILES):
                choose(n, n % TILES)
                kept_low(n)
            residual(B - 1)
        m.end()


def build(nc, io, stages="full"):
    with ExitStack() as ctx:
        k = Alloc(nc, ctx, "keep")
        keep = {"ident": k.sb("ident", [P, P]), "causal": k.sb("causal", [P, S]),
                "mod": k.sb("mod", [P, 2, MODS * KD, B])}
        Apart.passed = k.sem("passed")
        keep["raw_loaded"] = [k.counted(f"raw_loaded{n}", 16) for n in range(4)]
        modulation_stage(nc, io, keep)
        if stages in ("full", "a"):
            attention_stage(nc, io, keep)
        if stages in ("full", "b"):
            moe_stage(nc, io, keep)
        if stages in ("full", "c"):
            gla_stage(nc, io, keep)
        if stages in ("full", "d"):
            sparse_ffn_stage(nc, io, keep)


def layout(i):
    import numpy as np
    f = {}
    f["x"] = i["L0_attn_x"].reshape(B * S, D)

    def feature_major(w):
        return w.reshape(NH, DH, KD, P).transpose(3, 0, 2, 1).reshape(P, NH, KD * DH)

    f["wqk"] = np.stack([feature_major(i["L0_attn_W_Q"]), feature_major(i["L0_attn_W_K"])], axis=2)
    f["wv"] = i["L0_attn_W_V"].reshape(PAIRS, 2, DH, KD, P).transpose(4, 0, 3, 1, 2).reshape(P, PAIRS, KD * 2 * DH)
    f["wo"] = i["L0_attn_W_O"].transpose(2, 0, 1).reshape(P, PAIRS, 2 * D)
    for l in range(2):
        f[f"c{l}"] = i[f"L{l}_c"].T.reshape(KD, P, B).transpose(1, 0, 2).reshape(P, KD * B)
        f[f"wmod{l}"] = i[f"L{l}_wmod"]

    def rows(w):
        return w.reshape(-1, P, w.shape[1]).transpose(1, 0, 2).reshape(P, -1)

    for n in ("gate", "up", "down"):
        f[f"sp_{n}"] = rows(i[f"L1_ffn_w_{n}"])
        f[f"ex_{n}"] = rows(i[f"L0_ffn_w_{n}"])
        f[f"sh_{n}"] = rows(i[f"L0_ffn_shared_w_{n}"])
    f["g_q"], f["g_k"], f["g_o"] = (rows(i[f"L1_attn_w{n}"]) for n in "qko")
    f["g_vg"] = rows(np.concatenate([i["L1_attn_wv"], i["L1_attn_wg"]], axis=1))
    wide = 768
    for n in ("gate", "up"):
        f[f"g_{n}"] = rows(np.pad(i[f"L1_attn_w_{n}"], ((0, 0), (0, wide - 704))))
    f["g_down"] = rows(np.pad(i["L1_attn_w_down"], ((0, wide - 704), (0, 0))))
    f["gk_w1"] = rows(i["L1_attn_gk_w1"]).reshape(P, KD, 16)
    f["gk_w2"] = i["L1_attn_gk_w2"]
    f["gk_b"] = i["L1_attn_gk_b"].reshape(P, 1)
    f["norm_cols"] = np.stack([i["L1_attn_norm1_w"].reshape(KD, P).T, i["L1_attn_ffn_norm_w"].reshape(KD, P).T], axis=1)
    f["gnorm"] = i["L1_attn_gnorm_w"].reshape(1, 32)
    f["router"] = rows(i["L0_ffn_w_router"])
    f["amplitudes"] = i["L0_ffn_amplitudes"]
    f["expert_scale"] = i["L0_ffn_expert_scale"].reshape(P, 1)
    return {n: np.ascontiguousarray(a) for n, a in f.items()}


def declare(nc, arrays):
    io = {n: nc.dram_tensor(f"in_{n}_dram", a.shape, F32, kind="ExternalInput").ap() for n, a in arrays.items()}
    for n in ("x1", "x2", "x3"):
        io[n] = nc.dram_tensor(n, (B * S, D), F32, kind="Internal").ap()
    io["mod_rows"] = nc.dram_tensor("scratch_mod_rows", (2, B, MODS * D), F32, kind="Internal").ap()
    io["out"] = nc.dram_tensor("out_0_dram", (B, S, D), F32, kind="ExternalOutput").ap()
    io["out_rows"] = io["out"].rearrange("b s d -> (b s) d")
    return io, ["out_0_dram"]


def kernel(**inputs):
    import numpy as np
    import concourse.bacc as bacc
    from concourse.bass_utils import run_bass_kernel_spmd

    nc = bacc.Bacc("TRN2", target_bir_lowering=False, num_devices=1)
    arrays = layout({n: np.asarray(a) for n, a in inputs.items()})
    io, outs = declare(nc, arrays)
    build(nc, io)
    r = run_bass_kernel_spmd(nc, [{f"in_{n}_dram": a for n, a in arrays.items()}], core_ids=[0])
    return r.results[0][outs[0]]
```
